# Optimizing a Trainium2 kernel written in Bass

```python
import numpy as np
import jax
import jax.numpy as jnp

def _softmax(x, axis=-1):
    return jax.nn.softmax(x, axis=axis)

def _gelu(x):
    return jax.nn.gelu(x, approximate=True)

def _silu(x):
    return jax.nn.silu(x)

def _sigmoid(x):
    return jax.nn.sigmoid(x)

def _layernorm(x, axis=-1, eps=1e-05):
    m = jnp.mean(x, axis=axis, keepdims=True)
    v = jnp.var(x, axis=axis, keepdims=True)
    return (x - m) / jnp.sqrt(v + eps)

def _scatter_add(tgt, idx, src, axis=0):
    return tgt.at[idx].add(src)

def _segment_sum(src, seg, n):
    return jax.ops.segment_sum(src, seg, n)
kernel_name = 'mk_recurrent_d1_jaxref_r4_a2041c'

def setup_inputs(seed: int=0):
    np.random.seed(seed)
    _w = jnp.asarray

    def _L0_attn_setup():
        import jax, jax.numpy as jnp
        import numpy as np
        B, T, C = (4, 512, 256)
        HD = 64
        H = C // HD
        DW, DA, DG = (64, 64, 128)
        EPS = 0.00064

        def _rwkv7_forward(x, x_r, x_w, x_k, x_v, x_a, x_g, W_r, W_k, W_v, W_o, w0, w1, w2, a0, a1, a2, g1, g2, k_k, k_a, r_k, ln_w, ln_b):
            Bq, Tq, Cq = x.shape
            xx = jnp.concatenate([jnp.zeros_like(x[:, :1]), x[:, :-1]], axis=1) - x
            xr = x + xx * x_r
            xw = x + xx * x_w
            xk = x + xx * x_k
            xv = x + xx * x_v
            xa = x + xx * x_a
            xg = x + xx * x_g
            r = xr @ W_r
            w = -jax.nn.softplus(-(w0 + jnp.tanh(xw @ w1) @ w2)) - 0.5
            k = xk @ W_k
            v = xv @ W_v
            v_first = v
            a = jax.nn.sigmoid(a0 + xa @ a1 @ a2)
            g = jax.nn.sigmoid(xg @ g1) @ g2
            kk = (k * k_k).reshape(Bq, Tq, H, HD)
            kk = kk / jnp.maximum(jnp.linalg.norm(kk, axis=-1, keepdims=True), 1e-12)
            k = k * (1.0 + (a - 1.0) * k_a)

            def heads_tfirst(t):
                return t.reshape(Bq, Tq, H, HD).transpose(1, 0, 2, 3)
            r_h, k_h, v_h, a_h = (heads_tfirst(r), heads_tfirst(k), heads_tfirst(v), heads_tfirst(a))
            kk_h = kk.transpose(1, 0, 2, 3)
            decay = jnp.exp(-jnp.exp(heads_tfirst(w)))

            def step(S, inp):
                rt, dt, kt, vt, kkt, at = inp
                sa = jnp.einsum('bhvk,bhk->bhv', S, -kkt)
                S = S * dt[:, :, None, :] + sa[..., None] * (kkt * at)[:, :, None, :] + vt[..., None] * kt[:, :, None, :]
                y = jnp.einsum('bhvk,bhk->bhv', S, rt)
                return (S, y)
            S0 = jnp.zeros((Bq, H, HD, HD), x.dtype)
            _, y = jax.lax.scan(step, S0, (r_h, decay, k_h, v_h, kk_h, a_h))
            y = y.transpose(1, 0, 2, 3)
            mean = y.mean(-1, keepdims=True)
            var = y.var(-1, keepdims=True)
            y = (y - mean) / jnp.sqrt(var + EPS) * ln_w.reshape(H, HD) + ln_b.reshape(H, HD)
            r4 = r.reshape(Bq, Tq, H, HD)
            k4 = k.reshape(Bq, Tq, H, HD)
            v4 = v.reshape(Bq, Tq, H, HD)
            y = y + jnp.sum(r4 * k4 * r_k, axis=-1, keepdims=True) * v4
            out = y.reshape(Bq, Tq, Cq) * g @ W_o
            return (out, v_first)

        def _reference_tuple_inner(x, x_r, x_w, x_k, x_v, x_a, x_g, W_r, W_k, W_v, W_o, w0, w1, w2, a0, a1, a2, g1, g2, k_k, k_a, r_k, ln_w, ln_b):
            return _rwkv7_forward(x, x_r, x_w, x_k, x_v, x_a, x_g, W_r, W_k, W_v, W_o, w0, w1, w2, a0, a1, a2, g1, g2, k_k, k_a, r_k, ln_w, ln_b)
        key = jax.random.key(seed)
        ks = jax.random.split(key, 24)

        def nrm(i, shape, s=1.0, off=0.0):
            return jax.random.normal(ks[i], shape, dtype=jnp.float32) * s + off

        def uni(i, shape):
            return jax.random.uniform(ks[i], shape, dtype=jnp.float32)
        return {'x': nrm(0, (B, T, C)), 'x_r': uni(1, (C,)), 'x_w': uni(2, (C,)), 'x_k': uni(3, (C,)), 'x_v': uni(4, (C,)), 'x_a': uni(5, (C,)), 'x_g': uni(6, (C,)), 'W_r': nrm(7, (C, C), 0.02), 'W_k': nrm(8, (C, C), 0.02), 'W_v': nrm(9, (C, C), 0.02), 'W_o': nrm(10, (C, C), 0.02), 'w0': nrm(11, (C,), 0.3, -6.0), 'w1': nrm(12, (C, DW), 0.02), 'w2': nrm(13, (DW, C), 0.02), 'a0': nrm(14, (C,), 0.1), 'a1': nrm(15, (C, DA), 0.02), 'a2': nrm(16, (DA, C), 0.02), 'g1': nrm(17, (C, DG), 0.02), 'g2': nrm(18, (DG, C), 0.02), 'k_k': nrm(19, (C,), 0.05, 0.85), 'k_a': nrm(20, (C,), 0.05, 1.0), 'r_k': nrm(21, (H, HD), 0.1), 'ln_w': jnp.ones((C,), jnp.float32), 'ln_b': jnp.zeros((C,), jnp.float32)}
    _L0_attn_in = _L0_attn_setup()

    def _L0_ffn_setup():
        import jax, jax.numpy as jnp
        import numpy as np
        DIM = 256
        HEADS = 16
        HD = DIM // HEADS
        M = 64
        E = 4
        K = 2
        HID = 512
        MID = 512
        LB = 0.01
        EPS = 1.1920929e-07

        def _rms(x, w):
            return x * jax.lax.rsqrt(jnp.mean(x * x, axis=-1, keepdims=True) + EPS) * w

        def _gelu(x):
            return jax.nn.gelu(x, approximate=False)
        key = jax.random.key(seed)
        ks = jax.random.split(key, 20)
        d = DIM
        w = lambda k, s: jax.random.normal(k, s, jnp.float32) * 0.02
        return {'x': jax.random.normal(ks[0], (4, 256, d), jnp.float32), 'n1_w': jnp.ones((d,), jnp.float32), 'n2_w': jnp.ones((d,), jnp.float32), 'wq': w(ks[1], (d, d)), 'wk': w(ks[2], (d, d)), 'wv': w(ks[3], (d, d)), 'wo': w(ks[4], (d, d)), 'qn_w': jnp.ones((HD,), jnp.float32), 'kn_w': jnp.ones((HD,), jnp.float32), 'gate_w': w(ks[5], (E, d)), 'e0_up': w(ks[6], (HID, d)), 'e0_down': w(ks[7], (d, HID)), 'e1_w1': w(ks[8], (HID, d)), 'e1_w2': w(ks[9], (HID, d)), 'e1_down': w(ks[10], (d, HID)), 'e2_l1': w(ks[11], (MID, d)), 'e2_l2': w(ks[12], (HID, MID)), 'e2_l3': w(ks[13], (MID, HID)), 'e2_l4': w(ks[14], (d, MID)), 'e3_down': w(ks[15], (d, d)), 'e3_up': w(ks[16], (HID, d)), 'e3_out': w(ks[17], (d, HID))}
    _L0_ffn_in = _L0_ffn_setup()
    _d = {'L0_attn_x': _L0_attn_in['x'], 'L0_attn_x_r': _L0_attn_in['x_r'], 'L0_attn_x_w': _L0_attn_in['x_w'], 'L0_attn_x_k': _L0_attn_in['x_k'], 'L0_attn_x_v': _L0_attn_in['x_v'], 'L0_attn_x_a': _L0_attn_in['x_a'], 'L0_attn_x_g': _L0_attn_in['x_g'], 'L0_attn_W_r': _L0_attn_in['W_r'], 'L0_attn_W_k': _L0_attn_in['W_k'], 'L0_attn_W_v': _L0_attn_in['W_v'], 'L0_attn_W_o': _L0_attn_in['W_o'], 'L0_attn_w0': _L0_attn_in['w0'], 'L0_attn_w1': _L0_attn_in['w1'], 'L0_attn_w2': _L0_attn_in['w2'], 'L0_attn_a0': _L0_attn_in['a0'], 'L0_attn_a1': _L0_attn_in['a1'], 'L0_attn_a2': _L0_attn_in['a2'], 'L0_attn_g1': _L0_attn_in['g1'], 'L0_attn_g2': _L0_attn_in['g2'], 'L0_attn_k_k': _L0_attn_in['k_k'], 'L0_attn_k_a': _L0_attn_in['k_a'], 'L0_attn_r_k': _L0_attn_in['r_k'], 'L0_attn_ln_w': _L0_attn_in['ln_w'], 'L0_attn_ln_b': _L0_attn_in['ln_b'], 'L0_ffn_n1_w': _L0_ffn_in['n1_w'], 'L0_ffn_n2_w': _L0_ffn_in['n2_w'], 'L0_ffn_wq': _L0_ffn_in['wq'], 'L0_ffn_wk': _L0_ffn_in['wk'], 'L0_ffn_wv': _L0_ffn_in['wv'], 'L0_ffn_wo': _L0_ffn_in['wo'], 'L0_ffn_qn_w': _L0_ffn_in['qn_w'], 'L0_ffn_kn_w': _L0_ffn_in['kn_w'], 'L0_ffn_gate_w': _L0_ffn_in['gate_w'], 'L0_ffn_e0_up': _L0_ffn_in['e0_up'], 'L0_ffn_e0_down': _L0_ffn_in['e0_down'], 'L0_ffn_e1_w1': _L0_ffn_in['e1_w1'], 'L0_ffn_e1_w2': _L0_ffn_in['e1_w2'], 'L0_ffn_e1_down': _L0_ffn_in['e1_down'], 'L0_ffn_e2_l1': _L0_ffn_in['e2_l1'], 'L0_ffn_e2_l2': _L0_ffn_in['e2_l2'], 'L0_ffn_e2_l3': _L0_ffn_in['e2_l3'], 'L0_ffn_e2_l4': _L0_ffn_in['e2_l4'], 'L0_ffn_e3_down': _L0_ffn_in['e3_down'], 'L0_ffn_e3_up': _L0_ffn_in['e3_up'], 'L0_ffn_e3_out': _L0_ffn_in['e3_out']}
    _x0 = _d['L0_attn_x']
    _d['L0_attn_x'] = jax.random.normal(jax.random.fold_in(jax.random.key(seed), 1), (2, 2048, 256), dtype=_x0.dtype)
    del _x0
    return _d

def reference(L0_attn_x, L0_attn_x_r, L0_attn_x_w, L0_attn_x_k, L0_attn_x_v, L0_attn_x_a, L0_attn_x_g, L0_attn_W_r, L0_attn_W_k, L0_attn_W_v, L0_attn_W_o, L0_attn_w0, L0_attn_w1, L0_attn_w2, L0_attn_a0, L0_attn_a1, L0_attn_a2, L0_attn_g1, L0_attn_g2, L0_attn_k_k, L0_attn_k_a, L0_attn_r_k, L0_attn_ln_w, L0_attn_ln_b, L0_ffn_n1_w, L0_ffn_n2_w, L0_ffn_wq, L0_ffn_wk, L0_ffn_wv, L0_ffn_wo, L0_ffn_qn_w, L0_ffn_kn_w, L0_ffn_gate_w, L0_ffn_e0_up, L0_ffn_e0_down, L0_ffn_e1_w1, L0_ffn_e1_w2, L0_ffn_e1_down, L0_ffn_e2_l1, L0_ffn_e2_l2, L0_ffn_e2_l3, L0_ffn_e2_l4, L0_ffn_e3_down, L0_ffn_e3_up, L0_ffn_e3_out):

    def _L0_attn_ref(x, x_r, x_w, x_k, x_v, x_a, x_g, W_r, W_k, W_v, W_o, w0, w1, w2, a0, a1, a2, g1, g2, k_k, k_a, r_k, ln_w, ln_b):
        import jax, jax.numpy as jnp
        import numpy as np
        B, T, C = (4, 512, 256)
        HD = 64
        H = C // HD
        DW, DA, DG = (64, 64, 128)
        EPS = 0.00064

        def _rwkv7_forward(x, x_r, x_w, x_k, x_v, x_a, x_g, W_r, W_k, W_v, W_o, w0, w1, w2, a0, a1, a2, g1, g2, k_k, k_a, r_k, ln_w, ln_b):
            Bq, Tq, Cq = x.shape
            xx = jnp.concatenate([jnp.zeros_like(x[:, :1]), x[:, :-1]], axis=1) - x
            xr = x + xx * x_r
            xw = x + xx * x_w
            xk = x + xx * x_k
            xv = x + xx * x_v
            xa = x + xx * x_a
            xg = x + xx * x_g
            r = xr @ W_r
            w = -jax.nn.softplus(-(w0 + jnp.tanh(xw @ w1) @ w2)) - 0.5
            k = xk @ W_k
            v = xv @ W_v
            v_first = v
            a = jax.nn.sigmoid(a0 + xa @ a1 @ a2)
            g = jax.nn.sigmoid(xg @ g1) @ g2
            kk = (k * k_k).reshape(Bq, Tq, H, HD)
            kk = kk / jnp.maximum(jnp.linalg.norm(kk, axis=-1, keepdims=True), 1e-12)
            k = k * (1.0 + (a - 1.0) * k_a)

            def heads_tfirst(t):
                return t.reshape(Bq, Tq, H, HD).transpose(1, 0, 2, 3)
            r_h, k_h, v_h, a_h = (heads_tfirst(r), heads_tfirst(k), heads_tfirst(v), heads_tfirst(a))
            kk_h = kk.transpose(1, 0, 2, 3)
            decay = jnp.exp(-jnp.exp(heads_tfirst(w)))

            def step(S, inp):
                rt, dt, kt, vt, kkt, at = inp
                sa = jnp.einsum('bhvk,bhk->bhv', S, -kkt)
                S = S * dt[:, :, None, :] + sa[..., None] * (kkt * at)[:, :, None, :] + vt[..., None] * kt[:, :, None, :]
                y = jnp.einsum('bhvk,bhk->bhv', S, rt)
                return (S, y)
            S0 = jnp.zeros((Bq, H, HD, HD), x.dtype)
            _, y = jax.lax.scan(step, S0, (r_h, decay, k_h, v_h, kk_h, a_h))
            y = y.transpose(1, 0, 2, 3)
            mean = y.mean(-1, keepdims=True)
            var = y.var(-1, keepdims=True)
            y = (y - mean) / jnp.sqrt(var + EPS) * ln_w.reshape(H, HD) + ln_b.reshape(H, HD)
            r4 = r.reshape(Bq, Tq, H, HD)
            k4 = k.reshape(Bq, Tq, H, HD)
            v4 = v.reshape(Bq, Tq, H, HD)
            y = y + jnp.sum(r4 * k4 * r_k, axis=-1, keepdims=True) * v4
            out = y.reshape(Bq, Tq, Cq) * g @ W_o
            return (out, v_first)

        def _reference_tuple_inner(x, x_r, x_w, x_k, x_v, x_a, x_g, W_r, W_k, W_v, W_o, w0, w1, w2, a0, a1, a2, g1, g2, k_k, k_a, r_k, ln_w, ln_b):
            return _rwkv7_forward(x, x_r, x_w, x_k, x_v, x_a, x_g, W_r, W_k, W_v, W_o, w0, w1, w2, a0, a1, a2, g1, g2, k_k, k_a, r_k, ln_w, ln_b)
        return _reference_tuple_inner(x, x_r, x_w, x_k, x_v, x_a, x_g, W_r, W_k, W_v, W_o, w0, w1, w2, a0, a1, a2, g1, g2, k_k, k_a, r_k, ln_w, ln_b)[0]

    def _L0_ffn_ref(x, n1_w, n2_w, wq, wk, wv, wo, qn_w, kn_w, gate_w, e0_up, e0_down, e1_w1, e1_w2, e1_down, e2_l1, e2_l2, e2_l3, e2_l4, e3_down, e3_up, e3_out):
        import jax, jax.numpy as jnp
        import numpy as np
        DIM = 256
        HEADS = 16
        HD = DIM // HEADS
        M = 64
        E = 4
        K = 2
        HID = 512
        MID = 512
        LB = 0.01
        EPS = 1.1920929e-07

        def _rms(x, w):
            return x * jax.lax.rsqrt(jnp.mean(x * x, axis=-1, keepdims=True) + EPS) * w

        def _gelu(x):
            return jax.nn.gelu(x, approximate=False)
        B, T, C = x.shape
        h = _rms(x, n1_w)
        heads = lambda w_: (h @ w_.T).reshape(B, T, HEADS, HD).transpose(0, 2, 1, 3)
        q = _rms(heads(wq), qn_w)
        k = _rms(heads(wk), kn_w)
        v = heads(wv)
        scores = jnp.einsum('bhqd,bhkd->bhqk', q, k) * HD ** (-0.5)
        causal = jnp.tril(jnp.ones((T, T), bool))
        scores = jnp.where(causal[None, None], scores, -jnp.inf)
        attn = jax.nn.softmax(scores, axis=-1)
        ao = jnp.einsum('bhqk,bhkd->bhqd', attn, v).transpose(0, 2, 1, 3).reshape(B, T, C) @ wo.T
        ao = ao.at[:, :, :M].set(0.0)
        x = x + ao
        xf = _rms(x, n2_w).reshape(-1, C)
        N = xf.shape[0]
        logits = jnp.nan_to_num(xf @ gate_w.T)
        probs = jax.nn.softmax(logits, axis=-1)
        topv, topi = jax.lax.top_k(probs, K)
        topv = topv / (topv.sum(-1, keepdims=True) + 1e-08)
        wts = jnp.zeros((N, E), x.dtype).at[jnp.arange(N)[:, None], topi].add(topv)
        o0 = _gelu(xf @ e0_up.T) @ e0_down.T
        o1 = jax.nn.silu(xf @ e1_w1.T) * (xf @ e1_w2.T) @ e1_down.T
        o2 = _gelu(_gelu(_gelu(xf @ e2_l1.T) @ e2_l2.T) @ e2_l3.T) @ e2_l4.T
        o3 = _gelu(_gelu(xf @ e3_down.T) @ e3_up.T) @ e3_out.T
        moe = wts[:, 0:1] * o0 + wts[:, 1:2] * o1 + wts[:, 2:3] * o2 + wts[:, 3:4] * o3
        moe = moe.reshape(B, T, C).at[:, :, :M].set(0.0)
        return x + moe
    x = L0_attn_x
    xn = _layernorm(x, axis=-1)
    s = _L0_attn_ref(xn, L0_attn_x_r, L0_attn_x_w, L0_attn_x_k, L0_attn_x_v, L0_attn_x_a, L0_attn_x_g, L0_attn_W_r, L0_attn_W_k, L0_attn_W_v, L0_attn_W_o, L0_attn_w0, L0_attn_w1, L0_attn_w2, L0_attn_a0, L0_attn_a1, L0_attn_a2, L0_attn_g1, L0_attn_g2, L0_attn_k_k, L0_attn_k_a, L0_attn_r_k, L0_attn_ln_w, L0_attn_ln_b)
    g = _silu(_L0_ffn_ref(xn, L0_ffn_n1_w, L0_ffn_n2_w, L0_ffn_wq, L0_ffn_wk, L0_ffn_wv, L0_ffn_wo, L0_ffn_qn_w, L0_ffn_kn_w, L0_ffn_gate_w, L0_ffn_e0_up, L0_ffn_e0_down, L0_ffn_e1_w1, L0_ffn_e1_w2, L0_ffn_e1_down, L0_ffn_e2_l1, L0_ffn_e2_l2, L0_ffn_e2_l3, L0_ffn_e2_l4, L0_ffn_e3_down, L0_ffn_e3_up, L0_ffn_e3_out))
    x = x + s * g
    return x

_drawn_inputs = setup_inputs


def setup_inputs(seed=0):
    import zlib

    import numpy as np

    out = dict(_drawn_inputs(seed))
    spreads = {'L0_attn_ln_w': (1.0, 0.6),
     'L0_attn_ln_b': (0.0, 2.0),
     'L0_ffn_n1_w': (1.0, 0.6),
     'L0_ffn_n2_w': (1.0, 0.6),
     'L0_ffn_qn_w': (1.0, 0.6),
     'L0_ffn_kn_w': (1.0, 0.6)}
    factors = {'L0_attn_x_r': 4.875,
     'L0_attn_x_w': 8.0,
     'L0_attn_x_k': 5.398,
     'L0_attn_x_v': 5.833,
     'L0_attn_x_a': 8.0,
     'L0_attn_x_g': 8.0,
     'L0_attn_w0': 8.0,
     'L0_attn_w1': 8.0,
     'L0_attn_w2': 8.0,
     'L0_attn_a0': 8.0,
     'L0_attn_a1': 8.0,
     'L0_attn_a2': 8.0,
     'L0_attn_g1': 8.0,
     'L0_attn_k_k': 64.0,
     'L0_attn_k_a': 8.0,
     'L0_attn_r_k': 8.0,
     'L0_ffn_wq': 8.0,
     'L0_ffn_wk': 8.0,
     'L0_ffn_wv': 8.0,
     'L0_ffn_wo': 8.0,
     'L0_ffn_gate_w': 8.0,
     'L0_ffn_e0_up': 8.0,
     'L0_ffn_e0_down': 8.0,
     'L0_ffn_e1_w1': 8.0,
     'L0_ffn_e1_w2': 8.0,
     'L0_ffn_e1_down': 8.0,
     'L0_ffn_e2_l1': 8.0,
     'L0_ffn_e2_l2': 8.0,
     'L0_ffn_e2_l3': 8.0,
     'L0_ffn_e2_l4': 8.0,
     'L0_ffn_e3_down': 8.0,
     'L0_ffn_e3_up': 8.0,
     'L0_ffn_e3_out': 8.0}
    for name, (base, spread) in spreads.items():
        noise = np.random.default_rng([zlib.crc32(name.encode()), seed]).standard_normal(out[name].shape)
        drawn = base * np.exp(spread * noise) if base else spread * noise
        out[name] = jnp.asarray(drawn.astype(out[name].dtype))
    for name, factor in factors.items():
        out[name] = (out[name] * factor).astype(out[name].dtype)
    return out
```

```python
import concourse.bass as bass
from concourse import mybir
from contextlib import ExitStack
import math

FP32 = mybir.dt.float32
BF16 = mybir.dt.bfloat16
ALU = mybir.AluOpType
ACT = mybir.ActivationFunctionType
AX = mybir.AxisListType

B, T, C = 2, 2048, 256
HALVES = C // 128
RH, RD = 4, 64
CH = 64
TT = 256
NT = T // TT
COLS = B * TT
CB = COLS // CH
PAIRS = CB * HALVES
LEVELS = int(math.log2(CH))
LN_EPS, GN_EPS, RMS_EPS = 1e-5, 0.00064, 1.1920929e-07
NEG_DECAY = math.exp(-0.5)

AH, AD, HID = 16, 16, 512
EXPERTS = 4

F32_TABLE = [("ident", 128), ("neg_kq", 128), ("neg_qk", 128), ("ones64", 128), ("ones16", 128), ("ones128", 128),
             ("amask", 7 * 64), ("eye64", 64), ("low0", 64), ("low0t", 64),
             ("lev", (LEVELS - 1) * 64), ("reset", COLS), ("eps", 4), ("earlier", EXPERTS * EXPERTS)]
VECS = ["x_r", "x_w", "x_k", "x_v", "x_a", "x_g", "w0", "a0", "k_k", "k_a", "r_k", "ln_w", "ln_b",
        "n1_w", "n2_w", "qn_w", "kn_w"]


def table_at():
    at, n = {}, 0
    for name, width in F32_TABLE:
        at[name] = (n, n + width)
        n += width
    return at, n


class Signal:

    def __init__(self, sem, per, unit=1):
        self.sem, self.per, self.unit, self.n = sem, per, unit, 0

    def open(self, eng):
        eng.sem_inc(self.sem, self.per * self.unit)

    def up(self):
        self.n += 1
        return self.unit

    def at(self, turn, n=None, back=0):
        return turn * (self.per * self.unit) + (self.per * (1 - back) + (self.n if n is None else n)) * self.unit

    def whole(self):
        assert self.n == self.per, (self.n, self.per)


def recurrent_phase(nc, io, keep, signal):
    ctx = ExitStack()
    with ctx:
        def sb(name, shape, dt=FP32):
            return ctx.enter_context(nc.sbuf_tensor("r_" + name, shape, dt))

        def sig(name, per, unit=1):
            return signal("r_" + name, per, unit)

        cst, at, vec, xn_all = keep["cst"], keep["at"], keep["vec"], keep["xn_all"]
        s_const = keep["s_const"]

        def const(name, lo=0, hi=None):
            a, b = at[name]
            return cst[:, a + lo:(a + hi if hi is not None else b)]

        def v(name, h):
            return vec[:, VECS.index(name), h:h + 1]

        ident, ones64 = const("ident"), const("ones64")

        w_in = {n: sb(n, [128, HALVES, w]) for n, w in
                [("W_r", C), ("W_k", C), ("W_v", C), ("W_o", C), ("w1", 64), ("a1", 64), ("g1", 128)]}
        w_up = {n: sb(n, [k, C]) for n, k in [("w2", 64), ("a2", 64), ("g2", 128)]}
        x_tok = sb("x_tok", [128, 4, C])
        xn_tok = sb("xn_tok", [128, 4, C])
        bn6, mv = sb("bn6", [128, 4, 6]), sb("mv", [128, 4, 2])
        std, rstd = sb("std", [128, 4]), sb("rstd", [128, 4])
        dx = sb("dx", [128, HALVES, COLS])
        mixed = {n: sb("x" + n, [128, HALVES, COLS]) for n in "gwakrv"}
        tg, tw, ta = sb("tg", [128, COLS]), sb("tw", [64, COLS]), sb("ta", [64, COLS])
        kraw, rT, vT, gT = (sb(n, [128, HALVES, COLS]) for n in ("kraw", "rT", "vT", "gT"))
        sg, av = sb("sg", [128, HALVES, COLS]), sb("av", [128, HALVES, COLS])
        v_st = sb("v_st", [128, CB, HALVES, 64])
        kk, sq, nrm = (sb(n, [128, HALVES, COLS]) for n in ("kk", "sq", "nrm"))
        kmod = sb("kmod", [128, HALVES, COLS])
        cs, csp = dx, mixed["g"]
        p_now, p_inv, p_prev = mixed["w"], mixed["a"], mixed["k"]
        tmp, bonus = mixed["r"], mixed["v"]
        ari = sb("ari", [128, HALVES, CB, 3, 64])
        bT, kT = sb("bT", [128, HALVES, CB, 64]), sb("kT", [128, HALVES, CB, 64])
        am = sb("am", [128, PAIRS, 7, 64])
        inv, invT = sb("inv", [128, PAIRS, 64]), sb("invT", [128, PAIRS, 64])
        as_pairs = lambda a: a[:, :, :].rearrange("p h (a c) -> p (h a) c", c=64)
        lj = [as_pairs(csp), as_pairs(cs)]
        zz = as_pairs(kraw)
        state = sb("state", [128, B, HALVES, 64])
        stmp = sb("stmp", [128, B, HALVES, 64])
        g_sb, u_sb = sb("g_sb", [128, B, HALVES, 64]), sb("u_sb", [128, B, HALVES, 64])
        yT = rT
        yc, yg = kk, sq
        s_tok = sb("s_tok", [128, 4, C])

        ps = ctx.enter_context(nc.psum_tensor("r_ps", [128, 8, 512], FP32))

        JOBS = [("g1", "A"), ("w1", "A"), ("a1", "V"), ("k0", "V"), ("k1", "V"), ("w20", "A"), ("w21", "A"),
                ("a20", "A"), ("a21", "A"), ("r0", "A"), ("r1", "A"), ("v0", "A"), ("v1", "A"),
                ("g20", "V"), ("g21", "V"), ("s0", "V"), ("s1", "V"),
                ("n0", "A"), ("n1", "A"), ("b0", "V"), ("b1", "V")]
        NJ = len(JOBS)
        job_no = {n: i for i, (n, _) in enumerate(JOBS)}
        taken = {}
        for who in "AV":
            for i, n in enumerate([n for n, w in JOBS if w == who]):
                taken[n] = (who, i + 1)

        def bank(name):
            return (job_no[name] + 2) % 8

        s_w = sig("weights", 1, 16 * 10)
        s_x = sig("x_in", 1, 32)
        s_var = sig("var", 1)
        s_std = sig("std", 1)
        s_xn = sig("xn", 1)
        s_tr = sig("xn_transposed", 2)
        s_xt = sig("xn_kept", 2)
        s_mix = sig("mixed", 6)
        s_job = sig("job", NJ)
        took = {"A": sig("act_took", sum(w == "A" for _, w in JOBS)),
                "V": sig("dve_took", sum(w == "V" for _, w in JOBS))}
        s_kk, s_sq = sig("kk", 1), sig("kk_squared", 1)
        s_cs, s_exp = sig("log_decay", 1), sig("decays", 1)
        s_rk = sig("r_times_k", 1)
        s_feat = sig("features", 1)
        s_am, s_amsb = sig("products", PAIRS), sig("products_kept", PAIRS)
        s_lj, s_z, s_zsb, s_inv = sig("level_off", LEVELS - 1), sig("z", LEVELS - 1), sig("z_kept", LEVELS - 1), sig("inverse_step", LEVELS - 1)
        s_invsb = sig("inverse_kept", LEVELS - 1)
        s_g, s_gsb = sig("chunk_g", 4), sig("chunk_g_kept", 4)
        s_u, s_usb = sig("chunk_u", 4), sig("chunk_u_kept", 4)
        s_sn, s_state = sig("state_gain", 4), sig("state", 4)
        s_y, s_ysb = sig("chunk_y", 4), sig("chunk_y_kept", 4)
        s_mean, s_yc, s_ycsq, s_gvar = sig("y_mean", 1), sig("y_centred", 1), sig("y_squared", 1), sig("y_var", 1)
        s_gstd, s_yg = sig("y_std", 1), sig("y_gated", 1)
        s_out, s_outsb, s_store = sig("s_out", 1), sig("s_out_kept", 1), sig("s_stored", 1, 64)
        dve_step = sig("dve_step", keep["r_dve_steps"])
        s_init = sig("init", 1)
        s_passed = sig("passed", 1).sem

        def both(ap):
            return ap[:, :, :].rearrange("p h (b t) -> p h b t", b=B)

        block = ctx.enter_context(nc.Block())

        @block.sync
        def _(sp):
            for n, t in list(w_in.items()):
                sp.dma_start(t[:, :, :], io[n]).then_inc(s_w.sem, 16)
            for n, t in list(w_up.items()):
                sp.dma_start(t[:, :], io[n]).then_inc(s_w.sem, 16)
            s_x.open(sp)
            s_store.open(sp)
            with sp.Fori(0, NT) as t:
                sp.wait_ge(s_xn.sem, s_xn.at(t, 1, back=1))
                for b in range(B):
                    sp.dma_start(x_tok[:, 2 * b:2 * b + 2, :],
                                 io["x"][b, bass.ds(t * TT, TT), :].rearrange("(s p) c -> p s c", p=128)
                                 ).then_inc(s_x.sem, 16)
                sp.wait_ge(s_outsb.sem, s_outsb.at(t, 1))
                for s in range(4):
                    sp.dma_start(io["s_dram"][s // 2, bass.ds(t * TT + (s % 2) * 128, 128), :],
                                 s_tok[:, s, :]).then_inc(s_store.sem, 16)
            sp.wait_ge(s_store.sem, s_store.at(NT - 1, 1))

        @block.tensor
        def _(pe):
            for q in (s_tr, s_job, s_am, s_z, s_inv, s_g, s_u, s_sn, s_y, s_mean, s_gvar, s_out):
                q.open(pe)
            pe.wait_ge(s_const, keep["n_const"])
            pe.wait_ge(s_w.sem, 16 * 10)
            mm = nc.tensor.matmul
            with pe.Fori(0, NT) as t:
                pe.wait_ge(s_xn.sem, s_xn.at(t, 1))
                pe.wait_ge(s_outsb.sem, s_outsb.at(t, 1, back=1))
                for h in range(HALVES):
                    for s in range(4):
                        last = nc.tensor.transpose(ps[:, h, 128 * s:128 * s + 128],
                                                   xn_tok[:, s, 128 * h:128 * h + 128], ident)
                    last.then_inc(s_tr.sem, s_tr.up())

                def job(name, which, weights, src, m=128):
                    out = ps[0:m, bank(name), :]
                    for i, (wt, x) in enumerate(zip(weights, src)):
                        last = mm(out, wt, x, start=(i == 0), stop=(i == len(src) - 1))
                    last.then_inc(s_job.sem, s_job.up())

                def free(name):
                    n = job_no[name]
                    if n >= 8:
                        who, i = taken[JOBS[n - 8][0]]
                        pe.wait_ge(took[who].sem, took[who].at(t, i))
                    elif n >= 6:
                        pe.wait_ge(s_xt.sem, s_xt.at(t, 2))

                for name, k, m in (("g1", 1, 128), ("w1", 2, 64), ("a1", 3, 64)):
                    pe.wait_ge(s_mix.sem, s_mix.at(t, k))
                    free(name)
                    job(name, 0, [w_in[name][:, i, :] for i in range(2)],
                        [mixed[name[0]][:, i, :] for i in range(2)], m)
                pe.wait_ge(s_mix.sem, s_mix.at(t, 4))
                for h in range(2):
                    free(f"k{h}")
                    job(f"k{h}", 0, [w_in["W_k"][:, i, 128 * h:128 * h + 128] for i in range(2)],
                        [mixed["k"][:, i, :] for i in range(2)])
                for name, src, first in (("w2", tw, "w1"), ("a2", ta, "a1")):
                    pe.wait_ge(took[taken[first][0]].sem, took[taken[first][0]].at(t, taken[first][1]))
                    for h in range(2):
                        free(f"{name}{h}")
                        job(f"{name}{h}", 0, [w_up[name][:, 128 * h:128 * h + 128]], [src[:, :]])
                for name, k in (("r", 5), ("v", 6)):
                    pe.wait_ge(s_mix.sem, s_mix.at(t, k))
                    for h in range(2):
                        free(f"{name}{h}")
                        job(f"{name}{h}", 0, [w_in["W_" + name][:, i, 128 * h:128 * h + 128] for i in range(2)],
                            [mixed[name][:, i, :] for i in range(2)])
                for h in range(2):
                    free(f"g2{h}")
                    pe.wait_ge(took["A"].sem, took["A"].at(t, taken["g1"][1]))
                    job(f"g2{h}", 0, [w_up["g2"][:, 128 * h:128 * h + 128]], [tg[:, :]])
                w_v = w_in["W_v"][:, :, :].rearrange("p k (g j d) -> p k g j d", j=2, d=64)
                for q in range(2):
                    free(f"s{q}")
                    for c in range(4):
                        cb = 4 * q + c
                        for j in range(2):
                            for i in range(2):
                                last = mm(ps[64 * j:64 * j + 64, bank(f"s{q}"), 128 * c:128 * c + 128],
                                          mixed["v"][:, i, 64 * cb:64 * cb + 64], w_v[:, i, :, j, :],
                                          start=(i == 0), stop=(i == 1))
                    last.then_inc(s_job.sem, s_job.up())
                for name, src, ready in (("n", sq, s_sq), ("b", tmp, s_rk)):
                    pe.wait_ge(ready.sem, ready.at(t, 1))
                    for h in range(2):
                        free(f"{name}{h}")
                        job(f"{name}{h}", 0, [ones64], [src[:, h, :]])
                def apart():
                    pe.sem_inc(s_passed, 1)

                pe.wait_ge(s_feat.sem, s_feat.at(t, 1))
                for p in range(PAIRS):
                    cb, g = divmod(p, 2)
                    if p >= 8:
                        pe.wait_ge(s_amsb.sem, s_amsb.at(t, p - 7))
                    apart()
                    for j in range(2):
                        q = slice(64 * j, 64 * j + 64)
                        rhs = ari[q, g, cb, :, :].rearrange("p a c -> p (a c)")
                        mm(ps[q, p % 8, 0:192], bT[q, g, cb, :], rhs, start=True, stop=True)
                        mm(ps[q, p % 8, 192:384], kT[q, g, cb, :], rhs, start=True, stop=True)
                        last = mm(ps[q, p % 8, 384:448], ari[q, g, cb, 0, :], bT[q, g, cb, :], start=True, stop=True)
                    last.then_inc(s_am.sem, s_am.up())

                def pairwise(first_bank, left, right):
                    apart()
                    for p in range(PAIRS):
                        for j in range(2):
                            q = slice(64 * j, 64 * j + 64)
                            last = mm(ps[q, first_bank + p // 8, 64 * (p % 8):64 * (p % 8) + 64],
                                      left[q, p, :], right[q, p, :], start=True, stop=True)
                    return last

                for lev in range(LEVELS - 1):
                    if lev:
                        pe.wait_ge(s_invsb.sem, s_invsb.at(t, lev))
                    pe.wait_ge(s_lj.sem, s_lj.at(t, lev + 1))
                    if not lev:
                        pe.wait_ge(s_amsb.sem, s_amsb.at(t, PAIRS))
                    pairwise(0, lj[lev % 2], inv).then_inc(s_z.sem, s_z.up())
                    pe.wait_ge(s_zsb.sem, s_zsb.at(t, lev + 1))
                    pairwise(2, invT, zz)
                    pairwise(4, zz, invT).then_inc(s_inv.sem, s_inv.up())

                pe.wait_ge(s_invsb.sem, s_invsb.at(t, LEVELS - 1))
                for c in range(4):
                    units = [(b, g, (b * 4 + c) * 2 + g, b * 4 + c) for b in range(B) for g in range(2)]

                    def into(bk, col, left, right, first):
                        last = None
                        apart()
                        for n, (b, g, p, cb) in enumerate(units):
                            for j in range(2):
                                q = slice(64 * j, 64 * j + 64)
                                o = 64 * (2 * b + g)
                                last = mm(ps[q, bk, o:o + 64], left(q, b, g, p, cb), right(q, b, g, p, cb),
                                          start=(first and n == 0), stop=True, skip_group_check=True)
                        return last

                    yb = 1 + c % 2
                    a_t = lambda q, b, g, p, cb: ari[q, g, cb, 0, :]
                    r_t = lambda q, b, g, p, cb: ari[q, g, cb, 1, :]
                    st = lambda q, b, g, p, cb: state[q, b, g, :]
                    vv = lambda q, b, g, p, cb: v_st[q, cb, g, :]
                    gg = lambda q, b, g, p, cb: g_sb[q, b, g, :]
                    uu = lambda q, b, g, p, cb: u_sb[q, b, g, :]
                    prod = lambda k: (lambda q, b, g, p, cb: am[q, p, k, :])
                    into(6, 0, prod(3), vv, True)
                    if c:
                        pe.wait_ge(s_state.sem, s_state.at(t, c))
                    elif True:
                        pe.wait_ge(s_state.sem, s_state.at(t, 4, back=1))
                    into(6, 0, a_t, st, False).then_inc(s_g.sem, s_g.up())
                    if c >= 2:
                        pe.wait_ge(s_ysb.sem, s_ysb.at(t, c - 1))
                    into(yb, 0, st, r_t, True)
                    into(yb, 0, vv, prod(4), False)
                    into(0, 0, prod(5), vv, True)
                    pe.wait_ge(s_gsb.sem, s_gsb.at(t, c + 1))
                    into(7, 0, lambda q, b, g, p, cb: invT[q, p, :], gg, True).then_inc(s_u.sem, s_u.up())
                    pe.wait_ge(s_usb.sem, s_usb.at(t, c + 1))
                    into(0, 0, prod(2), uu, False).then_inc(s_sn.sem, s_sn.up())
                    into(yb, 0, uu, prod(1), False).then_inc(s_y.sem, s_y.up())

                pe.wait_ge(s_ysb.sem, s_ysb.at(t, 4))
                for h in range(2):
                    last = mm(ps[:, 3 + h, :], ones64, yT[:, h, :], start=True, stop=True)
                last.then_inc(s_mean.sem, s_mean.up())
                pe.wait_ge(s_ycsq.sem, s_ycsq.at(t, 1))
                for h in range(2):
                    last = mm(ps[:, 5 + h, :], ones64, sq[:, h, :], start=True, stop=True)
                last.then_inc(s_gvar.sem, s_gvar.up())
                pe.wait_ge(s_yg.sem, s_yg.at(t, 1))
                for s in range(4):
                    for h in range(2):
                        last = mm(ps[:, 1 + s // 2, 256 * (s % 2):256 * (s % 2) + 256],
                                  yg[:, h, 128 * s:128 * s + 128], w_in["W_o"][:, h, :],
                                  start=(h == 0), stop=(h == 1))
                last.then_inc(s_out.sem, s_out.up())

        @block.scalar
        def _(act):
            for q in (s_std, s_xt, took["A"], s_sq, s_exp, s_zsb, s_ysb, s_ycsq, s_gstd, s_outsb):
                q.open(act)
            act.wait_ge(s_const, keep["n_const"])
            f = nc.scalar.activation
            eps_ln, eps_gn = const("eps", 0, 1), const("eps", 1, 2)
            with act.Fori(0, NT) as t:
                act.wait_ge(s_var.sem, s_var.at(t, 1))
                f(std[:, :], mv[:, :, 1], ACT.Sqrt, bias=eps_ln, scale=1.0).then_inc(s_std.sem, s_std.up())
                for h in range(2):
                    act.wait_ge(s_tr.sem, s_tr.at(t, h + 1))
                    nc.scalar.copy(xn_all[:, h, :, bass.ds(t * TT + 1, TT)],
                                               ps[:, h, :].rearrange("p (b t) -> p b t", b=B)).then_inc(s_xt.sem, s_xt.up())

                def take(name, out, func, **kw):
                    act.wait_ge(s_job.sem, s_job.at(t, job_no[name] + 1))
                    m = 64 if name == "w1" else 128
                    f(out, ps[0:m, bank(name), :], func, **kw).then_inc(took["A"].sem, took["A"].up())

                take("g1", tg[:, :], ACT.Sigmoid)
                take("w1", tw[:, :], ACT.Tanh)
                for h in range(2):
                    take(f"w2{h}", sg[:, h, :], ACT.Sigmoid, bias=v("w0", h), scale=1.0)
                for h in range(2):
                    take(f"a2{h}", av[:, h, :], ACT.Sigmoid, bias=v("a0", h), scale=1.0)
                for h in range(2):
                    take(f"r{h}", rT[:, h, :], ACT.Copy)
                for h in range(2):
                    take(f"v{h}", vT[:, h, :], ACT.Copy)
                act.wait_ge(s_kk.sem, s_kk.at(t, 1))
                f(sq[:, :, :], kk[:, :, :], ACT.Square).then_inc(s_sq.sem, s_sq.up())
                for h in range(2):
                    take(f"n{h}", nrm[:, h, :], ACT.Sqrt)
                act.wait_ge(s_cs.sem, s_cs.at(t, 1))
                f(p_now[:, :, :], cs[:, :, :], ACT.Exp, scale=-NEG_DECAY)
                f(p_inv[:, :, :], cs[:, :, :], ACT.Exp, scale=NEG_DECAY)
                f(p_prev[:, :, :], csp[:, :, :], ACT.Exp, scale=-NEG_DECAY).then_inc(s_exp.sem, s_exp.up())
                for lev in range(LEVELS - 1):
                    act.wait_ge(s_z.sem, s_z.at(t, lev + 1))
                    f(zz[:, :, :].rearrange("p a c -> p (a c)"),
                                   ps[:, 0:2, :].rearrange("p a c -> p (a c)"), ACT.Copy).then_inc(s_zsb.sem, s_zsb.up())
                for c in range(4):
                    act.wait_ge(s_y.sem, s_y.at(t, c + 1))
                    nc.scalar.copy(
                        both(yT)[:, :, :, 64 * c:64 * c + 64],
                        ps[:, 1 + c % 2, 0:256].rearrange("p (b g v) -> p g b v", b=2, g=2)).then_inc(s_ysb.sem, s_ysb.up())
                act.wait_ge(s_yc.sem, s_yc.at(t, 1))
                f(sq[:, :, :], yc[:, :, :], ACT.Square).then_inc(s_ycsq.sem, s_ycsq.up())
                act.wait_ge(s_gvar.sem, s_gvar.at(t, 1))
                f(nrm[:, :, :].rearrange("p a c -> p (a c)"),
                                ps[:, 5:7, :].rearrange("p a c -> p (a c)"), ACT.Sqrt,
                                bias=eps_gn, scale=1.0 / RD).then_inc(s_gstd.sem, s_gstd.up())
                act.wait_ge(s_out.sem, s_out.at(t, 1))
                act.wait_ge(s_store.sem, s_store.at(t, 1, back=1))
                f(s_tok[:, :, :].rearrange("p a c -> p (a c)"),
                                 ps[:, 1:3, :].rearrange("p a c -> p (a c)"), ACT.Copy).then_inc(s_outsb.sem, s_outsb.up())

        @block.vector
        def _(dve):
            for q in (s_var, s_xn, s_mix, took["V"], s_kk, s_cs, s_rk, s_feat, s_amsb, s_lj, s_invsb,
                      s_gsb, s_usb, s_state, s_yc, s_yg, dve_step):
                q.open(dve)
            dve.wait_ge(s_const, keep["n_const"])
            vec_ = nc.vector
            vec_.memset(state[:, :, :, :], 0.0)
            vec_.memset(xn_all[:, :, :, 0:1], 0.0)
            for g in range(2):
                last = vec_.tensor_copy(ari[:, g, :, 2, :], const("eye64").unsqueeze(1).to_broadcast([128, CB, 64]))
            last.then_inc(s_init.sem, 1)
            dve.wait_ge(s_init.sem, 1)
            with dve.Fori(0, NT) as t:
                dve.wait_ge(s_x.sem, s_x.at(t, 1))
                for s in range(4):
                    last = vec_.bn_stats(bn6[:, s, :], x_tok[:, s, :])
                last.then_inc(dve_step.sem, dve_step.up())
                dve.wait_ge(dve_step.sem, dve_step.at(t))
                dve.sem_inc(s_passed, 1)
                for s in range(4):
                    last = vec_.bn_aggr(mv[:, s, :], bn6[:, s, :])
                last.then_inc(s_var.sem, s_var.up())
                dve.wait_ge(s_var.sem, s_var.at(t))
                dve.wait_ge(s_std.sem, s_std.at(t, 1))
                vec_.reciprocal(rstd[:, :], std[:, :]).then_inc(dve_step.sem, dve_step.up())
                dve.wait_ge(dve_step.sem, dve_step.at(t))
                dve.wait_ge(s_tr.sem, s_tr.at(t, 2, back=1))
                for s in range(4):
                    last = vec_.tensor_scalar(xn_tok[:, s, :], x_tok[:, s, :], mv[:, s, 0:1], rstd[:, s:s + 1],
                                              ALU.subtract, ALU.mult)
                last.then_inc(s_xn.sem, s_xn.up())
                dve.wait_ge(s_xt.sem, s_xt.at(t, 2))
                now = xn_all[:, :, :, bass.ds(t * TT + 1, TT)]
                before = xn_all[:, :, :, bass.ds(t * TT, TT)]
                dve.wait_ge(s_yg.sem, s_yg.at(t, 1, back=1))
                vec_.tensor_tensor(both(dx), before, now, ALU.subtract).then_inc(dve_step.sem, dve_step.up())
                dve.wait_ge(dve_step.sem, dve_step.at(t))
                for n in "gwakrv":
                    for h in range(2):
                        last = vec_.scalar_tensor_tensor(
                            mixed[n][:, h, :].rearrange("p (b t) -> p b t", b=B),
                            dx[:, h, :].rearrange("p (b t) -> p b t", b=B), v("x_" + n, h),
                            xn_all[:, h, :, bass.ds(t * TT + 1, TT)], ALU.mult, ALU.add)
                    last.then_inc(s_mix.sem, s_mix.up())

                def take(name, out):
                    dve.wait_ge(s_job.sem, s_job.at(t, job_no[name] + 1))
                    m = 64 if name == "a1" else 128
                    vec_.tensor_copy(out, ps[0:m, bank(name), :]).then_inc(took["V"].sem, took["V"].up())

                take("a1", ta[:, :])
                take("k0", kraw[:, 0, :])
                take("k1", kraw[:, 1, :])
                dve.wait_ge(took["V"].sem, took["V"].at(t))
                for h in range(2):
                    last = vec_.tensor_scalar(kk[:, h, :], kraw[:, h, :], v("k_k", h), None, ALU.mult)
                last.then_inc(s_kk.sem, s_kk.up())
                dve.wait_ge(took["A"].sem, took["A"].at(t, taken["a21"][1]))
                for h in range(2):
                    last = vec_.tensor_scalar(kmod[:, h, :], av[:, h, :], 1.0, v("k_a", h), ALU.subtract, ALU.mult)
                last.then_inc(dve_step.sem, dve_step.up())
                dve.wait_ge(dve_step.sem, dve_step.at(t))
                vec_.scalar_tensor_tensor(kmod[:, :, :], kmod[:, :, :], 1.0, kraw[:, :, :], ALU.add, ALU.mult).then_inc(dve_step.sem, dve_step.up())
                dve.wait_ge(dve_step.sem, dve_step.at(t))
                take("g20", gT[:, 0, :])
                take("g21", gT[:, 1, :])
                for q in range(2):
                    take(f"s{q}", v_st[:, 4 * q:4 * q + 4, :, :].rearrange("p a g d -> p (a g d)"))
                for h in range(2):
                    last = vec_.tensor_tensor_scan(cs[:, h, :], const("reset"), sg[:, h, :], 0.0, ALU.mult, ALU.add)
                last.then_inc(dve_step.sem, dve_step.up())
                dve.wait_ge(dve_step.sem, dve_step.at(t))
                vec_.tensor_tensor(csp[:, :, :], cs[:, :, :], sg[:, :, :], ALU.subtract).then_inc(s_cs.sem, s_cs.up())
                dve.wait_ge(s_cs.sem, s_cs.at(t))
                dve.wait_ge(took["A"].sem, took["A"].at(t, taken["r1"][1]))
                for h in range(2):
                    last = vec_.scalar_tensor_tensor(tmp[:, h, :], rT[:, h, :], v("r_k", h), kmod[:, h, :],
                                                     ALU.mult, ALU.mult)
                last.then_inc(s_rk.sem, s_rk.up())
                dve.wait_ge(s_rk.sem, s_rk.at(t))
                dve.wait_ge(took["A"].sem, took["A"].at(t, taken["n1"][1]))
                vec_.tensor_scalar(nrm[:, :, :], nrm[:, :, :], 1e-12, None, ALU.max).then_inc(dve_step.sem, dve_step.up())
                dve.wait_ge(dve_step.sem, dve_step.at(t))
                vec_.reciprocal(nrm[:, :, :], nrm[:, :, :]).then_inc(dve_step.sem, dve_step.up())
                dve.wait_ge(dve_step.sem, dve_step.at(t))
                vec_.tensor_tensor(kk[:, :, :], kk[:, :, :], nrm[:, :, :], ALU.mult).then_inc(dve_step.sem, dve_step.up())
                dve.wait_ge(dve_step.sem, dve_step.at(t))
                vec_.tensor_tensor(av[:, :, :], kk[:, :, :], av[:, :, :], ALU.mult).then_inc(dve_step.sem, dve_step.up())
                dve.wait_ge(dve_step.sem, dve_step.at(t))
                dve.wait_ge(s_exp.sem, s_exp.at(t, 1))

                def cut(ap):
                    return ap.rearrange("p (c t) -> p c t", c=CB)

                for h in range(2):
                    vec_.scalar_tensor_tensor(ari[:, h, :, 0, :], cut(kk[:, h, :]), -1.0, cut(p_prev[:, h, :]),
                                              ALU.mult, ALU.mult)
                    vec_.tensor_tensor(ari[:, h, :, 1, :], cut(rT[:, h, :]), cut(p_now[:, h, :]), ALU.mult)
                    vec_.tensor_tensor(bT[:, h, :, :], cut(av[:, h, :]), cut(p_inv[:, h, :]), ALU.mult)
                    vec_.tensor_tensor(kT[:, h, :, :], cut(kmod[:, h, :]), cut(p_inv[:, h, :]), ALU.mult)
                for h in range(2):
                    dve.wait_ge(s_job.sem, s_job.at(t, job_no[f"b{h}"] + 1))
                    vec_.tensor_tensor(bonus[:, h, :], ps[:, bank(f"b{h}"), :], vT[:, h, :], ALU.mult).then_inc(took["V"].sem, took["V"].up())
                vec_.tensor_copy(stmp[:, 0, 0, 0:1], const("eps", 0, 1)).then_inc(s_feat.sem, s_feat.up())
                for p in range(PAIRS):
                    dve.wait_ge(s_am.sem, s_am.at(t, p + 1))
                    vec_.tensor_tensor(am[:, p, :, :].rearrange("p a c -> p (a c)"),
                                                         ps[:, p % 8, 0:448], const("amask"), ALU.mult).then_inc(s_amsb.sem, s_amsb.up())
                dve.wait_ge(s_amsb.sem, s_amsb.at(t, PAIRS))

                def wide(name, lo=0, hi=64):
                    return const(name, lo, hi).unsqueeze(1).to_broadcast([128, PAIRS, 64])

                vec_.tensor_tensor(inv[:, :, :], am[:, :, 6, :], wide("low0"), ALU.mult)
                vec_.tensor_tensor(invT[:, :, :], am[:, :, 0, :], wide("low0t"), ALU.mult).then_inc(dve_step.sem, dve_step.up())
                dve.wait_ge(dve_step.sem, dve_step.at(t))
                vec_.tensor_tensor(inv[:, :, :], inv[:, :, :], wide("eye64"), ALU.add)
                vec_.tensor_tensor(invT[:, :, :], invT[:, :, :], wide("eye64"), ALU.add).then_inc(dve_step.sem, dve_step.up())
                dve.wait_ge(dve_step.sem, dve_step.at(t))
                for lev in range(LEVELS - 1):
                    vec_.tensor_tensor(lj[lev % 2][:, :, :], am[:, :, 0, :],
                                                   wide("lev", 64 * lev, 64 * lev + 64), ALU.mult).then_inc(s_lj.sem, s_lj.up())
                    dve.wait_ge(s_inv.sem, s_inv.at(t, lev + 1))
                    flat = lambda a: a[:, :, :].rearrange("p a c -> p (a c)")
                    vec_.tensor_tensor(flat(inv), flat(inv), ps[:, 2:4, :].rearrange("p a c -> p (a c)"), ALU.add)
                    vec_.tensor_tensor(flat(invT), flat(invT), ps[:, 4:6, :].rearrange("p a c -> p (a c)"), ALU.add).then_inc(s_invsb.sem, s_invsb.up())
                    dve.wait_ge(s_invsb.sem, s_invsb.at(t))
                for c in range(4):
                    fl = lambda a: a[:, :, :, :].rearrange("p b g v -> p (b g v)")
                    dve.wait_ge(s_g.sem, s_g.at(t, c + 1))
                    vec_.tensor_copy(fl(g_sb), ps[:, 6, 0:256]).then_inc(s_gsb.sem, s_gsb.up())
                    dve.wait_ge(s_u.sem, s_u.at(t, c + 1))
                    s_y_prev = None
                    vec_.tensor_copy(fl(u_sb), ps[:, 7, 0:256]).then_inc(s_usb.sem, s_usb.up())
                    dve.wait_ge(s_sn.sem, s_sn.at(t, c + 1))
                    vec_.tensor_tensor(fl(stmp), fl(state), ps[:, 0, 0:256], ALU.add).then_inc(dve_step.sem, dve_step.up())
                    dve.wait_ge(dve_step.sem, dve_step.at(t))
                    end = both(p_now)[:, :, :, 64 * c + 63:64 * c + 64].rearrange("p g b o -> p b g o")
                    vec_.tensor_tensor(state[:, :, :, :], stmp[:, :, :, :],
                                            end.to_broadcast([128, B, 2, 64]), ALU.mult).then_inc(s_state.sem, s_state.up())
                    dve.wait_ge(s_state.sem, s_state.at(t))
                dve.wait_ge(s_mean.sem, s_mean.at(t, 1))
                for h in range(2):
                    last = vec_.scalar_tensor_tensor(yc[:, h, :], ps[:, 3 + h, :], -1.0 / RD, yT[:, h, :],
                                                     ALU.mult, ALU.add)
                last.then_inc(s_yc.sem, s_yc.up())
                dve.wait_ge(s_yc.sem, s_yc.at(t))
                dve.wait_ge(s_gstd.sem, s_gstd.at(t, 1))
                vec_.reciprocal(nrm[:, :, :], nrm[:, :, :]).then_inc(dve_step.sem, dve_step.up())
                dve.wait_ge(dve_step.sem, dve_step.at(t))
                vec_.tensor_tensor(yc[:, :, :], yc[:, :, :], nrm[:, :, :], ALU.mult).then_inc(dve_step.sem, dve_step.up())
                dve.wait_ge(dve_step.sem, dve_step.at(t))
                for h in range(2):
                    last = vec_.tensor_scalar(yc[:, h, :], yc[:, h, :], v("ln_w", h), v("ln_b", h), ALU.mult, ALU.add)
                last.then_inc(dve_step.sem, dve_step.up())
                dve.wait_ge(dve_step.sem, dve_step.at(t))
                vec_.tensor_tensor(yc[:, :, :], yc[:, :, :], bonus[:, :, :], ALU.add).then_inc(dve_step.sem, dve_step.up())
                dve.wait_ge(dve_step.sem, dve_step.at(t))
                vec_.tensor_tensor(yg[:, :, :], yc[:, :, :], gT[:, :, :], ALU.mult).then_inc(s_yg.sem, s_yg.up())
                dve.wait_ge(s_yg.sem, s_yg.at(t))
                dve_step.whole()


def qkv_phase(nc, io, keep, signal):
    ctx = ExitStack()
    with ctx:
        def sb(name, shape, dt=FP32):
            return ctx.enter_context(nc.sbuf_tensor("q_" + name, shape, dt))

        def sig(name, per, unit=1):
            return signal("q_" + name, per, unit)

        cst, at, vec, xn_all, v_all = (keep[n] for n in ("cst", "at", "vec", "xn_all", "v_all"))
        const = lambda name, lo=0, hi=None: cst[:, at[name][0] + lo:(at[name][0] + hi if hi is not None else at[name][1])]
        v = lambda name, h: vec[:, VECS.index(name), h:h + 1]
        w = {n: sb(n, [128, HALVES, C]) for n in ("wq", "wk", "wv")}
        xsq = sb("xsq", [128, HALVES, COLS])
        rms, hT = sb("rms", [128, COLS]), sb("hT", [128, HALVES, COLS])
        raw = {n: sb(n + "_raw", [128, HALVES, COLS]) for n in "qk"}
        sq = {n: sb(n + "_sq", [128, HALVES, COLS]) for n in "qk"}
        part = {n: sb(n + "_part", [128, 3, HALVES, COLS], BF16) for n in "qk"}
        ps = ctx.enter_context(nc.psum_tensor("q_ps", [128, 8, 512], FP32))
        s_w = sig("weights", 1, 48)
        s_xsq, s_ms, s_rms, s_h = sig("x_squared", 1), sig("x_sum", 1), sig("x_rms", 1), sig("h", 1)
        s_proj, s_raw, s_sq = sig("projected", 4), sig("raw", 4), sig("squared", 4)
        s_v, s_vsb = sig("v", 1), sig("v_kept", 1)
        s_sum, s_root = sig("head_sum", 2), sig("head_rms", 2)
        s_part, s_store = sig("parts", 2), sig("parts_stored", 1, 16 * 24)
        dve_step = sig("dve_step", 11)
        block = ctx.enter_context(nc.Block())

        @block.sync
        def _(sp):
            for n, t in w.items():
                sp.dma_start(t[:, :, :], io[n]).then_inc(s_w.sem, 16)
            s_store.open(sp)
            with sp.Fori(0, NT) as t:
                for i, n in enumerate("qk"):
                    sp.wait_ge(s_part.sem, s_part.at(t, i + 1))
                    for k in range(3):
                        for h in range(HALVES):
                            for b in range(B):
                                sp.dma_start(io[n + "_dram"][k, b, 128 * h:128 * h + 128, bass.ds(t * TT, TT)],
                                             part[n][:, k, h, TT * b:TT * b + TT]).then_inc(s_store.sem, 16)
            sp.wait_ge(s_store.sem, s_store.at(NT - 1, 1))

        @block.tensor
        def _(pe):
            for q in (s_ms, s_proj, s_v, s_sum):
                q.open(pe)
            pe.wait_ge(s_w.sem, 48)
            mm = nc.tensor.matmul
            with pe.Fori(0, NT) as t:
                pe.wait_ge(s_xsq.sem, s_xsq.at(t, 1))
                for h in range(2):
                    last = mm(ps[:, 0, :], const("ones128"), xsq[:, h, :], start=(h == 0), stop=(h == 1))
                last.then_inc(s_ms.sem, s_ms.up())
                pe.wait_ge(s_h.sem, s_h.at(t, 1))
                pe.wait_ge(s_part.sem, s_part.at(t, 2, back=1))
                for i, n in enumerate("qk"):
                    for h in range(2):
                        for k in range(2):
                            last = mm(ps[:, 1 + 2 * i + h, :], w["w" + n][:, k, 128 * h:128 * h + 128], hT[:, k, :],
                                      start=(k == 0), stop=(k == 1))
                        last.then_inc(s_proj.sem, s_proj.up())
                for s in range(4):
                    for k in range(2):
                        last = mm(ps[:, 5 + s // 2, 256 * (s % 2):256 * (s % 2) + 256], hT[:, k, 128 * s:128 * s + 128],
                                  w["wv"][:, k, :], start=(k == 0), stop=(k == 1))
                last.then_inc(s_v.sem, s_v.up())
                for i, n in enumerate("qk"):
                    pe.wait_ge(s_sq.sem, s_sq.at(t, 2 * i + 2))
                    for h in range(2):
                        last = mm(ps[:, 1 + 2 * i + h, :], const("ones16"), sq[n][:, h, :], start=True, stop=True)
                    last.then_inc(s_sum.sem, s_sum.up())

        @block.scalar
        def _(act):
            for q in (s_xsq, s_rms, s_raw, s_sq, s_vsb, s_root):
                q.open(act)
            f = nc.scalar.activation
            with act.Fori(0, NT) as t:
                act.wait_ge(s_ms.sem, s_ms.at(t, 1, back=1))
                f(xsq[:, :, :].rearrange("p h (b t) -> p h b t", b=B),
                               xn_all[:, :, :, bass.ds(t * TT + 1, TT)], ACT.Square).then_inc(s_xsq.sem, s_xsq.up())
                act.wait_ge(s_ms.sem, s_ms.at(t, 1))
                f(rms[:, :], ps[:, 0, :], ACT.Sqrt, bias=const("eps", 2, 3), scale=1.0 / C).then_inc(s_rms.sem, s_rms.up())
                for i, n in enumerate("qk"):
                    for h in range(2):
                        act.wait_ge(s_proj.sem, s_proj.at(t, 2 * i + h + 1))
                        f(raw[n][:, h, :], ps[:, 1 + 2 * i + h, :], ACT.Copy).then_inc(s_raw.sem, s_raw.up())
                        f(sq[n][:, h, :], ps[:, 1 + 2 * i + h, :], ACT.Square).then_inc(s_sq.sem, s_sq.up())
                act.wait_ge(s_v.sem, s_v.at(t, 1))
                nc.scalar.copy(v_all[:, :, bass.ds(t * 2, 2), :],
                                            ps[:, 5:7, :].rearrange("p b (s c) -> p b s c", s=2)).then_inc(s_vsb.sem, s_vsb.up())
                for i, (n, scale, eps) in enumerate((("q", 1.0, 3), ("k", 1.0 / AD, 2))):
                    act.wait_ge(s_sum.sem, s_sum.at(t, i + 1))
                    act.wait_ge(s_raw.sem, s_raw.at(t, 2 * i + 2))
                    f(sq[n][:, :, :].rearrange("p h c -> p (h c)"),
                                    ps[:, 1 + 2 * i:3 + 2 * i, :].rearrange("p h c -> p (h c)"), ACT.Sqrt,
                                    bias=const("eps", eps, eps + 1), scale=scale).then_inc(s_root.sem, s_root.up())

        @block.vector
        def _(dve):
            for q in (s_h, s_part, dve_step):
                q.open(dve)
            ve = nc.vector
            with dve.Fori(0, NT) as t:
                dve.wait_ge(s_rms.sem, s_rms.at(t, 1))
                ve.reciprocal(rms[:, :], rms[:, :]).then_inc(dve_step.sem, dve_step.up())
                dve.wait_ge(dve_step.sem, dve_step.at(t))
                for h in range(2):
                    last = ve.scalar_tensor_tensor(hT[:, h, :].rearrange("p (b t) -> p b t", b=B),
                                                   xn_all[:, h, :, bass.ds(t * TT + 1, TT)], v("n1_w", h),
                                                   rms[:, :].rearrange("p (b t) -> p b t", b=B), ALU.mult, ALU.mult)
                last.then_inc(s_h.sem, s_h.up())
                for i, n in enumerate("qk"):
                    hi, mid, lo = (part[n][:, k, :, :] for k in range(3))
                    dve.wait_ge(s_root.sem, s_root.at(t, i + 1))
                    ve.reciprocal(sq[n][:, :, :], sq[n][:, :, :]).then_inc(dve_step.sem, dve_step.up())
                    dve.wait_ge(dve_step.sem, dve_step.at(t))
                    for h in range(2):
                        last = ve.scalar_tensor_tensor(raw[n][:, h, :], raw[n][:, h, :], v(n + "n_w", h),
                                                       sq[n][:, h, :], ALU.mult, ALU.mult)
                    last.then_inc(dve_step.sem, dve_step.up())
                    dve.wait_ge(dve_step.sem, dve_step.at(t))
                    dve.wait_ge(s_store.sem, s_store.at(t, 1, back=1))
                    ve.tensor_copy(hi, raw[n][:, :, :]).then_inc(dve_step.sem, dve_step.up())
                    dve.wait_ge(dve_step.sem, dve_step.at(t))
                    ve.tensor_tensor(raw[n][:, :, :], raw[n][:, :, :], hi, ALU.subtract).then_inc(dve_step.sem, dve_step.up())
                    dve.wait_ge(dve_step.sem, dve_step.at(t))
                    ve.tensor_copy(mid, raw[n][:, :, :]).then_inc(dve_step.sem, dve_step.up())
                    dve.wait_ge(dve_step.sem, dve_step.at(t))
                    last = ve.tensor_tensor(lo, raw[n][:, :, :], mid, ALU.subtract)
                    last.then_inc(s_part.sem, s_part.up())
                    dve.wait_ge(s_part.sem, s_part.at(t))
                dve_step.whole()


PARTS_Q, PARTS_K = (0, 0, 0, 1, 1, 2), (0, 1, 2, 0, 1, 0)
NP = 6 * AD
NROW = NP + 2
KTS, QC = T // 128, T // 512
LAG, UNTIL = 8, 37


def attention_phase(nc, io, keep, signal):
    ctx = ExitStack()
    with ctx:
        def sb(name, shape, dt=FP32):
            return ctx.enter_context(nc.sbuf_tensor("a_" + name, shape, dt))

        def sig(name, per, unit=1):
            return signal("a_" + name, per, unit)

        cst, at, v_all = keep["cst"], keep["at"], keep["v_all"]
        const = lambda name, lo=0, hi=None: cst[:, at[name][0] + lo:(at[name][0] + hi if hi is not None else at[name][1])]
        cb16 = sb("masks", [128, 3, 128], BF16)
        qa = [sb(f"qa{b}", [NROW, 4, T], BF16) for b in range(B)]
        ka = [sb(f"ka{b}", [NROW, 4, T], BF16) for b in range(B)]
        v_st = [sb(f"v_st{b}", [128, KTS, 4, 32]) for b in range(B)]
        pt = [[sb(f"pt{x}{i}", [128, 2, 512]) for i in range(2)] for x in range(2)]
        o_sb = [sb(f"o_sb{b}", [128, T]) for b in range(B)]
        mx = sb("mx", [128, 4, KTS, 4])
        m = sb("m", [128, 4 * KTS])
        mt, mrow = sb("mt", [4 * KTS, 128]), sb("mrow", [4 * KTS, 2, 128], BF16)
        sc = [ctx.enter_context(nc.psum_tensor(f"a_sc{x}", [128, 2, 512], FP32)) for x in range(2)]
        po = [ctx.enter_context(nc.psum_tensor(f"a_po{x}", [128, 512], FP32)) for x in range(2)]
        pm = [ctx.enter_context(nc.psum_tensor(f"a_pm{x}", [128, 512], FP32)) for x in range(2)]

        STEPS = [(qc, j) for qc in range(QC) for j in range(4 * qc + 4)]
        NS = len(STEPS)
        UNITS = [(qt, kc, h) for qt in range(KTS) for kc in range(qt // 4 + 1) for h in range(4)]
        NU = len(UNITS)

        def units_of(step):
            a, b = (max(0, min(NU, (s - LAG) * NU // (UNTIL - LAG))) for s in (step, step + 1))
            return range(a, b)

        s_passed = sig("passed", 1).sem
        s_load = [sig(f"loaded{b}", 1, 16 * 12) for b in range(B)]
        s_vst = [sig(f"v_ready{b}", 1) for b in range(B)]
        s_ones, s_one = sig("ones", 1), sig("dve_ones", 1)
        s_sc = [sig(f"scores{x}", B * NS) for x in range(2)]
        s_p = [sig(f"weights{x}", B * NS) for x in range(2)]
        s_pv = sig("summed", B * NS)
        s_o = sig("out_kept", B * QC)
        s_max, s_red = sig("max_scores", B * NU), sig("max_found", B * NU)
        s_m, s_mt, s_mrow = sig("m", B), sig("m_transposed", B), sig("m_rows", B)
        s_mload = [sig(f"m_loaded{b}", 1, 16 * 2) for b in range(B)]
        s_ostore = [sig(f"o_stored{b}", 1, 16) for b in range(B)]
        dve_step = sig("dve_step", 2 * B)
        block = ctx.enter_context(nc.Block())

        def load(sp, b, hg):
            for tile, n, parts in ((qa[b], "q", PARTS_Q), (ka[b], "k", PARTS_K)):
                for r, k in enumerate(parts):
                    src = io[n + "_dram"][k, b, bass.ds(hg * 64, 64), :]
                    sp.dma_start(tile[AD * r:AD * r + AD, :, :], src.rearrange("(h d) t -> d h t", d=AD)
                                 ).then_inc(s_load[b].sem, 16)

        def load_rows(sp, b, turn):
            for k in range(2):
                sp.dma_start(qa[b][NP + k:NP + k + 1, :, :].rearrange("o h (q t) -> o (h q) t", t=128),
                             mrow[:, k, :]).then_inc(s_mload[b].sem, 16)

        @block.sync
        def _(sp):
            for b in range(B):
                s_mload[b].open(sp)
                s_ostore[b].open(sp)
            load(sp, 0, 0)
            sp.wait_ge(s_mrow.sem, B)
            load_rows(sp, 0, 0)
            s_load[1].open(sp)
            with sp.Fori(0, 4) as u:
                sp.wait_ge(s_pv.sem, s_pv.at(u, 2 * NS, back=1))
                load(sp, 1, u)
                sp.wait_ge(s_mrow.sem, s_mrow.at(u, 1))
                load_rows(sp, 1, u)
                sp.wait_ge(s_o.sem, s_o.at(u, QC))
                sp.dma_start(io["o_dram"][0, bass.ds(u * 128, 128), :], o_sb[0][:, :]).then_inc(s_ostore[0].sem, 16)
                sp.wait_ge(s_pv.sem, s_pv.at(u, NS))
                load(sp, 0, (u + 1) % 4)
                sp.wait_ge(s_mrow.sem, s_mrow.at(u, 2))
                load_rows(sp, 0, u)
                sp.wait_ge(s_o.sem, s_o.at(u, 2 * QC))
                sp.dma_start(io["o_dram"][1, bass.ds(u * 128, 128), :], o_sb[1][:, :]).then_inc(s_ostore[1].sem, 16)
            for b in range(B):
                sp.wait_ge(s_ostore[b].sem, s_ostore[b].at(3, 1))
            sp.wait_ge(s_mload[0].sem, 32 * 6)

        @block.gpsimd
        def _(pool):
            for b in range(B):
                nc.gpsimd.memset(v_st[b][:, :, :, 16:32], 1.0).then_inc(s_ones.sem, 1)
                s_vst[b].open(pool)
            pool.wait_ge(s_ones.sem, B)
            with pool.Fori(0, 4) as u:
                for b in range(B):
                    pool.wait_ge(s_pv.sem, s_pv.at(u, NS * (b + 1), back=1))
                    nc.gpsimd.tensor_copy(
                        v_st[b][:, :, :, 0:16],
                        v_all[:, b, :, bass.ds(u * 64, 64)].rearrange("p k (h d) -> p k h d", h=4)).then_inc(s_vst[b].sem, s_vst[b].up())

        @block.tensor
        def _(pe):
            for q in (*s_sc, s_pv):
                q.open(pe)
            pe.wait_ge(s_ones.sem, B)
            pe.wait_ge(s_one.sem, 1)
            mm = nc.tensor.matmul
            ident16, neg_kq, neg_qk = (cb16[:, i, :] for i in range(3))

            def max_unit(b, i):
                qt, kc, h = UNITS[i]
                width = min(512, 128 * (qt + 1) - 512 * kc)
                diag = kc == qt // 4
                out = pm[i % 2]
                last = mm(out[:, 0:width], qa[b][0:NP, h, 128 * qt:128 * qt + 128],
                          ka[b][0:NP, h, 512 * kc:512 * kc + width], start=True, stop=not diag)
                if diag:
                    last = mm(out[:, width - 128:width], ident16, neg_qk, start=False, stop=True)
                return last

            pe.wait_ge(s_load[0].sem, 16 * 12)
            pe.sem_inc(s_max.sem, NU)
            for i in range(NU):
                if i >= 2:
                    pe.wait_ge(s_red.sem, NU + i - 1)
                max_unit(0, i).then_inc(s_max.sem, 1)
            pe.wait_ge(s_m.sem, B)
            nc.tensor.transpose(pm[0][0:4 * KTS, 0:128], m[:, :], const("ident")).then_inc(s_mt.sem, B)
            with pe.Fori(0, 4) as u:
                for b in range(B):
                    other = 1 - b

                    def scores(s, x, turn=u):
                        qc, j = STEPS[s]
                        off = max(0, 128 * (j - 4 * qc))
                        n = b * NS + s
                        if n:
                            pe.wait_ge(s_p[x].sem, s_p[x].at(u, n))
                        else:
                            pe.wait_ge(s_p[x].sem, s_p[x].at(u, B * NS, back=1))
                        for y in range(2):
                            h = 2 * x + y
                            diag = j >= 4 * qc
                            last = mm(sc[x][:, y, off:512], ka[b][:, h, 128 * j:128 * j + 128],
                                      qa[b][:, h, 512 * qc + off:512 * qc + 512], start=True, stop=not diag)
                            if diag:
                                last = mm(sc[x][:, y, off:off + 128], ident16, neg_kq, start=False, stop=True)
                        last.then_inc(s_sc[x].sem, s_sc[x].up())

                    pe.wait_ge(s_mload[b].sem, s_mload[1].at(u, 1) if b else u * 32 + 64)
                    pe.wait_ge(s_vst[b].sem, s_vst[b].at(u, 1))
                    scores(0, 0)
                    scores(0, 1)
                    for s, (qc, j) in enumerate(STEPS):
                        n = b * NS + s
                        off = max(0, 128 * (j - 4 * qc))
                        if s + 1 < NS:
                            scores(s + 1, 0)
                        us = units_of(s)
                        if us and us[0] == 0:
                            if b:
                                pe.wait_ge(s_load[0].sem, u * 192 + 384)
                            else:
                                pe.wait_ge(s_load[1].sem, s_load[1].at(u, 1))
                        for i in us:
                            k = b * NU + i
                            if k >= 2:
                                pe.wait_ge(s_red.sem, s_red.at(u, k - 1))
                            else:
                                pe.wait_ge(s_red.sem, s_red.at(u, B * NU + k - 1, back=1))
                            if i == 0:
                                pe.wait_ge(s_mrow.sem, s_mrow.at(u, 1) if b else s_mrow.at(u, 2, back=1))
                            max_unit(other, i).then_inc(s_max.sem, s_max.up())
                        if s + 1 < NS:
                            scores(s + 1, 1)
                        pe.wait_ge(s_p[0].sem, s_p[0].at(u, n + 1))
                        pe.wait_ge(s_p[1].sem, s_p[1].at(u, n + 1))
                        if j == 0:
                            o = b * QC + qc
                            if o >= 2:
                                pe.wait_ge(s_o.sem, s_o.at(u, o - 1))
                            else:
                                pe.wait_ge(s_o.sem, s_o.at(u, B * QC + o - 1, back=1))
                        for h in range(4):
                            last = mm(po[qc % 2][32 * h:32 * h + 32, off:512], v_st[b][:, j, h, :],
                                      pt[h // 2][n % 2][:, h % 2, off:512], start=(j == 0), stop=(j == 4 * qc + 3),
                                      tile_position=(0, 32 * h), skip_group_check=True)
                        last.then_inc(s_pv.sem, s_pv.up())
                        if s == UNTIL + 1:
                            pe.wait_ge(s_m.sem, s_m.at(u, b + 1))
                            pe.sem_inc(s_passed, 1)
                            nc.tensor.transpose(pm[0][0:4 * KTS, 0:128], m[:, :], const("ident")).then_inc(s_mt.sem, s_mt.up())

        @block.scalar
        def _(act):
            for q in s_p:
                q.open(act)
            with act.Fori(0, 4) as u:
                for b in range(B):
                    for s, (qc, j) in enumerate(STEPS):
                        n = b * NS + s
                        off = max(0, 128 * (j - 4 * qc))
                        if n >= 2:
                            act.wait_ge(s_pv.sem, s_pv.at(u, n - 1))
                        else:
                            act.wait_ge(s_pv.sem, s_pv.at(u, B * NS + n - 1, back=1))
                        for x in range(2):
                            act.wait_ge(s_sc[x].sem, s_sc[x].at(u, n + 1))
                            nc.scalar.activation(pt[x][n % 2][:, :, off:512], sc[x][:, :, off:512],
                                                               ACT.Exp).then_inc(s_p[x].sem, s_p[x].up())

        @block.vector
        def _(dve):
            ve = nc.vector
            s_o.open(dve)
            for b in range(B):
                ve.memset(ka[b][NP:NROW, :, :], 1.0)
            for i, name in enumerate(("ident", "neg_kq", "neg_qk")):
                ve.tensor_copy(cb16[:, i, :], const(name))
            ve.memset(mx[:, :, :, :], -3e38).then_inc(s_one.sem, 1)
            dve.wait_ge(s_one.sem, 1)

            def reduce_unit(i):
                qt, kc, h = UNITS[i]
                width = min(512, 128 * (qt + 1) - 512 * kc)
                return ve.tensor_reduce(mx[:, h, qt, kc:kc + 1], pm[i % 2][:, 0:width], axis=AX.X, op=ALU.max)

            by_tile = mx[:, :, :, :].rearrange("p h q k -> p (h q) k")
            dve.sem_inc(s_red.sem, NU)
            for i in range(NU):
                dve.wait_ge(s_max.sem, NU + i + 1)
                reduce_unit(i).then_inc(s_red.sem, 1)
            dve.wait_ge(s_red.sem, 2 * NU)
            ve.tensor_reduce(m[:, :], by_tile, axis=AX.X, op=ALU.max).then_inc(s_m.sem, B)
            dve.wait_ge(s_mt.sem, B)
            ve.tensor_scalar(mt[:, :], pm[0][0:4 * KTS, 0:128], -1.0, None, ALU.mult).then_inc(dve_step.sem, B)
            dve.wait_ge(dve_step.sem, B)
            ve.tensor_copy(mrow[:, 0, :], mt[:, :]).then_inc(dve_step.sem, B)
            dve.wait_ge(dve_step.sem, 2 * B)
            ve.tensor_tensor(mrow[:, 1, :], mt[:, :], mrow[:, 0, :], ALU.subtract).then_inc(s_mrow.sem, B)
            with dve.Fori(0, 4) as u:
                for b in range(B):
                    for s, (qc, j) in enumerate(STEPS):
                        us = units_of(s)
                        for i in us:
                            dve.wait_ge(s_max.sem, s_max.at(u, b * NU + i + 1))
                            reduce_unit(i).then_inc(s_red.sem, s_red.up())
                            if i == NU - 1:
                                dve.wait_ge(s_red.sem, s_red.at(u))
                                ve.tensor_reduce(m[:, :], by_tile, axis=AX.X, op=ALU.max).then_inc(s_m.sem, s_m.up())
                        if s == UNTIL + 1:
                            dve.wait_ge(s_mt.sem, s_mt.at(u, b + 1))
                            dve.wait_ge(s_mload[b].sem, s_mload[1].at(u, 1) if b else u * 32 + 64)
                            ve.tensor_scalar(mt[:, :], pm[0][0:4 * KTS, 0:128], -1.0, None, ALU.mult).then_inc(dve_step.sem, dve_step.up())
                            dve.wait_ge(dve_step.sem, dve_step.at(u))
                            ve.tensor_copy(mrow[:, 0, :], mt[:, :]).then_inc(dve_step.sem, dve_step.up())
                            dve.wait_ge(dve_step.sem, dve_step.at(u))
                            ve.tensor_tensor(mrow[:, 1, :], mt[:, :], mrow[:, 0, :], ALU.subtract).then_inc(s_mrow.sem, s_mrow.up())
                        if j == 4 * qc + 3:
                            dve.wait_ge(s_pv.sem, s_pv.at(u, b * NS + s + 1))
                            if qc == 0:
                                dve.wait_ge(s_ostore[b].sem, s_ostore[b].at(u, 1, back=1))
                            ve.tensor_copy(o_sb[b][:, 512 * qc:512 * qc + 512], po[qc % 2][:, :]).then_inc(s_o.sem, s_o.up())


STAGES = [("e0_up", "xf", "h0", "Gelu"), ("e2_l1", "xf", "h2", "Gelu"), ("e3_down", "xf", "h3", "Gelu"),
          ("e1_w1", "xf", "h1", "Silu"), ("e1_w2", "xf", "h1", "times"), ("e0_down", "h0", 0, "out"),
          ("e2_l2", "h2", "h4", "Gelu"), ("e1_down", "h1", 1, "out"), ("e3_up", "h3", "h5", "Gelu"),
          ("e2_l3", "h4", "h2", "Gelu"), ("e3_out", "h5", 3, "out"), ("e2_l4", "h2", 2, "out")]
WIDE = {"e0_up": (2, 4), "e2_l1": (2, 4), "e3_down": (2, 2), "e1_w1": (2, 4), "e1_w2": (2, 4),
        "e2_l2": (4, 4), "e3_up": (2, 4), "e2_l3": (4, 4),
        "e0_down": (4, 2), "e1_down": (4, 2), "e3_out": (4, 2), "e2_l4": (4, 2)}
MASKED = 64


def expert_phase(nc, io, keep, signal):
    ctx = ExitStack()
    with ctx:
        def sb(name, shape, dt=FP32):
            return ctx.enter_context(nc.sbuf_tensor("e_" + name, shape, dt))

        def sig(name, per, unit=1):
            return signal("e_" + name, per, unit)

        cst, at, vec, xn_all = (keep[n] for n in ("cst", "at", "vec", "xn_all"))
        const = lambda name, lo=0, hi=None: cst[:, at[name][0] + lo:(at[name][0] + hi if hi is not None else at[name][1])]
        v = lambda name, h: vec[:, VECS.index(name), h:h + 1]
        w = {n: sb(n, [128, i, 128 * o]) for n, (i, o) in WIDE.items()}
        w["wo"], w["gate_w"] = sb("wo", [128, 2, C]), sb("gate_w", [128, 2, EXPERTS])
        NW = len(w)
        ao, asum = sb("ao", [128, HALVES, COLS]), sb("asum", [128, HALVES, COLS])
        x2, xf = sb("x2", [128, HALVES, COLS]), sb("xf", [128, HALVES, COLS])
        rms = sb("rms", [128, COLS])
        hid = {f"h{i}": sb(f"h{i}", [128, 2 if i == 3 else 4, COLS]) for i in range(6)}
        hid["xf"] = xf
        acc, s_tok, x_tok = sb("acc", [128, 4, C]), sb("s_tok", [128, 4, C]), sb("x_tok", [128, 4, C])
        x2sq = hid["h3"]
        SE = [128, 4, EXPERTS]
        lg, ok_, zero, ex, pr, sel, wt = (sb(n, SE) for n in ("lg", "ok_", "zero", "ex", "pr", "sel", "wt"))
        okm = sb("okm", SE, mybir.dt.int32)
        mxl, den = sb("mxl", [128, 4]), sb("den", [128, 4])
        cmp_, eq = sb("cmp_", [128, 4, EXPERTS, EXPERTS]), sb("eq", [128, 4, EXPERTS, EXPERTS])
        ps = ctx.enter_context(nc.psum_tensor("e_ps", [128, 8, 512], FP32))

        s_w = sig("weights", 1, 16 * NW)
        s_in, s_ready_w = sig("inputs", 1, 16 * 24), sig("weights_masked", 1)
        s_ao, s_wo, s_x2, s_x2sq, s_ms, s_rms, s_xf = (sig(n, 1) for n in (
            "ao", "projected", "x2", "x2_squared", "x2_sum", "x2_rms", "xf"))
        s_gate, s_x2t, s_acc0, s_soft, s_exp, s_wt = (sig(n, 1) for n in (
            "logits", "x2_transposed", "x2_kept", "logits_shifted", "logits_exp", "gates"))
        BLOCKS = [(i, o) for i, (n, _, _, f) in enumerate(STAGES) if f != "out" for o in range(WIDE[n][1])]
        s_hid = sig("hidden", len(BLOCKS))
        by = {"A": sig("act_took", sum(STAGES[i][3] != "times" for i, _ in BLOCKS)),
              "V": sig("dve_took", sum(STAGES[i][3] == "times" for i, _ in BLOCKS))}
        took = []
        for i, o in BLOCKS:
            who = "V" if STAGES[i][3] == "times" else "A"
            took.append((who, 1 + sum(w_ == who for w_, _ in took)))
        first_block = {i: min(n for n, (k, _) in enumerate(BLOCKS) if k == i) for i in {i for i, _ in BLOCKS}}
        s_down, s_sum = sig("expert_out", 4), sig("expert_added", 4)
        s_gated, s_out = sig("silu", 1), sig("out", 1)
        s_store = sig("out_stored", 1, 16 * 4)
        s_passed = sig("passed", 1).sem
        dve_step = sig("dve_step", 21)
        block = ctx.enter_context(nc.Block())

        @block.sync
        def _(sp):
            for n, tile in w.items():
                sp.dma_start(tile[:, :, :], io[n]).then_inc(s_w.sem, 16)
            s_in.open(sp)
            s_store.open(sp)
            with sp.Fori(0, NT) as t:
                sp.wait_ge(s_out.sem, s_out.at(t, 1, back=1))
                for h in range(HALVES):
                    for b in range(B):
                        rows_ = io["o_dram"][b, :, bass.ds(t * TT, TT)].rearrange("(g h e) t -> g h e t", h=8, e=32)
                        for tile, lo in ((ao, 0), (asum, 16)):
                            for r in range(2):
                                sp.dma_start(tile[64 * r:64 * r + 64, h, TT * b:TT * b + TT],
                                             rows_[h, 4 * r:4 * r + 4, lo:lo + 16, :]).then_inc(s_in.sem, 16)
                for s in range(4):
                    tok = bass.ds(t * TT + (s % 2) * 128, 128)
                    sp.dma_start(s_tok[:, s, :], io["s_dram"][s // 2, tok, :]).then_inc(s_in.sem, 16)
                    sp.dma_start(x_tok[:, s, :], io["x"][s // 2, tok, :]).then_inc(s_in.sem, 16)
                sp.wait_ge(s_out.sem, s_out.at(t, 1))
                for s in range(4):
                    sp.dma_start(io["out"][s // 2, bass.ds(t * TT + (s % 2) * 128, 128), :],
                                 acc[:, s, :]).then_inc(s_store.sem, 16)
            sp.wait_ge(s_store.sem, s_store.at(NT - 1, 1))

        @block.tensor
        def _(pe):
            for q in (s_wo, s_ms, s_gate, s_x2t, s_hid, s_down):
                q.open(pe)
            pe.wait_ge(s_w.sem, 16 * NW)
            pe.wait_ge(s_ready_w.sem, 1)
            mm = nc.tensor.matmul
            with pe.Fori(0, NT) as t:
                pe.wait_ge(s_ao.sem, s_ao.at(t, 1))
                pe.wait_ge(s_sum.sem, s_sum.at(t, 4, back=1))
                for h in range(2):
                    for k in range(2):
                        last = mm(ps[:, h, :], w["wo"][:, k, 128 * h:128 * h + 128], ao[:, k, :], start=(k == 0), stop=(k == 1))
                last.then_inc(s_wo.sem, s_wo.up())
                pe.wait_ge(s_x2sq.sem, s_x2sq.at(t, 1))
                for h in range(2):
                    last = mm(ps[:, 2, :], const("ones128"), x2sq[:, h, :], start=(h == 0), stop=(h == 1))
                last.then_inc(s_ms.sem, s_ms.up())
                for s in range(4):
                    for h in range(2):
                        last = nc.tensor.transpose(ps[:, 4 + s // 2, 256 * (s % 2) + 128 * h:256 * (s % 2) + 128 * h + 128],
                                                   x2[:, h, 128 * s:128 * s + 128], const("ident"))
                last.then_inc(s_x2t.sem, s_x2t.up())
                pe.wait_ge(s_xf.sem, s_xf.at(t, 1))
                for s in range(4):
                    for h in range(2):
                        last = mm(ps[:, 3, 4 * s:4 * s + 4], xf[:, h, 128 * s:128 * s + 128], w["gate_w"][:, h, :],
                                  start=(h == 0), stop=(h == 1))
                last.then_inc(s_gate.sem, s_gate.up())
                pe.wait_ge(s_x2.sem, s_x2.at(t, 1))
                downs = 0
                written = {}
                for i, (name, src, dst, func) in enumerate(STAGES):
                    ins, outs = WIDE[name]
                    if src != "xf":
                        who, n = took[written[src]]
                        pe.wait_ge(by[who].sem, by[who].at(t, n))
                    if func == "out":
                        downs += 1
                        if downs > 1:
                            pe.wait_ge(s_sum.sem, s_sum.at(t, downs - 1))
                        for s in range(4):
                            for k in range(ins):
                                last = mm(ps[:, 6 + s // 2, 256 * (s % 2):256 * (s % 2) + 256],
                                          hid[src][:, k, 128 * s:128 * s + 128], w[name][:, k, :],
                                          start=(k == 0), stop=(k == ins - 1))
                        last.then_inc(s_down.sem, s_down.up())
                        continue
                    for o in range(outs):
                        n = first_block[i] + o
                        if n >= 4:
                            who, m = took[n - 4]
                            pe.wait_ge(by[who].sem, by[who].at(t, m))
                        elif n == 3:
                            pe.wait_ge(s_soft.sem, s_soft.at(t, 1))
                        for k in range(ins):
                            last = mm(ps[:, n % 4, :], w[name][:, k, 128 * o:128 * o + 128], hid[src][:, k, :],
                                      start=(k == 0), stop=(k == ins - 1))
                        last.then_inc(s_hid.sem, s_hid.up())
                        written[dst] = n

        @block.scalar
        def _(act):
            for q in (s_x2sq, s_rms, s_acc0, s_exp, by["A"], s_gated):
                q.open(act)
            f = nc.scalar.activation
            with act.Fori(0, NT) as t:
                act.wait_ge(s_x2.sem, s_x2.at(t, 1))
                f(x2sq[:, :, :], x2[:, :, :], ACT.Square).then_inc(s_x2sq.sem, s_x2sq.up())
                act.wait_ge(s_ms.sem, s_ms.at(t, 1))
                f(rms[:, :], ps[:, 2, :], ACT.Sqrt, bias=const("eps", 2, 3), scale=1.0 / C).then_inc(s_rms.sem, s_rms.up())
                act.wait_ge(s_x2t.sem, s_x2t.at(t, 1))
                act.wait_ge(s_store.sem, s_store.at(t, 1, back=1))
                f(acc[:, :, :].rearrange("p s c -> p (s c)"),
                                ps[:, 4:6, :].rearrange("p a c -> p (a c)"), ACT.Copy).then_inc(s_acc0.sem, s_acc0.up())
                act.wait_ge(s_soft.sem, s_soft.at(t, 1))
                f(ex[:, :, :], lg[:, :, :], ACT.Exp).then_inc(s_exp.sem, s_exp.up())
                for n, (i, o) in enumerate(BLOCKS):
                    name, src, dst, func = STAGES[i]
                    if func == "times":
                        continue
                    act.wait_ge(s_hid.sem, s_hid.at(t, n + 1))
                    f(hid[dst][:, o, :], ps[:, n % 4, :], ACT.Gelu if func == "Gelu" else ACT.Silu).then_inc(by["A"].sem, by["A"].up())
                act.wait_ge(s_sum.sem, s_sum.at(t, 4))
                f(acc[:, :, :], acc[:, :, :], ACT.Silu).then_inc(s_gated.sem, s_gated.up())

        @block.vector
        def _(dve):
            for q in (s_ao, s_x2, s_xf, s_soft, s_wt, by["V"], s_sum, s_out, dve_step):
                q.open(dve)
            ve = nc.vector
            dve.wait_ge(s_w.sem, 16 * NW)
            for n in ("wo", "e0_down", "e1_down", "e2_l4", "e3_out"):
                ve.memset(w[n][:, :, 0:MASKED], 0.0)
            ve.memset(zero[:, :, :], 0.0).then_inc(s_ready_w.sem, 1)
            dve.wait_ge(s_ready_w.sem, 1)
            with dve.Fori(0, NT) as t:
                dve.wait_ge(s_in.sem, s_in.at(t, 1))
                ve.reciprocal(asum[:, :, :], asum[:, :, :]).then_inc(dve_step.sem, dve_step.up())
                dve.wait_ge(dve_step.sem, dve_step.at(t))
                ve.tensor_tensor(ao[:, :, :], ao[:, :, :], asum[:, :, :], ALU.mult).then_inc(s_ao.sem, s_ao.up())
                dve.wait_ge(s_ao.sem, s_ao.at(t))
                dve.wait_ge(s_wo.sem, s_wo.at(t, 1))
                for h in range(2):
                    last = ve.tensor_tensor(x2[:, h, :].rearrange("p (b t) -> p b t", b=B),
                                            ps[:, h, :].rearrange("p (b t) -> p b t", b=B),
                                            xn_all[:, h, :, bass.ds(t * TT + 1, TT)], ALU.add)
                last.then_inc(s_x2.sem, s_x2.up())
                dve.wait_ge(s_x2.sem, s_x2.at(t))
                dve.wait_ge(s_rms.sem, s_rms.at(t, 1))
                ve.reciprocal(rms[:, :], rms[:, :]).then_inc(dve_step.sem, dve_step.up())
                dve.wait_ge(dve_step.sem, dve_step.at(t))
                for h in range(2):
                    last = ve.scalar_tensor_tensor(xf[:, h, :], x2[:, h, :], v("n2_w", h), rms[:, :], ALU.mult, ALU.mult)
                last.then_inc(s_xf.sem, s_xf.up())
                dve.wait_ge(s_xf.sem, s_xf.at(t))
                dve.wait_ge(s_gate.sem, s_gate.at(t, 1))
                ve.tensor_copy(lg[:, :, :], ps[:, 3, 0:16].rearrange("p (s e) -> p s e", e=EXPERTS)).then_inc(dve_step.sem, dve_step.up())
                dve.wait_ge(dve_step.sem, dve_step.at(t))
                ve.tensor_tensor(okm[:, :, :], lg[:, :, :], lg[:, :, :], ALU.is_equal).then_inc(dve_step.sem, dve_step.up())
                dve.wait_ge(dve_step.sem, dve_step.at(t))
                ve.tensor_copy(ok_[:, :, :], zero[:, :, :]).then_inc(dve_step.sem, dve_step.up())
                dve.wait_ge(dve_step.sem, dve_step.at(t))
                dve.sem_inc(s_passed, 1)
                ve.copy_predicated(ok_[:, :, :], okm[:, :, :], lg[:, :, :]).then_inc(dve_step.sem, dve_step.up())
                dve.wait_ge(dve_step.sem, dve_step.at(t))
                ve.tensor_scalar(ok_[:, :, :], ok_[:, :, :], 3.4028234e38, -3.4028234e38, ALU.min, ALU.max).then_inc(dve_step.sem, dve_step.up())
                dve.wait_ge(dve_step.sem, dve_step.at(t))
                ve.tensor_reduce(mxl[:, :], ok_[:, :, :], axis=AX.X, op=ALU.max).then_inc(dve_step.sem, dve_step.up())
                dve.wait_ge(dve_step.sem, dve_step.at(t))
                wide = lambda a: a.unsqueeze(2).to_broadcast([128, 4, EXPERTS])
                ve.tensor_tensor(lg[:, :, :], ok_[:, :, :], wide(mxl[:, :]), ALU.subtract).then_inc(s_soft.sem, s_soft.up())
                dve.wait_ge(s_soft.sem, s_soft.at(t))
                dve.wait_ge(s_exp.sem, s_exp.at(t, 1))
                ve.tensor_reduce(den[:, :], ex[:, :, :], axis=AX.X, op=ALU.add).then_inc(dve_step.sem, dve_step.up())
                dve.wait_ge(dve_step.sem, dve_step.at(t))
                ve.reciprocal(den[:, :], den[:, :]).then_inc(dve_step.sem, dve_step.up())
                dve.wait_ge(dve_step.sem, dve_step.at(t))
                ve.tensor_tensor(pr[:, :, :], ex[:, :, :], wide(den[:, :]), ALU.mult).then_inc(dve_step.sem, dve_step.up())
                dve.wait_ge(dve_step.sem, dve_step.at(t))
                other = pr[:, :, :].unsqueeze(2).to_broadcast([128, 4, EXPERTS, EXPERTS])
                this = pr[:, :, :].unsqueeze(3).to_broadcast([128, 4, EXPERTS, EXPERTS])
                ve.tensor_tensor(cmp_[:, :, :, :], other, this, ALU.is_gt)
                ve.tensor_tensor(eq[:, :, :, :], other, this, ALU.is_equal).then_inc(dve_step.sem, dve_step.up())
                dve.wait_ge(dve_step.sem, dve_step.at(t))
                earlier = const("earlier").rearrange("p (e j) -> p e j", j=EXPERTS).unsqueeze(1)\
                    .to_broadcast([128, 4, EXPERTS, EXPERTS])
                ve.tensor_tensor(eq[:, :, :, :], eq[:, :, :, :], earlier, ALU.mult).then_inc(dve_step.sem, dve_step.up())
                dve.wait_ge(dve_step.sem, dve_step.at(t))
                ve.tensor_tensor(cmp_[:, :, :, :], cmp_[:, :, :, :], eq[:, :, :, :], ALU.add).then_inc(dve_step.sem, dve_step.up())
                dve.wait_ge(dve_step.sem, dve_step.at(t))
                ve.tensor_reduce(sel[:, :, :], cmp_[:, :, :, :], axis=AX.X, op=ALU.add).then_inc(dve_step.sem, dve_step.up())
                dve.wait_ge(dve_step.sem, dve_step.at(t))
                ve.scalar_tensor_tensor(wt[:, :, :], sel[:, :, :], 2.0, pr[:, :, :], ALU.is_lt, ALU.mult).then_inc(dve_step.sem, dve_step.up())
                dve.wait_ge(dve_step.sem, dve_step.at(t))
                ve.tensor_reduce(den[:, :], wt[:, :, :], axis=AX.X, op=ALU.add).then_inc(dve_step.sem, dve_step.up())
                dve.wait_ge(dve_step.sem, dve_step.at(t))
                ve.tensor_scalar(den[:, :], den[:, :], 1e-8, None, ALU.add).then_inc(dve_step.sem, dve_step.up())
                dve.wait_ge(dve_step.sem, dve_step.at(t))
                ve.reciprocal(den[:, :], den[:, :]).then_inc(dve_step.sem, dve_step.up())
                dve.wait_ge(dve_step.sem, dve_step.at(t))
                ve.tensor_tensor(wt[:, :, :], wt[:, :, :], wide(den[:, :]), ALU.mult).then_inc(dve_step.sem, dve_step.up())
                dve.wait_ge(dve_step.sem, dve_step.at(t))
                dve.wait_ge(s_acc0.sem, s_acc0.at(t, 1))
                downs = 0
                for i, (name, src, dst, func) in enumerate(STAGES):
                    if func == "times":
                        for o in range(4):
                            n = first_block[i] + o
                            dve.wait_ge(s_hid.sem, s_hid.at(t, n + 1))
                            who, m = took[first_block[i - 1] + o]
                            dve.wait_ge(by[who].sem, by[who].at(t, m))
                            ve.tensor_tensor(hid[dst][:, o, :], ps[:, n % 4, :], hid[dst][:, o, :], ALU.mult).then_inc(by["V"].sem, by["V"].up())
                    if func == "out":
                        downs += 1
                        dve.wait_ge(s_down.sem, s_down.at(t, downs))
                        for s in range(4):
                            last = ve.scalar_tensor_tensor(acc[:, s, :], ps[:, 6 + s // 2, 256 * (s % 2):256 * (s % 2) + 256],
                                                           wt[:, s, dst:dst + 1], acc[:, s, :], ALU.mult, ALU.add)
                        last.then_inc(s_sum.sem, s_sum.up())
                        dve.wait_ge(s_sum.sem, s_sum.at(t))
                dve.wait_ge(s_gated.sem, s_gated.at(t, 1))
                ve.tensor_tensor(acc[:, :, :], acc[:, :, :], s_tok[:, :, :], ALU.mult).then_inc(dve_step.sem, dve_step.up())
                dve.wait_ge(dve_step.sem, dve_step.at(t))
                ve.tensor_tensor(acc[:, :, :], acc[:, :, :], x_tok[:, :, :], ALU.add).then_inc(s_out.sem, s_out.up())
                dve.wait_ge(s_out.sem, s_out.at(t))
                dve_step.whole()


def program(nc, io):
    ctx = ExitStack()
    with ctx:
        at, width = table_at()
        io["s_dram"] = nc.dram_tensor("s_scratch", (B, T, C), FP32, kind="Internal").ap()
        for n in "qk":
            io[n + "_dram"] = nc.dram_tensor(n + "_scratch", (3, B, C, T), BF16, kind="Internal").ap()
        io["o_dram"] = nc.dram_tensor("o_scratch", (B, AH * 32, T), FP32, kind="Internal").ap()
        keep = {"at": at, "r_dve_steps": 20, "n_const": 32}
        keep["cst"] = ctx.enter_context(nc.sbuf_tensor("cst", [128, width], FP32))
        keep["vec"] = ctx.enter_context(nc.sbuf_tensor("vec", [128, len(VECS), 2], FP32))
        keep["xn_all"] = ctx.enter_context(nc.sbuf_tensor("xn_all", [128, HALVES, B, T + 1], FP32))
        keep["s_const"] = ctx.enter_context(nc.semaphore("s_const"))

        def signal(name, per, unit=1):
            return Signal(ctx.enter_context(nc.semaphore(name)), per, unit)

        nc.sync.dma_start(keep["cst"][:, :], io["table"]).then_inc(keep["s_const"], 16)
        nc.sync.dma_start(keep["vec"][:, :, :], io["vecs"]).then_inc(keep["s_const"], 16)
        recurrent_phase(nc, io, keep, signal)
        with ExitStack() as v_life:
            keep["v_all"] = v_life.enter_context(nc.sbuf_tensor("v_all", [128, B, T // 128, C], FP32))
            qkv_phase(nc, io, keep, signal)
            attention_phase(nc, io, keep, signal)
        expert_phase(nc, io, keep, signal)


def host_tables():
    import numpy as np
    at, width = table_at()
    tab = np.zeros((128, width), np.float32)
    def put(name, a):
        tab[:, at[name][0]:at[name][1]] = a.reshape(128, -1)
    r = np.arange(128)
    put("ident", np.eye(128))
    put("neg_kq", (r[None] < r[:, None]) * -1e30)
    put("neg_qk", (r[None] > r[:, None]) * -1e30)
    put("ones64", (r[:, None] // 64 == r[None] // 64))
    put("ones16", (r[:, None] // 16 == r[None] // 16))
    put("ones128", np.ones((128, 128)))
    i, j = np.arange(64)[:, None], np.arange(64)[None]
    two = lambda a: np.concatenate([a, a], axis=0).astype(np.float32)
    one = np.ones((64, 64))
    put("amask", two(np.concatenate([i < j, i <= j, one, i < j, i <= j, one, i > j], axis=1)))
    put("eye64", two(i == j))
    off = lambda n: (i // (2 * n) == j // (2 * n)) & ((i // n) % 2 == 1) & ((j // n) % 2 == 0)
    put("low0", two(off(1)))
    put("low0t", two(off(1).T))
    put("lev", two(np.concatenate([off(2 ** k).T for k in range(1, LEVELS)], axis=1)))
    put("reset", np.broadcast_to((np.arange(COLS) % CH != 0), (128, COLS)))
    put("eps", np.broadcast_to(np.array([LN_EPS, GN_EPS, RMS_EPS, AD * RMS_EPS]), (128, 4)))
    e, j = np.arange(4)[:, None], np.arange(4)[None]
    put("earlier", np.broadcast_to((j < e).reshape(1, 16), (128, 16)))
    return tab


def ffn_arrays(give, g, rows):
    for n in ("wq", "wk", "wv", "wo", "gate_w", "e0_up", "e0_down", "e1_w1", "e1_w2", "e1_down",
              "e2_l1", "e2_l2", "e2_l3", "e2_l4", "e3_down", "e3_up", "e3_out"):
        give(n, rows(g("L0_ffn_" + n).T))


def kernel(**inputs):
    import numpy as np
    import concourse.bacc as _bacc
    from concourse.bass_utils import run_bass_kernel_spmd as _run

    nc = _bacc.Bacc("TRN2", target_bir_lowering=False, num_devices=1)
    arrays, io = {}, {}

    def give(name, a):
        a = np.ascontiguousarray(a)
        arrays["in_" + name] = a
        io[name] = nc.dram_tensor("in_" + name, a.shape, mybir.dt.from_np(a.dtype), kind="ExternalInput").ap()

    g = lambda n: np.asarray(inputs[n])
    rows = lambda a: a.reshape(-1, 128, a.shape[1]).transpose(1, 0, 2)
    give("x", g("L0_attn_x"))
    for n in ("W_r", "W_k", "W_v", "W_o", "w1", "a1", "g1"):
        give(n, rows(g("L0_attn_" + n)))
    for n in ("w2", "a2", "g2"):
        give(n, g("L0_attn_" + n))
    vecs = [g("L0_ffn_" + n) if n in ("n1_w", "n2_w") else np.tile(g("L0_ffn_" + n), AH) if n in ("qn_w", "kn_w")
            else g("L0_attn_" + n).reshape(-1) for n in VECS]
    give("vecs", np.stack(vecs).reshape(len(VECS), 2, 128).transpose(2, 0, 1))
    give("table", host_tables())
    ffn_arrays(give, g, rows)
    io["out"] = nc.dram_tensor("out_dram", (B, T, C), FP32, kind="ExternalOutput").ap()
    program(nc, io)
    r = _run(nc, [arrays], core_ids=[0])
    return r.results[0]["out_dram"]
```

```python
import concourse.bass as bass
from concourse import mybir
from contextlib import ExitStack
import math

FP32 = mybir.dt.float32
BF16 = mybir.dt.bfloat16
ALU = mybir.AluOpType
ACT = mybir.ActivationFunctionType
AX = mybir.AxisListType

B, T, C = 2, 2048, 256
HALVES = C // 128
RH, RD = 4, 64
CH = 64
TT = 128
NT = T // TT
COLS = B * TT
NCH = TT // CH
CB = COLS // CH
PAIRS = CB * HALVES
LEVELS = int(math.log2(CH))
LN_EPS, GN_EPS, RMS_EPS = 1e-5, 0.00064, 1.1920929e-07
NEG_DECAY = math.exp(-0.5)

AH, AD, HID = 16, 16, 512
EXPERTS = 4
ETT = 256
ENT, ECOLS = T // ETT, B * ETT

F32_TABLE = [("ident", 128), ("neg_kq", 128), ("neg_qk", 128), ("ones64", 128), ("ones16", 128), ("ones128", 128),
             ("amask", 7 * 64), ("eye64", 64), ("low0", 64), ("low0t", 64),
             ("lev", (LEVELS - 1) * 64), ("reset", COLS), ("eps", 4), ("earlier", EXPERTS * EXPERTS)]
VECS = ["x_r", "x_w", "x_k", "x_v", "x_a", "x_g", "w0", "a0", "k_k", "k_a", "r_k", "ln_w", "ln_b",
        "n1_w", "n2_w", "qn_w", "kn_w"]


def table_at():
    at, n = {}, 0
    for name, width in F32_TABLE:
        at[name] = (n, n + width)
        n += width
    return at, n


class Signal:

    def __init__(self, sem, per, unit=1):
        self.sem, self.per, self.unit, self.n = sem, per, unit, 0

    def open(self, eng):
        eng.sem_inc(self.sem, self.per * self.unit)

    def up(self):
        self.n += 1
        return self.unit

    def at(self, turn, n=None, back=0):
        return turn * (self.per * self.unit) + (self.per * (1 - back) + (self.n if n is None else n)) * self.unit

    def restart(self, eng=None):
        if eng is not None and self.n < self.per:
            eng.sem_inc(self.sem, (self.per - self.n) * self.unit)
        self.n = 0

    def whole(self):
        assert self.n == self.per, (self.n, self.per)


FIRST = -1


def all_strands(eng, front, back, tail):
    for _ in front(FIRST):
        pass

    def turn(t, before, after):
        strands = [tail(t - 1) if before else iter(()), front(t) if after else iter(())]

        def give_way():
            for strand in strands:
                next(strand, None)

        back(t, give_way)
        for strand in strands:
            for _ in strand:
                raise AssertionError("the strands differ in length")

    turn(0, False, True)
    with eng.Fori(1, NT - 1) as t:
        turn(t, True, True)
    turn(NT - 1, True, False)
    for _ in tail(NT - 1):
        pass


def recurrent_phase(nc, io, keep, signal):
    ctx = ExitStack()
    with ctx:
        def sb(name, shape, dt=FP32):
            return ctx.enter_context(nc.sbuf_tensor("r_" + name, shape, dt))

        def sig(name, per, unit=1):
            return signal("r_" + name, per, unit)

        cst, at, vec, xn_all, v_all = (keep[n] for n in ("cst", "at", "vec", "xn_all", "v_all"))
        s_const = keep["s_const"]

        def const(name, lo=0, hi=None):
            a, b = at[name]
            return cst[:, a + lo:(a + hi if hi is not None else b)]

        def v(name, h):
            return vec[:, VECS.index(name), h:h + 1]

        ident, ones64 = const("ident"), const("ones64")
        FM = [128, HALVES, COLS]
        w_in = {n: sb(n, [128, HALVES, w]) for n, w in
                [("W_r", C), ("W_k", C), ("W_v", C), ("W_o", C), ("w1", 64), ("a1", 64), ("g1", 128),
                 ("wq", C), ("wk", C), ("wv", C)]}
        w_up = {n: sb(n, [k, C]) for n, k in [("w2", 64), ("a2", 64), ("g2", 128)]}
        NWT = len(w_in) + len(w_up)
        x_tok, xn_tok = sb("x_tok", [128, B, C]), sb("xn_tok", [128, B, C])
        bn6, mv = sb("bn6", [128, B, 6]), sb("mv", [128, B, 2])
        std, rstd = sb("std", [128, B]), sb("rstd", [128, B])
        dx = sb("dx", FM)
        mixed = {n: sb("x" + n, FM) for n in "gwakrv"}
        tg, tw, ta = sb("tg", [128, COLS]), sb("tw", [64, COLS]), sb("ta", [64, COLS])
        kraw, rT, vT, gT, sg, av, kk, sq, nrm, kmod, bonus = (
            sb(n, FM) for n in ("kraw", "rT", "vT", "gT", "sg", "av", "kk", "sq", "nrm", "kmod", "bonus"))
        cs, csp = dx, mixed["g"]
        p_now, p_inv, p_prev, rk = mixed["w"], mixed["a"], mixed["k"], mixed["r"]
        rdec = sb("rdec", FM)
        xsq, rms = sb("xsq", FM), sb("rms", [128, COLS])
        hT = xsq
        raw = {n: sb(n + "_raw", FM) for n in "qk"}
        hsq = {n: sb(n + "_sq", FM) for n in "qk"}
        part = {n: sb(n + "_part", [128, 3, HALVES, COLS], BF16) for n in "qk"}
        v_st = sb("v_st", [128, CB, HALVES, 64])
        ari = sb("ari", [128, HALVES, CB, 3, 64])
        bT, kT = sb("bT", [128, HALVES, CB, 64]), sb("kT", [128, HALVES, CB, 64])
        p_end = sb("p_end", [128, NCH, B, HALVES])
        am = sb("am", [128, PAIRS, 7, 64])
        inv, invT, zz = (sb(n, [128, PAIRS, 64]) for n in ("inv", "invT", "zz"))
        lj = [sb(f"lj{i}", [128, PAIRS, 64]) for i in range(2)]
        state, stmp, g_sb, u_sb = (sb(n, [128, B, HALVES, 64]) for n in ("state", "stmp", "g_sb", "u_sb"))
        yT, yc, ystd, yg, gain, shift = (sb(n, FM) for n in ("yT", "yc", "ystd", "yg", "gain", "shift"))
        ysq = yg
        s_tok = sb("s_tok", [128, B, C])

        ps = ctx.enter_context(nc.psum_tensor("r_ps", [128, 8, 512], FP32))
        F = 4
        JOBS = [("tr", "A"), ("g1", "A"), ("w1", "A"), ("a1", "V"), ("k", "V"), ("ms", "A"), ("w2", "A"),
                ("a2", "A"), ("r", "A"), ("v", "A"), ("n", "A"), ("aq", "A"), ("ak", "A"), ("av", "A"),
                ("qs", "A"), ("ks", "A"), ("vst", "V"), ("g2", "V"), ("b", "V")]
        NJ = len(JOBS)
        job_no = {n: i for i, (n, _) in enumerate(JOBS)}
        taken = {}
        for who in "AV":
            for i, n in enumerate([n for n, w in JOBS if w == who]):
                taken[n] = (who, i + 1)

        def bank(name, m=128, wide=2 * COLS):
            return ps[0:m, job_no[name] % F, 0:wide]

        def halves(ap):
            return ap.rearrange("p (h c) -> p h c", h=HALVES)

        def by_batch(ap):
            return ap.rearrange("p (b t) -> p b t", b=B)

        s_w = sig("weights", 1, 16 * NWT)
        s_x, s_parts = sig("x_in", 1, 32), sig("parts_stored", 1, 16 * 24)
        s_var, s_std, s_xn, s_mix = sig("var", 1), sig("std", 1), sig("xn", 1), sig("mixed", 6)
        s_job = sig("job", NJ)
        took = {"A": sig("act_took", sum(w == "A" for _, w in JOBS)),
                "V": sig("dve_took", sum(w == "V" for _, w in JOBS))}
        s_kk, s_sq, s_cs, s_exp, s_rk, s_feat = (sig(n, 1) for n in (
            "kk", "kk_squared", "log_decay", "decays", "r_times_k", "features"))
        s_adec, s_vst = sig("a_r_decayed", 1), sig("v_stacked", 1)
        s_xsq, s_h, s_hsq, s_cut = sig("xn_squared", 1), sig("h", 1), sig("qk_squared", 2), sig("parts", 2)
        s_am, s_amsb = sig("products", PAIRS), sig("products_kept", PAIRS)
        s_lj, s_z, s_zsb, s_inv, s_invsb = (sig(n, LEVELS - 1) for n in (
            "level_off", "z", "z_kept", "inverse_step", "inverse_kept"))
        s_g, s_gsb, s_u, s_usb, s_sn, s_state, s_y, s_ysb = (sig(n, NCH) for n in (
            "chunk_g", "chunk_g_kept", "chunk_u", "chunk_u_kept", "state_gain", "state", "chunk_y", "chunk_y_kept"))
        s_mean, s_yc, s_ycsq, s_gvar, s_gstd, s_yg, s_out, s_outsb = (sig(n, 1) for n in (
            "y_mean", "y_centred", "y_squared", "y_var", "y_std", "y_gated", "s_out", "s_out_kept"))
        s_store = sig("s_stored", 1, 32)
        front_step, back_step, tail_step = sig("dve_front_step", 21), sig("dve_back_step", 5), sig("dve_tail_step", 3)
        s_base = sig("transposed_base", 1)
        s_init, s_passed = sig("init", 1), sig("passed", 1).sem
        SLOTS = 3 + 2 * (LEVELS - 1) + 3 * NCH

        block = ctx.enter_context(nc.Block())

        @block.sync
        def _(sp):
            for n, tile in list(w_in.items()):
                sp.dma_start(tile[:, :, :], io[n]).then_inc(s_w.sem, 16)
            for n, tile in list(w_up.items()):
                sp.dma_start(tile[:, :], io[n]).then_inc(s_w.sem, 16)
            s_store.open(sp)

            def load_x(t):
                for b in range(B):
                    sp.dma_start(x_tok[:, b, :], io["x"][b, bass.ds((t + 1) * TT, TT), :]).then_inc(s_x.sem, 16)

            def store_parts(t):
                for i, n in enumerate("qk"):
                    sp.wait_ge(s_cut.sem, s_cut.at(t, i + 1))
                    sp.sem_inc(s_passed, 1)
                    for k in range(3):
                        for h in range(HALVES):
                            for b in range(B):
                                sp.dma_start(io[n + "_dram"][k, b, 128 * h:128 * h + 128, bass.ds((t + 1) * TT, TT)],
                                             part[n][:, k, h, TT * b:TT * b + TT]).then_inc(s_parts.sem, 16)

            def store_s(t):
                sp.wait_ge(s_outsb.sem, s_outsb.at(t, 1))
                sp.sem_inc(s_passed, 1)
                for b in range(B):
                    sp.dma_start(io["s_dram"][b, bass.ds(t * TT, TT), :], s_tok[:, b, :]).then_inc(s_store.sem, 16)

            def turn(t, before):
                sp.wait_ge(s_xn.sem, s_xn.at(t, 0))
                sp.sem_inc(s_passed, 1)
                load_x(t)
                if before:
                    store_s(t - 1)
                store_parts(t)

            load_x(-1)
            store_parts(-1)
            turn(0, False)
            with sp.Fori(1, NT - 1) as t:
                turn(t, True)
            store_s(NT - 2)
            store_s(NT - 1)
            sp.wait_ge(s_store.sem, s_store.at(NT - 1, 1))
            sp.wait_ge(s_parts.sem, s_parts.at(NT - 2, 1))

        @block.tensor
        def _(pe):
            back_signals, tail_signals = (s_am, s_z, s_inv, s_g, s_u, s_sn, s_y), (s_mean, s_gvar, s_out)
            for q in back_signals + tail_signals:
                q.open(pe)
            pe.wait_ge(s_const, keep["n_const"])
            pe.wait_ge(s_w.sem, 16 * NWT)
            mm = nc.tensor.matmul

            def front(t):
                def free(name):
                    n = job_no[name] - F
                    if n >= 0:
                        who, i = taken[JOBS[n][0]]
                        pe.wait_ge(took[who].sem, took[who].at(t, i))
                    elif t is not FIRST:
                        n = max(m for m in range(NJ) if m % F == job_no[name] % F)
                        who, i = taken[JOBS[n][0]]
                        pe.wait_ge(took[who].sem, took[who].at(t, i, back=1))

                def project(name, weights, src, m=128):
                    free(name)
                    outs = weights[0].shape[1] // m
                    for o in range(outs):
                        for i, (wt, x) in enumerate(zip(weights, src)):
                            last = mm(ps[0:m, job_no[name] % F, COLS * o:COLS * o + COLS], wt[:, m * o:m * o + m], x,
                                      start=(i == 0), stop=(i == len(src) - 1))
                    last.then_inc(s_job.sem, s_job.up())

                def per_half(name, ones, src):
                    free(name)
                    for h in range(2):
                        last = mm(ps[:, job_no[name] % F, COLS * h:COLS * h + COLS], ones, src[:, h, :], start=True, stop=True)
                    last.then_inc(s_job.sem, s_job.up())

                two = lambda a: [a[:, i, :] for i in range(2)]
                yield 0
                yield 1
                pe.wait_ge(s_xn.sem, s_xn.at(t, 1))
                free("tr")
                for h in range(HALVES):
                    for b in range(B):
                        last = nc.tensor.transpose(ps[:, job_no["tr"] % F, COLS * h + TT * b:COLS * h + TT * b + TT],
                                                   xn_tok[:, b, 128 * h:128 * h + 128], ident)
                last.then_inc(s_job.sem, s_job.up())
                yield 2
                pe.wait_ge(s_mix.sem, s_mix.at(t, 1))
                project("g1", two(w_in["g1"]), two(mixed["g"]))
                pe.wait_ge(s_mix.sem, s_mix.at(t, 2))
                project("w1", two(w_in["w1"]), two(mixed["w"]), 64)
                yield 3
                pe.wait_ge(s_mix.sem, s_mix.at(t, 3))
                project("a1", two(w_in["a1"]), two(mixed["a"]), 64)
                pe.wait_ge(s_mix.sem, s_mix.at(t, 4))
                project("k", two(w_in["W_k"]), two(mixed["k"]))
                yield 4
                pe.wait_ge(s_xsq.sem, s_xsq.at(t, 1))
                free("ms")
                for h in range(2):
                    last = mm(bank("ms", wide=COLS), const("ones128"), xsq[:, h, :], start=(h == 0), stop=(h == 1))
                last.then_inc(s_job.sem, s_job.up())
                pe.wait_ge(took["A"].sem, took["A"].at(t, taken["w1"][1]))
                project("w2", [w_up["w2"]], [tw[:, :]])
                yield 5
                pe.wait_ge(took["V"].sem, took["V"].at(t, taken["a1"][1]))
                project("a2", [w_up["a2"]], [ta[:, :]])
                pe.wait_ge(s_mix.sem, s_mix.at(t, 5))
                project("r", two(w_in["W_r"]), two(mixed["r"]))
                yield 6
                pe.wait_ge(s_mix.sem, s_mix.at(t, 6))
                project("v", two(w_in["W_v"]), two(mixed["v"]))
                pe.wait_ge(s_sq.sem, s_sq.at(t, 1))
                per_half("n", ones64, sq)
                yield 7
                pe.wait_ge(s_h.sem, s_h.at(t, 1))
                project("aq", two(w_in["wq"]), two(hT))
                yield 8
                project("ak", two(w_in["wk"]), two(hT))
                yield 9
                free("av")
                for b in range(B):
                    for k in range(2):
                        last = mm(ps[:, job_no["av"] % F, C * b:C * b + C], hT[:, k, TT * b:TT * b + TT],
                                  w_in["wv"][:, k, :], start=(k == 0), stop=(k == 1))
                last.then_inc(s_job.sem, s_job.up())
                yield 10
                pe.wait_ge(s_hsq.sem, s_hsq.at(t, 1))
                per_half("qs", const("ones16"), hsq["q"])
                yield 11
                pe.wait_ge(s_hsq.sem, s_hsq.at(t, 2))
                per_half("ks", const("ones16"), hsq["k"])
                for k in range(12, 16):
                    yield k
                free("vst")
                w_v = w_in["W_v"][:, :, :].rearrange("p k (g j d) -> p k g j d", j=2, d=64)
                for cb in range(CB):
                    for i in range(2):
                        for j in range(2):
                            last = mm(ps[64 * j:64 * j + 64, job_no["vst"] % F, 128 * cb:128 * cb + 128],
                                      mixed["v"][:, i, 64 * cb:64 * cb + 64], w_v[:, i, :, j, :],
                                      start=(i == 0), stop=(i == 1))
                last.then_inc(s_job.sem, s_job.up())
                yield 16
                yield 17
                project("g2", [w_up["g2"]], [tg[:, :]])
                pe.wait_ge(s_rk.sem, s_rk.at(t, 1))
                per_half("b", ones64, rk)
                yield 18
                s_job.whole()
                s_job.restart()

            def apart():
                pe.sem_inc(s_passed, 1)

            def back(t, give_way):
                give_way()
                pe.wait_ge(s_feat.sem, s_feat.at(t, 0))
                for p in range(PAIRS):
                    cb, g = divmod(p, 2)
                    if p >= 3:
                        pe.wait_ge(s_amsb.sem, s_amsb.at(t, p - 2))
                    elif p == 2:
                        pe.wait_ge(s_state.sem, s_state.at(t, NCH, back=1))
                    apart()
                    for lo, n, left, right in ((0, 192, bT[:, g, cb, :], ari[:, g, cb, :, :].rearrange("p a c -> p (a c)")),
                                               (192, 192, kT[:, g, cb, :], ari[:, g, cb, :, :].rearrange("p a c -> p (a c)")),
                                               (384, 64, ari[:, g, cb, 0, :], bT[:, g, cb, :])):
                        for j in range(2):
                            q = slice(64 * j, 64 * j + 64)
                            last = mm(ps[q, 4 + p % 3, lo:lo + n], left[q], right[q], start=True, stop=True)
                    last.then_inc(s_am.sem, s_am.up())
                    if p == 3:
                        give_way()
                give_way()

                def pairwise(bk, left, right):
                    apart()
                    for p in range(PAIRS):
                        for j in range(2):
                            q = slice(64 * j, 64 * j + 64)
                            last = mm(ps[q, bk, 64 * p:64 * p + 64], left[q, p, :], right[q, p, :], start=True, stop=True)
                    return last

                for lev in range(LEVELS - 1):
                    if lev:
                        pe.wait_ge(s_invsb.sem, s_invsb.at(t, lev))
                    pe.wait_ge(s_lj.sem, s_lj.at(t, lev + 1))
                    pairwise(4, lj[lev % 2], inv).then_inc(s_z.sem, s_z.up())
                    give_way()
                    pe.wait_ge(s_zsb.sem, s_zsb.at(t, lev + 1))
                    if lev == 0:
                        pe.wait_ge(s_base.sem, s_base.at(t, 1))
                    if lev < LEVELS - 2:
                        pairwise(5, invT, zz)
                    pairwise(6, zz, invT).then_inc(s_inv.sem, s_inv.up())
                    give_way()

                pe.wait_ge(s_vst.sem, s_vst.at(t, 0))
                pe.wait_ge(s_invsb.sem, s_invsb.at(t, LEVELS - 1))
                for c in range(NCH):
                    units = [(b, g, (b * NCH + c) * 2 + g, b * NCH + c) for b in range(B) for g in range(2)]

                    def into(bk, left, right, first):
                        last = None
                        apart()
                        for n, (b, g, p, cb) in enumerate(units):
                            for j in range(2):
                                q = slice(64 * j, 64 * j + 64)
                                o = 64 * (2 * b + g)
                                last = mm(ps[q, bk, o:o + 64], left(q, b, g, p, cb), right(q, b, g, p, cb),
                                          start=(first and n == 0), stop=True, skip_group_check=True)
                        return last

                    a_t = lambda q, b, g, p, cb: ari[q, g, cb, 0, :]
                    r_t = lambda q, b, g, p, cb: ari[q, g, cb, 1, :]
                    st = lambda q, b, g, p, cb: state[q, b, g, :]
                    vv = lambda q, b, g, p, cb: v_st[q, cb, g, :]
                    gg = lambda q, b, g, p, cb: g_sb[q, b, g, :]
                    uu = lambda q, b, g, p, cb: u_sb[q, b, g, :]
                    prod = lambda k: (lambda q, b, g, p, cb: am[q, p, k, :])
                    into(4, prod(3), vv, True)
                    pe.wait_ge(s_state.sem, s_state.at(t, c) if c else s_state.at(t, NCH, back=1))
                    into(4, a_t, st, False).then_inc(s_g.sem, s_g.up())
                    if c:
                        pe.wait_ge(s_ysb.sem, s_ysb.at(t, c))
                    else:
                        pe.wait_ge(s_outsb.sem, s_outsb.at(t, 0))
                    into(7, st, r_t, True)
                    into(7, vv, prod(4), False)
                    into(6, prod(5), vv, True)
                    give_way()
                    pe.wait_ge(s_gsb.sem, s_gsb.at(t, c + 1))
                    into(5, lambda q, b, g, p, cb: invT[q, p, :], gg, True).then_inc(s_u.sem, s_u.up())
                    give_way()
                    pe.wait_ge(s_usb.sem, s_usb.at(t, c + 1))
                    into(6, prod(2), uu, False).then_inc(s_sn.sem, s_sn.up())
                    into(7, uu, prod(1), False).then_inc(s_y.sem, s_y.up())
                    give_way()

                for q in back_signals:
                    q.restart()

            def tail(t):
                pe.wait_ge(s_ysb.sem, s_ysb.at(t, NCH))
                for h in range(2):
                    last = mm(ps[:, 7, COLS * h:COLS * h + COLS], ones64, yT[:, h, :], start=True, stop=True)
                last.then_inc(s_mean.sem, s_mean.up())
                yield 0
                pe.wait_ge(s_ycsq.sem, s_ycsq.at(t, 1))
                for h in range(2):
                    last = mm(ps[:, 7, COLS * h:COLS * h + COLS], ones64, ysq[:, h, :], start=True, stop=True)
                last.then_inc(s_gvar.sem, s_gvar.up())
                yield 1
                yield 2
                pe.wait_ge(s_yg.sem, s_yg.at(t, 1))
                for b in range(B):
                    for h in range(2):
                        last = mm(ps[:, 7, C * b:C * b + C], yg[:, h, TT * b:TT * b + TT], w_in["W_o"][:, h, :],
                                  start=(h == 0), stop=(h == 1))
                last.then_inc(s_out.sem, s_out.up())
                yield 3
                for q in tail_signals:
                    q.restart()

            all_strands(pe, front, back, tail)

        @block.scalar
        def _(act):
            back_signals, tail_signals = (s_zsb, s_ysb), (s_ycsq, s_gstd, s_outsb)
            for q in back_signals + tail_signals:
                q.open(act)
            act.wait_ge(s_const, keep["n_const"])
            f = nc.scalar.activation
            eps_ln, eps_gn, eps_rms, eps_rms16 = (const("eps", i, i + 1) for i in range(4))

            def front(t):
                def ready(name):
                    act.wait_ge(s_job.sem, s_job.at(t, job_no[name] + 1))

                act.wait_ge(s_var.sem, s_var.at(t, 1))
                f(std[:, :], mv[:, :, 1], ACT.Sqrt, bias=eps_ln, scale=1.0).then_inc(s_std.sem, 1)
                yield 0
                yield 1
                ready("tr")
                nc.scalar.copy(xn_all[:, :, :, bass.ds((t + 1) * TT + 1, TT)],
                               bank("tr").rearrange("p (h b t) -> p h b t", h=HALVES, b=B)
                               ).then_inc(took["A"].sem, took["A"].up())
                act.wait_ge(took["A"].sem, took["A"].at(t, 1))
                if t is not FIRST:
                    act.wait_ge(took["A"].sem, took["A"].at(t, taken["ms"][1], back=1))
                act.sem_inc(s_passed, 1)
                f(xsq[:, :, :].rearrange("p h (b t) -> p h b t", b=B), xn_all[:, :, :, bass.ds((t + 1) * TT + 1, TT)],
                  ACT.Square).then_inc(s_xsq.sem, 1)
                yield 2
                ready("g1")
                f(tg[:, :], bank("g1", wide=COLS), ACT.Sigmoid).then_inc(took["A"].sem, took["A"].up())
                ready("w1")
                f(tw[:, :], bank("w1", 64, COLS), ACT.Tanh).then_inc(took["A"].sem, took["A"].up())
                yield 3
                yield 4
                ready("ms")
                f(rms[:, :], bank("ms", wide=COLS), ACT.Sqrt, bias=eps_rms, scale=1.0 / C
                  ).then_inc(took["A"].sem, took["A"].up())
                ready("w2")
                f(sg[:, 0, :], halves(bank("w2"))[:, 0, :], ACT.Sigmoid, bias=v("w0", 0), scale=1.0)
                f(sg[:, 1, :], halves(bank("w2"))[:, 1, :], ACT.Sigmoid, bias=v("w0", 1), scale=1.0
                  ).then_inc(took["A"].sem, took["A"].up())
                yield 5
                ready("a2")
                f(av[:, 0, :], halves(bank("a2"))[:, 0, :], ACT.Sigmoid, bias=v("a0", 0), scale=1.0)
                f(av[:, 1, :], halves(bank("a2"))[:, 1, :], ACT.Sigmoid, bias=v("a0", 1), scale=1.0
                  ).then_inc(took["A"].sem, took["A"].up())
                act.wait_ge(s_kk.sem, s_kk.at(t, 1))
                f(sq[:, :, :], kk[:, :, :], ACT.Square).then_inc(s_sq.sem, 1)
                ready("r")
                f(rT[:, :, :], halves(bank("r")), ACT.Copy).then_inc(took["A"].sem, took["A"].up())
                yield 6
                ready("v")
                f(vT[:, :, :], halves(bank("v")), ACT.Copy).then_inc(took["A"].sem, took["A"].up())
                ready("n")
                f(nrm[:, :, :], halves(bank("n")), ACT.Sqrt).then_inc(took["A"].sem, took["A"].up())
                yield 7
                act.wait_ge(s_cs.sem, s_cs.at(t, 1))
                f(p_now[:, :, :], cs[:, :, :], ACT.Exp, scale=-NEG_DECAY)
                f(p_inv[:, :, :], cs[:, :, :], ACT.Exp, scale=NEG_DECAY)
                f(p_prev[:, :, :], csp[:, :, :], ACT.Exp, scale=-NEG_DECAY).then_inc(s_exp.sem, 1)
                yield 8
                for i, n in enumerate("qk"):
                    ready("a" + n)
                    f(hsq[n][:, :, :], halves(bank("a" + n)), ACT.Square).then_inc(s_hsq.sem, 1)
                    f(raw[n][:, :, :], halves(bank("a" + n)), ACT.Copy).then_inc(took["A"].sem, took["A"].up())
                    if n == "q":
                        yield 9
                ready("av")
                nc.scalar.copy(v_all[:, :, bass.ds(t + 1, 1), :].rearrange("p b o c -> p (b o) c"),
                               bank("av").rearrange("p (b c) -> p b c", b=B)).then_inc(took["A"].sem, took["A"].up())
                yield 10
                ready("qs")
                f(hsq["q"][:, :, :], halves(bank("qs")), ACT.Sqrt, bias=eps_rms16, scale=1.0
                  ).then_inc(took["A"].sem, took["A"].up())
                yield 11
                ready("ks")
                f(hsq["k"][:, :, :], halves(bank("ks")), ACT.Sqrt, bias=eps_rms, scale=1.0 / AD
                  ).then_inc(took["A"].sem, took["A"].up())
                for k in range(12, 18):
                    yield k
                if t is not FIRST:
                    act.wait_ge(s_y.sem, s_y.at(t, NCH))
                act.wait_ge(s_adec.sem, s_adec.at(t, 1))
                for h in range(2):
                    f(ari[:, h, :, 0, :], kk[:, h, :].rearrange("p (c t) -> p c t", c=CB), ACT.Copy)
                    last = f(ari[:, h, :, 1, :], rdec[:, h, :].rearrange("p (c t) -> p c t", c=CB), ACT.Copy)
                last.then_inc(s_feat.sem, 1)
                yield 18
                took["A"].whole()
                took["A"].restart()

            def back(t, give_way):
                give_way()
                give_way()
                give_way()
                for lev in range(LEVELS - 1):
                    act.wait_ge(s_z.sem, s_z.at(t, lev + 1))
                    f(zz[:, :, :].rearrange("p a c -> p (a c)"), ps[:, 4, :], ACT.Copy).then_inc(s_zsb.sem, s_zsb.up())
                    give_way()
                    give_way()
                for c in range(NCH):
                    give_way()
                    give_way()
                    act.wait_ge(s_y.sem, s_y.at(t, c + 1))
                    nc.scalar.copy(yT[:, :, :].rearrange("p h (b t) -> p h b t", b=B)[:, :, :, 64 * c:64 * c + 64],
                                   ps[:, 7, 0:256].rearrange("p (b g v) -> p g b v", b=2, g=2)
                                   ).then_inc(s_ysb.sem, s_ysb.up())
                    give_way()
                for q in back_signals:
                    q.restart()

            def tail(t):
                act.wait_ge(s_yc.sem, s_yc.at(t, 1))
                f(ysq[:, :, :], yc[:, :, :], ACT.Square).then_inc(s_ycsq.sem, s_ycsq.up())
                yield 0
                act.wait_ge(s_gvar.sem, s_gvar.at(t, 1))
                f(ystd[:, :, :], halves(ps[:, 7, :]), ACT.Sqrt, bias=eps_gn, scale=1.0 / RD).then_inc(s_gstd.sem, s_gstd.up())
                yield 1
                yield 2
                act.wait_ge(s_out.sem, s_out.at(t, 1))
                act.wait_ge(s_store.sem, s_store.at(t, 1, back=1))
                f(s_tok[:, :, :], ps[:, 7, :].rearrange("p (b c) -> p b c", b=B), ACT.Copy).then_inc(s_outsb.sem, s_outsb.up())
                yield 3
                for q in tail_signals:
                    q.restart()

            all_strands(act, front, back, tail)

        @block.vector
        def _(dve):
            back_signals = (s_amsb, s_base, s_lj, s_invsb, s_gsb, s_usb, s_state, back_step)
            tail_signals = (s_yc, s_yg, tail_step)
            for q in back_signals + tail_signals:
                q.open(dve)
            dve.wait_ge(s_const, keep["n_const"])
            ve = nc.vector
            ve.memset(state[:, :, :, :], 0.0)
            ve.memset(xn_all[:, :, :, 0:1], 0.0)
            for g in range(2):
                last = ve.tensor_copy(ari[:, g, :, 2, :], const("eye64").unsqueeze(1).to_broadcast([128, CB, 64]))
            last.then_inc(s_init.sem, 1)
            dve.wait_ge(s_init.sem, 1)

            def cut(ap):
                return ap.rearrange("p (c t) -> p c t", c=CB)

            def front(t):
                def ready(name):
                    dve.wait_ge(s_job.sem, s_job.at(t, job_no[name] + 1))

                def mix(n):
                    for h in range(2):
                        last = ve.scalar_tensor_tensor(by_batch(mixed[n][:, h, :]), by_batch(dx[:, h, :]), v("x_" + n, h),
                                                       xn_all[:, h, :, bass.ds((t + 1) * TT + 1, TT)], ALU.mult, ALU.add)
                    last.then_inc(s_mix.sem, s_mix.up())

                dve.wait_ge(s_x.sem, s_x.at(t, 1))
                for b in range(B):
                    last = ve.bn_stats(bn6[:, b, :], x_tok[:, b, :])
                last.then_inc(front_step.sem, front_step.up())
                dve.wait_ge(front_step.sem, front_step.at(t))
                dve.sem_inc(s_passed, 1)
                for b in range(B):
                    last = ve.bn_aggr(mv[:, b, :], bn6[:, b, :])
                last.then_inc(s_var.sem, 1)
                yield 0
                dve.wait_ge(s_std.sem, s_std.at(t, 1))
                ve.reciprocal(rstd[:, :], std[:, :]).then_inc(front_step.sem, front_step.up())
                dve.wait_ge(front_step.sem, front_step.at(t))
                for b in range(B):
                    last = ve.tensor_scalar(xn_tok[:, b, :], x_tok[:, b, :], mv[:, b, 0:1], rstd[:, b:b + 1],
                                            ALU.subtract, ALU.mult)
                last.then_inc(s_xn.sem, 1)
                yield 1
                dve.wait_ge(took["A"].sem, took["A"].at(t, 1))
                ve.tensor_tensor(dx[:, :, :].rearrange("p h (b t) -> p h b t", b=B),
                                 xn_all[:, :, :, bass.ds((t + 1) * TT, TT)],
                                 xn_all[:, :, :, bass.ds((t + 1) * TT + 1, TT)], ALU.subtract
                                 ).then_inc(front_step.sem, front_step.up())
                dve.wait_ge(front_step.sem, front_step.at(t))
                mix("g")
                mix("w")
                yield 2
                mix("a")
                mix("k")
                yield 3
                mix("r")
                mix("v")
                ready("a1")
                ve.tensor_copy(ta[:, :], bank("a1", 64, COLS)).then_inc(took["V"].sem, took["V"].up())
                ready("k")
                ve.tensor_copy(kraw[:, :, :], halves(bank("k"))).then_inc(took["V"].sem, took["V"].up())
                dve.wait_ge(took["V"].sem, took["V"].at(t))
                yield 4
                for h in range(2):
                    last = ve.tensor_scalar(kk[:, h, :], kraw[:, h, :], v("k_k", h), None, ALU.mult)
                last.then_inc(s_kk.sem, 1)
                dve.wait_ge(took["A"].sem, took["A"].at(t, taken["ms"][1]))
                ve.reciprocal(rms[:, :], rms[:, :]).then_inc(front_step.sem, front_step.up())
                dve.wait_ge(front_step.sem, front_step.at(t))
                for h in range(2):
                    last = ve.scalar_tensor_tensor(by_batch(hT[:, h, :]), xn_all[:, h, :, bass.ds((t + 1) * TT + 1, TT)],
                                                   v("n1_w", h), by_batch(rms[:, :]), ALU.mult, ALU.mult)
                last.then_inc(s_h.sem, 1)
                yield 5
                dve.wait_ge(took["A"].sem, took["A"].at(t, taken["w2"][1]))
                for h in range(2):
                    last = ve.tensor_tensor_scan(cs[:, h, :], const("reset"), sg[:, h, :], 0.0, ALU.mult, ALU.add)
                last.then_inc(front_step.sem, front_step.up())
                dve.wait_ge(front_step.sem, front_step.at(t))
                ve.tensor_tensor(csp[:, :, :], cs[:, :, :], sg[:, :, :], ALU.subtract).then_inc(s_cs.sem, 1)
                yield 6
                dve.wait_ge(took["A"].sem, took["A"].at(t, taken["a2"][1]))
                for h in range(2):
                    last = ve.tensor_scalar(kmod[:, h, :], av[:, h, :], 1.0, v("k_a", h), ALU.subtract, ALU.mult)
                last.then_inc(front_step.sem, front_step.up())
                dve.wait_ge(front_step.sem, front_step.at(t))
                ve.scalar_tensor_tensor(kmod[:, :, :], kmod[:, :, :], 1.0, kraw[:, :, :], ALU.add, ALU.mult
                                        ).then_inc(front_step.sem, front_step.up())
                dve.wait_ge(front_step.sem, front_step.at(t))
                yield 7
                dve.wait_ge(took["A"].sem, took["A"].at(t, taken["r"][1]))
                for h in range(2):
                    last = ve.scalar_tensor_tensor(rk[:, h, :], rT[:, h, :], v("r_k", h), kmod[:, h, :], ALU.mult, ALU.mult)
                last.then_inc(s_rk.sem, 1)
                dve.wait_ge(took["A"].sem, took["A"].at(t, taken["n"][1]))
                ve.tensor_scalar(nrm[:, :, :], nrm[:, :, :], 1e-12, None, ALU.max).then_inc(front_step.sem, front_step.up())
                dve.wait_ge(front_step.sem, front_step.at(t))
                ve.reciprocal(nrm[:, :, :], nrm[:, :, :]).then_inc(front_step.sem, front_step.up())
                dve.wait_ge(front_step.sem, front_step.at(t))
                yield 8
                ve.tensor_tensor(kk[:, :, :], kk[:, :, :], nrm[:, :, :], ALU.mult).then_inc(front_step.sem, front_step.up())
                dve.wait_ge(front_step.sem, front_step.at(t))
                ve.tensor_tensor(av[:, :, :], kk[:, :, :], av[:, :, :], ALU.mult).then_inc(front_step.sem, front_step.up())
                dve.wait_ge(front_step.sem, front_step.at(t))
                yield 9
                dve.wait_ge(s_exp.sem, s_exp.at(t, 1))
                for h in range(2):
                    ve.tensor_tensor(bT[:, h, :, :], cut(av[:, h, :]), cut(p_inv[:, h, :]), ALU.mult)
                    ve.tensor_tensor(kT[:, h, :, :], cut(kmod[:, h, :]), cut(p_inv[:, h, :]), ALU.mult)
                yield 10
                for h in range(2):
                    ve.scalar_tensor_tensor(kk[:, h, :], kk[:, h, :], -1.0, p_prev[:, h, :], ALU.mult, ALU.mult)
                    last = ve.tensor_tensor(rdec[:, h, :], rT[:, h, :], p_now[:, h, :], ALU.mult)
                last.then_inc(s_adec.sem, 1)
                yield 11
                for i, n in enumerate("qk"):
                    hi, mid, lo = (part[n][:, k, :, :] for k in range(3))
                    dve.wait_ge(took["A"].sem, took["A"].at(t, taken[n + "s"][1]))
                    ve.reciprocal(hsq[n][:, :, :], hsq[n][:, :, :]).then_inc(front_step.sem, front_step.up())
                    dve.wait_ge(front_step.sem, front_step.at(t))
                    for h in range(2):
                        last = ve.scalar_tensor_tensor(raw[n][:, h, :], raw[n][:, h, :], v(n + "n_w", h), hsq[n][:, h, :],
                                                       ALU.mult, ALU.mult)
                    last.then_inc(front_step.sem, front_step.up())
                    dve.wait_ge(front_step.sem, front_step.at(t))
                    yield 12 + 3 * i
                    if t is not FIRST:
                        dve.wait_ge(s_parts.sem, s_parts.at(t, 1, back=1))
                    ve.tensor_copy(hi, raw[n][:, :, :]).then_inc(front_step.sem, front_step.up())
                    dve.wait_ge(front_step.sem, front_step.at(t))
                    ve.tensor_tensor(raw[n][:, :, :], raw[n][:, :, :], hi, ALU.subtract
                                     ).then_inc(front_step.sem, front_step.up())
                    dve.wait_ge(front_step.sem, front_step.at(t))
                    yield 13 + 3 * i
                    ve.tensor_copy(mid, raw[n][:, :, :]).then_inc(front_step.sem, front_step.up())
                    dve.wait_ge(front_step.sem, front_step.at(t))
                    ve.tensor_tensor(lo, raw[n][:, :, :], mid, ALU.subtract).then_inc(s_cut.sem, 1)
                    yield 14 + 3 * i
                if t is not FIRST:
                    dve.wait_ge(s_y.sem, s_y.at(t, NCH))
                ends = p_now[:, :, :].rearrange("p h (b c t) -> p c b h t", b=B, c=NCH)
                for c in range(NCH):
                    ve.tensor_copy(p_end[:, c, :, :], ends[:, c, :, :, CH - 1])
                ready("vst")
                ve.tensor_copy(v_st[:, :, :, :].rearrange("p a g d -> p (a g d)"), bank("vst")
                               ).then_inc(took["V"].sem, took["V"].up())
                dve.sem_inc(s_vst.sem, 1)
                ready("g2")
                ve.tensor_copy(gT[:, :, :], halves(bank("g2"))).then_inc(took["V"].sem, took["V"].up())
                ready("b")
                ve.tensor_tensor(bonus[:, :, :], halves(bank("b")), vT[:, :, :], ALU.mult
                                 ).then_inc(took["V"].sem, took["V"].up())
                dve.wait_ge(took["V"].sem, took["V"].at(t))
                yield 18
                front_step.whole()
                for q in (s_mix, took["V"], front_step):
                    q.restart()

            def back(t, give_way):
                flat = lambda a: a[:, :, :].rearrange("p a c -> p (a c)")
                wide = lambda name, lo=0, hi=64: const(name, lo, hi).unsqueeze(1).to_broadcast([128, PAIRS, 64])
                give_way()
                for p in range(PAIRS):
                    dve.wait_ge(s_am.sem, s_am.at(t, p + 1))
                    ve.tensor_tensor(am[:, p, :, :].rearrange("p a c -> p (a c)"), ps[:, 4 + p % 3, 0:448],
                                     const("amask"), ALU.mult).then_inc(s_amsb.sem, s_amsb.up())
                    if p == 3:
                        give_way()
                dve.wait_ge(s_amsb.sem, s_amsb.at(t))
                ve.tensor_tensor(inv[:, :, :], am[:, :, 6, :], wide("low0"), ALU.mult).then_inc(back_step.sem, back_step.up())
                ve.tensor_tensor(lj[0][:, :, :], am[:, :, 0, :], wide("lev", 0, 64), ALU.mult)
                dve.wait_ge(back_step.sem, back_step.at(t))
                ve.tensor_tensor(inv[:, :, :], inv[:, :, :], wide("eye64"), ALU.add).then_inc(s_lj.sem, s_lj.up())
                ve.tensor_tensor(invT[:, :, :], am[:, :, 0, :], wide("low0t"), ALU.mult
                                 ).then_inc(back_step.sem, back_step.up())
                dve.wait_ge(back_step.sem, back_step.at(t))
                ve.tensor_tensor(invT[:, :, :], invT[:, :, :], wide("eye64"), ALU.add).then_inc(s_base.sem, s_base.up())
                dve.wait_ge(s_base.sem, s_base.at(t))
                give_way()
                for lev in range(LEVELS - 1):
                    if lev < LEVELS - 2:
                        ve.tensor_tensor(lj[(lev + 1) % 2][:, :, :], am[:, :, 0, :], wide("lev", 64 * lev + 64, 64 * lev + 128),
                                         ALU.mult).then_inc(s_lj.sem, s_lj.up())
                    give_way()
                    dve.wait_ge(s_inv.sem, s_inv.at(t, lev + 1))
                    if lev < LEVELS - 2:
                        ve.tensor_tensor(flat(inv), flat(inv), ps[:, 5, :], ALU.add)
                    ve.tensor_tensor(flat(invT), flat(invT), ps[:, 6, :], ALU.add).then_inc(s_invsb.sem, s_invsb.up())
                    dve.wait_ge(s_invsb.sem, s_invsb.at(t))
                    if lev == 1:
                        for h in range(2):
                            ve.tensor_scalar(gain[:, h, :], gT[:, h, :], v("ln_w", h), None, ALU.mult)
                            last = ve.scalar_tensor_tensor(shift[:, h, :], bonus[:, h, :], v("ln_b", h), gT[:, h, :],
                                                           ALU.add, ALU.mult)
                        last.then_inc(back_step.sem, back_step.up())
                        dve.wait_ge(back_step.sem, back_step.at(t))
                    give_way()
                for c in range(NCH):
                    fl = lambda a: a[:, :, :, :].rearrange("p b g v -> p (b g v)")
                    dve.wait_ge(s_g.sem, s_g.at(t, c + 1))
                    ve.tensor_copy(fl(g_sb), ps[:, 4, 0:256]).then_inc(s_gsb.sem, s_gsb.up())
                    give_way()
                    dve.wait_ge(s_u.sem, s_u.at(t, c + 1))
                    ve.tensor_copy(fl(u_sb), ps[:, 5, 0:256]).then_inc(s_usb.sem, s_usb.up())
                    give_way()
                    dve.wait_ge(s_sn.sem, s_sn.at(t, c + 1))
                    ve.tensor_tensor(fl(stmp), fl(state), ps[:, 6, 0:256], ALU.add).then_inc(back_step.sem, back_step.up())
                    dve.wait_ge(back_step.sem, back_step.at(t))
                    ve.tensor_tensor(state[:, :, :, :], stmp[:, :, :, :],
                                     p_end[:, c, :, :].unsqueeze(3).to_broadcast([128, B, 2, 64]), ALU.mult
                                     ).then_inc(s_state.sem, s_state.up())
                    dve.wait_ge(s_state.sem, s_state.at(t))
                    give_way()
                back_step.whole()
                for q in back_signals:
                    q.restart()

            def tail(t):
                dve.wait_ge(s_mean.sem, s_mean.at(t, 1))
                ve.scalar_tensor_tensor(yc[:, :, :].rearrange("p h c -> p (h c)"), ps[:, 7, :], -1.0 / RD, yT[:, :, :].rearrange("p h c -> p (h c)"), ALU.mult, ALU.add
                                        ).then_inc(s_yc.sem, s_yc.up())
                dve.wait_ge(s_yc.sem, s_yc.at(t))
                yield
                dve.wait_ge(s_gstd.sem, s_gstd.at(t, 1))
                ve.reciprocal(ystd[:, :, :], ystd[:, :, :]).then_inc(tail_step.sem, tail_step.up())
                dve.wait_ge(tail_step.sem, tail_step.at(t))
                yield
                ve.tensor_tensor(yg[:, :, :], yc[:, :, :], ystd[:, :, :], ALU.mult).then_inc(tail_step.sem, tail_step.up())
                dve.wait_ge(tail_step.sem, tail_step.at(t))
                ve.tensor_tensor(yg[:, :, :], yg[:, :, :], gain[:, :, :], ALU.mult).then_inc(tail_step.sem, tail_step.up())
                dve.wait_ge(tail_step.sem, tail_step.at(t))
                ve.tensor_tensor(yg[:, :, :], yg[:, :, :], shift[:, :, :], ALU.add).then_inc(s_yg.sem, s_yg.up())
                dve.wait_ge(s_yg.sem, s_yg.at(t))
                yield
                yield
                tail_step.whole()
                for q in tail_signals:
                    q.restart()

            all_strands(dve, front, back, tail)


PARTS_Q, PARTS_K = (0, 0, 0, 1, 1, 2), (0, 1, 2, 0, 1, 0)
NP = 6 * AD
NROW = NP + 2
KTS, QC = T // 128, T // 512
UNTIL = 37


def attention_phase(nc, io, keep, signal):
    ctx = ExitStack()
    with ctx:
        def sb(name, shape, dt=FP32):
            return ctx.enter_context(nc.sbuf_tensor("a_" + name, shape, dt))

        def sig(name, per, unit=1):
            return signal("a_" + name, per, unit)

        cst, at, v_all = keep["cst"], keep["at"], keep["v_all"]
        const = lambda name, lo=0, hi=None: cst[:, at[name][0] + lo:(at[name][0] + hi if hi is not None else at[name][1])]
        cb16 = sb("masks", [128, 3, 128], BF16)
        qa = [sb(f"qa{b}", [NROW, 4, T], BF16) for b in range(B)]
        ka = [sb(f"ka{b}", [NROW, 4, T], BF16) for b in range(B)]
        v_st = [sb(f"v_st{b}", [128, KTS, 4, 32]) for b in range(B)]
        pt = [[sb(f"pt{x}{i}", [128, 2, 512]) for i in range(2)] for x in range(2)]
        o_sb = [sb(f"o_sb{b}", [128, T]) for b in range(B)]
        mx = sb("mx", [128, 4, KTS, 4])
        m = sb("m", [128, 4 * KTS])
        mt, mrow = sb("mt", [4 * KTS, 128]), sb("mrow", [4 * KTS, 2, 128], BF16)
        sc = [ctx.enter_context(nc.psum_tensor(f"a_sc{x}", [128, 2, 512], FP32)) for x in range(2)]
        po = [ctx.enter_context(nc.psum_tensor(f"a_po{x}", [128, 512], FP32)) for x in range(2)]
        pm = [ctx.enter_context(nc.psum_tensor(f"a_pm{x}", [128, 512], FP32)) for x in range(2)]

        CHUNKS = list(range(QC))[::-1]
        STEPS = [(qc, j) for qc in CHUNKS for j in range(4 * qc + 4)]
        NS = len(STEPS)
        last_step = {qc: max(s for s, (c, _) in enumerate(STEPS) if c == qc) + 1 for qc in CHUNKS}
        UNITS = [(qt, kc, h) for kc in CHUNKS for qt in range(KTS)[::-1] if qt // 4 >= kc for h in range(4)]
        NU = len(UNITS)
        unit_width = [min(512, 128 * (qt + 1) - 512 * kc) for qt, kc, h in UNITS]
        step_width = [512 - max(0, 128 * (j - 4 * qc)) for qc, j in STEPS]

        def units_of(step):
            upto = [sum(step_width[:min(s, UNTIL)]) / sum(step_width[:UNTIL]) for s in (step, step + 1)]
            edge = [sum(sum(unit_width[:i + 1]) <= f * sum(unit_width) + 1e-6 for i in range(NU)) for f in upto]
            return list(range(*edge))

        s_passed = sig("passed", 1).sem
        s_load = [[sig(f"loaded{b}{c}", 1, 16 * 12) for c in range(QC)] for b in range(B)]
        s_vst = [sig(f"v_ready{b}", 1) for b in range(B)]
        s_ones, s_one = sig("ones", 1), sig("dve_ones", 1)
        s_sc = [sig(f"scores{x}", B * NS) for x in range(2)]
        s_p = [sig(f"weights{x}", B * NS) for x in range(2)]
        s_pv = sig("summed", B * NS)
        s_o = sig("out_kept", B * QC)
        s_max, s_red = sig("max_scores", B * NU), sig("max_found", B * NU)
        s_m, s_mt, s_mrow = sig("m", B), sig("m_transposed", B), sig("m_rows", B)
        s_mload = [sig(f"m_loaded{b}", 1, 16 * 2) for b in range(B)]
        s_ostore = [sig(f"o_stored{b}", 1, 16) for b in range(B)]
        dve_step = sig("dve_step", 2 * B)
        block = ctx.enter_context(nc.Block())

        def load(sp, b, hg, c):
            tok = slice(512 * c, 512 * c + 512)
            for tile, n, parts in ((qa[b], "q", PARTS_Q), (ka[b], "k", PARTS_K)):
                for r, k in enumerate(parts):
                    src = io[n + "_dram"][k, b, bass.ds(hg * 64, 64), tok]
                    sp.dma_start(tile[AD * r:AD * r + AD, :, tok], src.rearrange("(h d) t -> d h t", d=AD)
                                 ).then_inc(s_load[b][c].sem, 16)

        def load_rows(sp, b, turn):
            for k in range(2):
                sp.dma_start(qa[b][NP + k:NP + k + 1, :, :].rearrange("o h (q t) -> o (h q) t", t=128),
                             mrow[:, k, :]).then_inc(s_mload[b].sem, 16)

        @block.sync
        def _(sp):
            for b in range(B):
                s_mload[b].open(sp)
                s_ostore[b].open(sp)
            for b in range(B):
                for c in CHUNKS:
                    load(sp, b, 0, c)
            sp.wait_ge(s_mrow.sem, B)
            load_rows(sp, 0, 0)
            with sp.Fori(0, 4) as u:
                for b in range(B):
                    for c in CHUNKS:
                        if c == 0:
                            sp.wait_ge(s_mrow.sem, s_mrow.at(u, b + 1))
                            load_rows(sp, 1 - b, u)
                        sp.wait_ge(s_pv.sem, s_pv.at(u, b * NS + last_step[c]))
                        sp.sem_inc(s_passed, 1)
                        load(sp, b, (u + 1) % 4, c)
                    sp.wait_ge(s_o.sem, s_o.at(u, (b + 1) * QC))
                    sp.dma_start(io["o_dram"][b, bass.ds(u * 128, 128), :], o_sb[b][:, :]).then_inc(s_ostore[b].sem, 16)
            for b in range(B):
                sp.wait_ge(s_ostore[b].sem, s_ostore[b].at(3, 1))
            sp.wait_ge(s_mload[0].sem, 32 * 6)
            for b in range(B):
                for c in CHUNKS:
                    sp.wait_ge(s_load[b][c].sem, 192 * 5)

        @block.gpsimd
        def _(pool):
            for b in range(B):
                nc.gpsimd.memset(v_st[b][:, :, :, 16:32], 1.0).then_inc(s_ones.sem, 1)
                s_vst[b].open(pool)
            pool.wait_ge(s_ones.sem, B)
            with pool.Fori(0, 4) as u:
                for b in range(B):
                    pool.wait_ge(s_pv.sem, s_pv.at(u, NS * (b + 1), back=1))
                    nc.gpsimd.tensor_copy(
                        v_st[b][:, :, :, 0:16],
                        v_all[:, b, :, bass.ds(u * 64, 64)].rearrange("p k (h d) -> p k h d", h=4)).then_inc(s_vst[b].sem, s_vst[b].up())

        @block.tensor
        def _(pe):
            for q in (*s_sc, s_pv):
                q.open(pe)
            pe.wait_ge(s_ones.sem, B)
            pe.wait_ge(s_one.sem, 1)
            mm = nc.tensor.matmul
            ident16, neg_kq, neg_qk = (cb16[:, i, :] for i in range(3))

            def max_unit(b, i):
                qt, kc, h = UNITS[i]
                width = min(512, 128 * (qt + 1) - 512 * kc)
                diag = kc == qt // 4
                out = pm[i % 2]
                last = mm(out[:, 0:width], qa[b][0:NP, h, 128 * qt:128 * qt + 128],
                          ka[b][0:NP, h, 512 * kc:512 * kc + width], start=True, stop=not diag)
                if diag:
                    last = mm(out[:, width - 128:width], ident16, neg_qk, start=False, stop=True)
                return last

            pe.sem_inc(s_max.sem, NU)
            for i, (qt, kc, h) in enumerate(UNITS):
                if i == 0 or kc != UNITS[i - 1][1]:
                    pe.wait_ge(s_load[0][kc].sem, 16 * 12)
                if i >= 2:
                    pe.wait_ge(s_red.sem, NU + i - 1)
                max_unit(0, i).then_inc(s_max.sem, 1)
            pe.wait_ge(s_m.sem, B)
            nc.tensor.transpose(pm[0][0:4 * KTS, 0:128], m[:, :], const("ident")).then_inc(s_mt.sem, B)
            with pe.Fori(0, 4) as u:
                for b in range(B):
                    other = 1 - b

                    def scores(s, x, turn=u):
                        qc, j = STEPS[s]
                        off = max(0, 128 * (j - 4 * qc))
                        n = b * NS + s
                        if n:
                            pe.wait_ge(s_p[x].sem, s_p[x].at(u, n))
                        else:
                            pe.wait_ge(s_p[x].sem, s_p[x].at(u, B * NS, back=1))
                        for y in range(2):
                            h = 2 * x + y
                            diag = j >= 4 * qc
                            last = mm(sc[x][:, y, off:512], ka[b][:, h, 128 * j:128 * j + 128],
                                      qa[b][:, h, 512 * qc + off:512 * qc + 512], start=True, stop=not diag)
                            if diag:
                                last = mm(sc[x][:, y, off:off + 128], ident16, neg_kq, start=False, stop=True)
                        last.then_inc(s_sc[x].sem, s_sc[x].up())

                    pe.wait_ge(s_mload[b].sem, s_mload[1].at(u, 1) if b else u * 32 + 64)
                    pe.wait_ge(s_vst[b].sem, s_vst[b].at(u, 1))

                    def maxima(units):
                        for i in units:
                            kc = UNITS[i][1]
                            if i == 0 or kc != UNITS[i - 1][1]:
                                pe.wait_ge(s_load[other][kc].sem, u * 192 + 192 * (b + 1))
                            k = b * NU + i
                            if k >= 2:
                                pe.wait_ge(s_red.sem, s_red.at(u, k - 1))
                            else:
                                pe.wait_ge(s_red.sem, s_red.at(u, B * NU + k - 1, back=1))
                            if i == 0:
                                pe.wait_ge(s_mrow.sem, s_mrow.at(u, 1) if b else s_mrow.at(u, 2, back=1))
                            max_unit(other, i).then_inc(s_max.sem, s_max.up())

                    scores(0, 0)
                    scores(0, 1)
                    for s, (qc, j) in enumerate(STEPS):
                        n = b * NS + s
                        off = max(0, 128 * (j - 4 * qc))
                        if s + 1 < NS:
                            scores(s + 1, 0)
                        us = units_of(s)
                        maxima(us[:2])
                        if s + 1 < NS:
                            scores(s + 1, 1)
                        maxima(us[2:3])
                        pe.wait_ge(s_p[0].sem, s_p[0].at(u, n + 1))
                        pe.wait_ge(s_p[1].sem, s_p[1].at(u, n + 1))
                        if j == 0:
                            o = b * QC + QC - 1 - qc
                            if o >= 2:
                                pe.wait_ge(s_o.sem, s_o.at(u, o - 1))
                            else:
                                pe.wait_ge(s_o.sem, s_o.at(u, B * QC + o - 1, back=1))
                        for h in range(4):
                            last = mm(po[qc % 2][32 * h:32 * h + 32, off:512], v_st[b][:, j, h, :],
                                      pt[h // 2][n % 2][:, h % 2, off:512], start=(j == 0), stop=(j == 4 * qc + 3),
                                      tile_position=(0, 32 * h), skip_group_check=True)
                        last.then_inc(s_pv.sem, s_pv.up())
                        maxima(us[3:])
                        if s == UNTIL + 1:
                            pe.wait_ge(s_m.sem, s_m.at(u, b + 1))
                            pe.sem_inc(s_passed, 1)
                            nc.tensor.transpose(pm[0][0:4 * KTS, 0:128], m[:, :], const("ident")).then_inc(s_mt.sem, s_mt.up())

        @block.scalar
        def _(act):
            for q in s_p:
                q.open(act)
            with act.Fori(0, 4) as u:
                for b in range(B):
                    for s, (qc, j) in enumerate(STEPS):
                        n = b * NS + s
                        off = max(0, 128 * (j - 4 * qc))
                        if n >= 2:
                            act.wait_ge(s_pv.sem, s_pv.at(u, n - 1))
                        else:
                            act.wait_ge(s_pv.sem, s_pv.at(u, B * NS + n - 1, back=1))
                        for x in range(2):
                            act.wait_ge(s_sc[x].sem, s_sc[x].at(u, n + 1))
                            nc.scalar.activation(pt[x][n % 2][:, :, off:512], sc[x][:, :, off:512],
                                                               ACT.Exp).then_inc(s_p[x].sem, s_p[x].up())

        @block.vector
        def _(dve):
            ve = nc.vector
            s_o.open(dve)
            for b in range(B):
                ve.memset(ka[b][NP:NROW, :, :], 1.0)
            for i, name in enumerate(("ident", "neg_kq", "neg_qk")):
                ve.tensor_copy(cb16[:, i, :], const(name))
            ve.memset(mx[:, :, :, :], -3e38).then_inc(s_one.sem, 1)
            dve.wait_ge(s_one.sem, 1)

            def reduce_unit(i):
                qt, kc, h = UNITS[i]
                width = min(512, 128 * (qt + 1) - 512 * kc)
                return ve.tensor_reduce(mx[:, h, qt, kc:kc + 1], pm[i % 2][:, 0:width], axis=AX.X, op=ALU.max)

            by_tile = mx[:, :, :, :].rearrange("p h q k -> p (h q) k")
            dve.sem_inc(s_red.sem, NU)
            for i in range(NU):
                dve.wait_ge(s_max.sem, NU + i + 1)
                reduce_unit(i).then_inc(s_red.sem, 1)
            dve.wait_ge(s_red.sem, 2 * NU)
            ve.tensor_reduce(m[:, :], by_tile, axis=AX.X, op=ALU.max).then_inc(s_m.sem, B)
            dve.wait_ge(s_mt.sem, B)
            ve.tensor_scalar(mt[:, :], pm[0][0:4 * KTS, 0:128], -1.0, None, ALU.mult).then_inc(dve_step.sem, B)
            dve.wait_ge(dve_step.sem, B)
            ve.tensor_copy(mrow[:, 0, :], mt[:, :]).then_inc(dve_step.sem, B)
            dve.wait_ge(dve_step.sem, 2 * B)
            ve.tensor_tensor(mrow[:, 1, :], mt[:, :], mrow[:, 0, :], ALU.subtract).then_inc(s_mrow.sem, B)
            with dve.Fori(0, 4) as u:
                for b in range(B):
                    for s, (qc, j) in enumerate(STEPS):
                        us = units_of(s)
                        for i in us:
                            dve.wait_ge(s_max.sem, s_max.at(u, b * NU + i + 1))
                            reduce_unit(i).then_inc(s_red.sem, s_red.up())
                            if i == NU - 1:
                                dve.wait_ge(s_red.sem, s_red.at(u))
                                ve.tensor_reduce(m[:, :], by_tile, axis=AX.X, op=ALU.max).then_inc(s_m.sem, s_m.up())
                        if s == UNTIL + 1:
                            dve.wait_ge(s_mt.sem, s_mt.at(u, b + 1))
                            dve.wait_ge(s_mload[b].sem, s_mload[1].at(u, 1) if b else u * 32 + 64)
                            ve.tensor_scalar(mt[:, :], pm[0][0:4 * KTS, 0:128], -1.0, None, ALU.mult).then_inc(dve_step.sem, dve_step.up())
                            dve.wait_ge(dve_step.sem, dve_step.at(u))
                            ve.tensor_copy(mrow[:, 0, :], mt[:, :]).then_inc(dve_step.sem, dve_step.up())
                            dve.wait_ge(dve_step.sem, dve_step.at(u))
                            ve.tensor_tensor(mrow[:, 1, :], mt[:, :], mrow[:, 0, :], ALU.subtract).then_inc(s_mrow.sem, s_mrow.up())
                        if j == 4 * qc + 3:
                            dve.wait_ge(s_pv.sem, s_pv.at(u, b * NS + s + 1))
                            if qc == QC - 1:
                                dve.wait_ge(s_ostore[b].sem, s_ostore[b].at(u, 1, back=1))
                            ve.tensor_copy(o_sb[b][:, 512 * qc:512 * qc + 512], po[qc % 2][:, :]).then_inc(s_o.sem, s_o.up())


STAGES = [("e0_up", "xf", "h0", "Gelu"), ("e2_l1", "xf", "h2", "Gelu"), ("e3_down", "xf", "h3", "Gelu"),
          ("e1_w1", "xf", "h1", "Silu"), ("e1_w2", "xf", "h1", "times"), ("e0_down", "h0", 0, "out"),
          ("e2_l2", "h2", "h4", "Gelu"), ("e1_down", "h1", 1, "out"), ("e3_up", "h3", "h5", "Gelu"),
          ("e2_l3", "h4", "h2", "Gelu"), ("e3_out", "h5", 3, "out"), ("e2_l4", "h2", 2, "out")]
WIDE = {"e0_up": (2, 4), "e2_l1": (2, 4), "e3_down": (2, 2), "e1_w1": (2, 4), "e1_w2": (2, 4),
        "e2_l2": (4, 4), "e3_up": (2, 4), "e2_l3": (4, 4),
        "e0_down": (4, 2), "e1_down": (4, 2), "e3_out": (4, 2), "e2_l4": (4, 2)}
MASKED = 64


def expert_phase(nc, io, keep, signal):
    ctx = ExitStack()
    with ctx:
        def sb(name, shape, dt=FP32):
            return ctx.enter_context(nc.sbuf_tensor("e_" + name, shape, dt))

        def sig(name, per, unit=1):
            return signal("e_" + name, per, unit)

        cst, at, vec, xn_all = (keep[n] for n in ("cst", "at", "vec", "xn_all"))
        const = lambda name, lo=0, hi=None: cst[:, at[name][0] + lo:(at[name][0] + hi if hi is not None else at[name][1])]
        v = lambda name, h: vec[:, VECS.index(name), h:h + 1]
        w = {n: sb(n, [128, i, 128 * o]) for n, (i, o) in WIDE.items()}
        w["wo"], w["gate_w"] = sb("wo", [128, 2, C]), sb("gate_w", [128, 2, EXPERTS])
        NW = len(w)
        ao, asum = sb("ao", [128, HALVES, ECOLS]), sb("asum", [128, HALVES, ECOLS])
        x2, xf = sb("x2", [128, HALVES, ECOLS]), sb("xf", [128, HALVES, ECOLS])
        rms = sb("rms", [128, ECOLS])
        hid = {f"h{i}": sb(f"h{i}", [128, 2 if i == 3 else 4, ECOLS]) for i in range(6)}
        hid["xf"] = xf
        acc, s_tok, x_tok = sb("acc", [128, 4, C]), sb("s_tok", [128, 4, C]), sb("x_tok", [128, 4, C])
        x2sq, x2_tok = sb("x2sq", [128, HALVES, ECOLS]), sb("x2_tok", [128, 4, C])
        SE = [128, 4, EXPERTS]
        lg, ok_, zero, ex, pr, sel, wt, wt_next = (
            sb(n, SE) for n in ("lg", "ok_", "zero", "ex", "pr", "sel", "wt", "wt_next"))
        okm = sb("okm", SE, mybir.dt.int32)
        mxl, den = sb("mxl", [128, 4]), sb("den", [128, 4])
        cmp_, eq = sb("cmp_", [128, 4, EXPERTS, EXPERTS]), sb("eq", [128, 4, EXPERTS, EXPERTS])
        ps = ctx.enter_context(nc.psum_tensor("e_ps", [128, 8, 512], FP32))

        s_w = sig("weights", 1, 16 * NW)
        s_in, s_xin, s_ready_w = sig("attention_in", 1, 16 * 16), sig("x_s_in", 1, 16 * 8), sig("weights_masked", 1)
        s_ao, s_wo, s_x2, s_x2sq, s_ms, s_rms, s_xf = (sig(n, 1) for n in (
            "ao", "projected", "x2", "x2_squared", "x2_sum", "x2_rms", "xf"))
        s_gate, s_x2t, s_acc0, s_soft, s_exp, s_wt = (sig(n, 1) for n in (
            "logits", "x2_transposed", "x2_kept", "logits_shifted", "logits_exp", "gates"))
        BLOCKS = [(i, o) for i, (n, _, _, f) in enumerate(STAGES) if f != "out" for o in range(WIDE[n][1])]
        s_hid = sig("hidden", len(BLOCKS))
        by = {"A": sig("act_took", sum(STAGES[i][3] != "times" for i, _ in BLOCKS)),
              "V": sig("dve_took", sum(STAGES[i][3] == "times" for i, _ in BLOCKS))}
        took = []
        for i, o in BLOCKS:
            who = "V" if STAGES[i][3] == "times" else "A"
            took.append((who, 1 + sum(w_ == who for w_, _ in took)))
        first_block = {i: min(n for n, (k, _) in enumerate(BLOCKS) if k == i) for i in {i for i, _ in BLOCKS}}
        s_down, s_sum = sig("expert_out", 4), sig("expert_added", 4)
        s_gated, s_out = sig("silu", 1), sig("out", 1)
        s_store = sig("out_stored", 1, 16 * 4)
        s_passed = sig("passed", 1).sem
        dve_step = sig("dve_step", 22)
        block = ctx.enter_context(nc.Block())

        @block.sync
        def _(sp):
            for n, tile in w.items():
                sp.dma_start(tile[:, :, :], io[n]).then_inc(s_w.sem, 16)

            def load_attention(t):
                for h in range(HALVES):
                    for b in range(B):
                        rows_ = io["o_dram"][b, :, bass.ds(t * ETT, ETT)].rearrange("(g h e) t -> g h e t", h=8, e=32)
                        for tile, lo in ((ao, 0), (asum, 16)):
                            for r in range(2):
                                sp.dma_start(tile[64 * r:64 * r + 64, h, ETT * b:ETT * b + ETT],
                                             rows_[h, 4 * r:4 * r + 4, lo:lo + 16, :]).then_inc(s_in.sem, 16)

            def turn(t, more):
                if more:
                    sp.wait_ge(s_wo.sem, s_wo.at(t, 0))
                    load_attention(t + 1)
                sp.wait_ge(s_out.sem, s_out.at(t, 1, back=1))
                for s in range(4):
                    tok = bass.ds(t * ETT + (s % 2) * 128, 128)
                    sp.dma_start(s_tok[:, s, :], io["s_dram"][s // 2, tok, :]).then_inc(s_xin.sem, 16)
                    sp.dma_start(x_tok[:, s, :], io["x"][s // 2, tok, :]).then_inc(s_xin.sem, 16)
                sp.wait_ge(s_out.sem, s_out.at(t, 1))
                for s in range(4):
                    sp.dma_start(io["out"][s // 2, bass.ds(t * ETT + (s % 2) * 128, 128), :],
                                 acc[:, s, :]).then_inc(s_store.sem, 16)

            s_store.open(sp)
            s_xin.open(sp)
            load_attention(0)
            with sp.Fori(0, ENT - 1) as t:
                turn(t, True)
            turn(ENT - 1, False)
            sp.wait_ge(s_store.sem, s_store.at(ENT - 1, 1))

        @block.tensor
        def _(pe):
            for q in (s_hid, s_down):
                q.open(pe)
            mm = nc.tensor.matmul
            pe.wait_ge(s_w.sem, 16 * NW)
            pe.wait_ge(s_ready_w.sem, 1)

            def project(t):
                pe.wait_ge(s_ao.sem, s_ao.at(t, 1))
                for h in range(2):
                    for k in range(2):
                        last = mm(ps[:, 4 + h, :], w["wo"][:, k, 128 * h:128 * h + 128], ao[:, k, :], start=(k == 0), stop=(k == 1))
                last.then_inc(s_wo.sem, 1)

            def sum_and_transpose(t):
                pe.wait_ge(s_x2sq.sem, s_x2sq.at(t, 1))
                for h in range(2):
                    last = mm(ps[:, 3, :], const("ones128"), x2sq[:, h, :], start=(h == 0), stop=(h == 1))
                last.then_inc(s_ms.sem, 1)
                for s in range(4):
                    for h in range(2):
                        last = nc.tensor.transpose(ps[:, 4 + s // 2, 256 * (s % 2) + 128 * h:256 * (s % 2) + 128 * h + 128],
                                                   x2[:, h, 128 * s:128 * s + 128], const("ident"))
                last.then_inc(s_x2t.sem, 1)

            def logits(t):
                pe.wait_ge(s_xf.sem, s_xf.at(t, 1))
                for s in range(4):
                    for h in range(2):
                        last = mm(ps[:, 3, 4 * s:4 * s + 4], xf[:, h, 128 * s:128 * s + 128], w["gate_w"][:, h, :],
                                  start=(h == 0), stop=(h == 1))
                last.then_inc(s_gate.sem, 1)

            def turn(t, more):
                downs = 0
                written = {}
                for i, (name, src, dst, func) in enumerate(STAGES):
                    ins, outs = WIDE[name]
                    if src == "xf":
                        pe.wait_ge(s_xf.sem, s_xf.at(t, 0))
                    else:
                        who, n = took[written[src]]
                        pe.wait_ge(by[who].sem, by[who].at(t, n))
                    if func == "out":
                        downs += 1
                        if downs > 1:
                            pe.wait_ge(s_sum.sem, s_sum.at(t, downs - 1))
                        else:
                            pe.wait_ge(s_sum.sem, s_sum.at(t, 4, back=1))
                        for s in range(4):
                            for k in range(ins):
                                last = mm(ps[:, 6 + s // 2, 256 * (s % 2):256 * (s % 2) + 256],
                                          hid[src][:, k, 128 * s:128 * s + 128], w[name][:, k, :],
                                          start=(k == 0), stop=(k == ins - 1))
                        last.then_inc(s_down.sem, s_down.up())
                    for o in range(outs if func != "out" else 0):
                        n = first_block[i] + o
                        if n >= 3:
                            who, m = took[n - 3]
                            pe.wait_ge(by[who].sem, by[who].at(t, m))
                        else:
                            who, m = took[len(took) - 3 + n]
                            pe.wait_ge(by[who].sem, by[who].at(t, m, back=1))
                        for k in range(ins):
                            last = mm(ps[:, n % 3, :], w[name][:, k, 128 * o:128 * o + 128], hid[src][:, k, :],
                                      start=(k == 0), stop=(k == ins - 1))
                        last.then_inc(s_hid.sem, s_hid.up())
                        written[dst] = n
                    if more and name == "e1_w2":
                        project(t)
                    if more and name == "e0_down":
                        sum_and_transpose(t)
                    if more and name == "e2_l2":
                        logits(t)
                for q in (s_hid, s_down):
                    q.restart()

            project(-1)
            sum_and_transpose(-1)
            logits(-1)
            with pe.Fori(0, ENT - 1) as t:
                turn(t, True)
            turn(ENT - 1, False)

        @block.scalar
        def _(act):
            for q in (by["A"], s_gated):
                q.open(act)
            f = nc.scalar.activation

            def squares(t):
                act.wait_ge(s_x2.sem, s_x2.at(t, 1))
                f(x2sq[:, :, :], x2[:, :, :], ACT.Square).then_inc(s_x2sq.sem, 1)
                act.wait_ge(s_ms.sem, s_ms.at(t, 1))
                f(rms[:, :], ps[:, 3, :], ACT.Sqrt, bias=const("eps", 2, 3), scale=1.0 / C).then_inc(s_rms.sem, 1)
                act.wait_ge(s_x2t.sem, s_x2t.at(t, 1))
                f(x2_tok[:, :, :].rearrange("p s c -> p (s c)"),
                  ps[:, 4:6, :].rearrange("p a c -> p (a c)"), ACT.Copy).then_inc(s_acc0.sem, 1)

            def exps(t):
                act.wait_ge(s_soft.sem, s_soft.at(t, 1))
                f(ex[:, :, :], lg[:, :, :], ACT.Exp).then_inc(s_exp.sem, 1)

            def turn(t, more):
                for n, (i, o) in enumerate(BLOCKS):
                    name, src, dst, func = STAGES[i]
                    if func == "times":
                        continue
                    if more and name == "e2_l2" and o == 0:
                        act.wait_ge(s_down.sem, s_down.at(t, 1))
                        act.wait_ge(s_sum.sem, s_sum.at(t, 1))
                        squares(t)
                    act.wait_ge(s_hid.sem, s_hid.at(t, n + 1))
                    f(hid[dst][:, o, :], ps[:, n % 3, :], ACT.Gelu if func == "Gelu" else ACT.Silu
                      ).then_inc(by["A"].sem, by["A"].up())
                    if more and name == "e3_up" and o == 3:
                        exps(t)
                act.wait_ge(s_sum.sem, s_sum.at(t, 4))
                f(acc[:, :, :], acc[:, :, :], ACT.Silu).then_inc(s_gated.sem, 1)
                by["A"].restart()

            squares(-1)
            exps(-1)
            with act.Fori(0, ENT - 1) as t:
                turn(t, True)
            turn(ENT - 1, False)

        @block.vector
        def _(dve):
            for q in (by["V"], s_sum, s_out):
                q.open(dve)
            ve = nc.vector
            dve.wait_ge(s_w.sem, 16 * NW)
            for n in ("wo", "e0_down", "e1_down", "e2_l4", "e3_out"):
                ve.memset(w[n][:, :, 0:MASKED], 0.0)
            ve.memset(zero[:, :, :], 0.0).then_inc(s_ready_w.sem, 1)
            dve.wait_ge(s_ready_w.sem, 1)

            def divide(t):
                dve.wait_ge(s_in.sem, s_in.at(t, 1))
                ve.reciprocal(asum[:, :, :], asum[:, :, :]).then_inc(dve_step.sem, dve_step.up())
                dve.wait_ge(dve_step.sem, dve_step.at(t))
                ve.tensor_tensor(ao[:, :, :], ao[:, :, :], asum[:, :, :], ALU.mult).then_inc(s_ao.sem, 1)

            def residual(t):
                dve.wait_ge(s_wo.sem, s_wo.at(t, 1))
                for h in range(2):
                    last = ve.tensor_tensor(x2[:, h, :].rearrange("p (b t) -> p b t", b=B),
                                            ps[:, 4 + h, :].rearrange("p (b t) -> p b t", b=B),
                                            xn_all[:, h, :, bass.ds((t + 1) * ETT + 1, ETT)], ALU.add)
                last.then_inc(s_x2.sem, 1)
                dve.wait_ge(s_x2.sem, s_x2.at(t, 1))

            def normalise(t):
                dve.wait_ge(s_rms.sem, s_rms.at(t, 1))
                ve.reciprocal(rms[:, :], rms[:, :]).then_inc(dve_step.sem, dve_step.up())
                dve.wait_ge(dve_step.sem, dve_step.at(t))
                for h in range(2):
                    last = ve.scalar_tensor_tensor(xf[:, h, :], x2[:, h, :], v("n2_w", h), rms[:, :], ALU.mult, ALU.mult)
                last.then_inc(s_xf.sem, 1)

            wide = lambda a: a.unsqueeze(2).to_broadcast([128, 4, EXPERTS])

            def shift_logits(t):
                dve.wait_ge(s_gate.sem, s_gate.at(t, 1))
                ve.tensor_copy(lg[:, :, :], ps[:, 3, 0:16].rearrange("p (s e) -> p s e", e=EXPERTS)).then_inc(dve_step.sem, dve_step.up())
                dve.wait_ge(dve_step.sem, dve_step.at(t))
                ve.tensor_tensor(okm[:, :, :], lg[:, :, :], lg[:, :, :], ALU.is_equal).then_inc(dve_step.sem, dve_step.up())
                dve.wait_ge(dve_step.sem, dve_step.at(t))
                ve.tensor_copy(ok_[:, :, :], zero[:, :, :]).then_inc(dve_step.sem, dve_step.up())
                dve.wait_ge(dve_step.sem, dve_step.at(t))
                dve.sem_inc(s_passed, 1)
                ve.copy_predicated(ok_[:, :, :], okm[:, :, :], lg[:, :, :]).then_inc(dve_step.sem, dve_step.up())
                dve.wait_ge(dve_step.sem, dve_step.at(t))
                ve.tensor_scalar(ok_[:, :, :], ok_[:, :, :], 3.4028234e38, -3.4028234e38, ALU.min, ALU.max).then_inc(dve_step.sem, dve_step.up())
                dve.wait_ge(dve_step.sem, dve_step.at(t))
                ve.tensor_reduce(mxl[:, :], ok_[:, :, :], axis=AX.X, op=ALU.max).then_inc(dve_step.sem, dve_step.up())
                dve.wait_ge(dve_step.sem, dve_step.at(t))
                ve.tensor_tensor(lg[:, :, :], ok_[:, :, :], wide(mxl[:, :]), ALU.subtract).then_inc(s_soft.sem, 1)
                dve.wait_ge(s_soft.sem, s_soft.at(t, 1))

            def top_two(t):
                dve.wait_ge(s_exp.sem, s_exp.at(t, 1))
                ve.tensor_reduce(den[:, :], ex[:, :, :], axis=AX.X, op=ALU.add).then_inc(dve_step.sem, dve_step.up())
                dve.wait_ge(dve_step.sem, dve_step.at(t))
                ve.reciprocal(den[:, :], den[:, :]).then_inc(dve_step.sem, dve_step.up())
                dve.wait_ge(dve_step.sem, dve_step.at(t))
                ve.tensor_tensor(pr[:, :, :], ex[:, :, :], wide(den[:, :]), ALU.mult).then_inc(dve_step.sem, dve_step.up())
                dve.wait_ge(dve_step.sem, dve_step.at(t))
                other = pr[:, :, :].unsqueeze(2).to_broadcast([128, 4, EXPERTS, EXPERTS])
                this = pr[:, :, :].unsqueeze(3).to_broadcast([128, 4, EXPERTS, EXPERTS])
                ve.tensor_tensor(cmp_[:, :, :, :], other, this, ALU.is_gt)
                ve.tensor_tensor(eq[:, :, :, :], other, this, ALU.is_equal).then_inc(dve_step.sem, dve_step.up())
                dve.wait_ge(dve_step.sem, dve_step.at(t))
                earlier = const("earlier").rearrange("p (e j) -> p e j", j=EXPERTS).unsqueeze(1)\
                    .to_broadcast([128, 4, EXPERTS, EXPERTS])
                ve.tensor_tensor(eq[:, :, :, :], eq[:, :, :, :], earlier, ALU.mult).then_inc(dve_step.sem, dve_step.up())
                dve.wait_ge(dve_step.sem, dve_step.at(t))
                ve.tensor_tensor(cmp_[:, :, :, :], cmp_[:, :, :, :], eq[:, :, :, :], ALU.add).then_inc(dve_step.sem, dve_step.up())
                dve.wait_ge(dve_step.sem, dve_step.at(t))
                ve.tensor_reduce(sel[:, :, :], cmp_[:, :, :, :], axis=AX.X, op=ALU.add).then_inc(dve_step.sem, dve_step.up())
                dve.wait_ge(dve_step.sem, dve_step.at(t))
                ve.scalar_tensor_tensor(wt_next[:, :, :], sel[:, :, :], 2.0, pr[:, :, :], ALU.is_lt, ALU.mult).then_inc(dve_step.sem, dve_step.up())
                dve.wait_ge(dve_step.sem, dve_step.at(t))
                ve.tensor_reduce(den[:, :], wt_next[:, :, :], axis=AX.X, op=ALU.add).then_inc(dve_step.sem, dve_step.up())
                dve.wait_ge(dve_step.sem, dve_step.at(t))
                ve.tensor_scalar(den[:, :], den[:, :], 1e-8, None, ALU.add).then_inc(dve_step.sem, dve_step.up())
                dve.wait_ge(dve_step.sem, dve_step.at(t))
                ve.reciprocal(den[:, :], den[:, :]).then_inc(dve_step.sem, dve_step.up())
                dve.wait_ge(dve_step.sem, dve_step.at(t))
                ve.tensor_tensor(wt_next[:, :, :], wt_next[:, :, :], wide(den[:, :]), ALU.mult).then_inc(dve_step.sem, dve_step.up())
                dve.wait_ge(dve_step.sem, dve_step.at(t))

            def turn(t, more):
                ve.tensor_copy(wt[:, :, :], wt_next[:, :, :]).then_inc(dve_step.sem, dve_step.up())
                dve.wait_ge(dve_step.sem, dve_step.at(t))
                if more:
                    divide(t)
                dve.wait_ge(s_acc0.sem, s_acc0.at(t, 0))
                downs = 0
                for i, (name, src, dst, func) in enumerate(STAGES):
                    if func == "times":
                        for o in range(4):
                            n = first_block[i] + o
                            dve.wait_ge(s_hid.sem, s_hid.at(t, n + 1))
                            who, m = took[first_block[i - 1] + o]
                            dve.wait_ge(by[who].sem, by[who].at(t, m))
                            ve.tensor_tensor(hid[dst][:, o, :], ps[:, n % 3, :], hid[dst][:, o, :], ALU.mult
                                             ).then_inc(by["V"].sem, by["V"].up())
                        if more:
                            residual(t)
                    if func == "out":
                        downs += 1
                        if downs == 1:
                            dve.wait_ge(s_store.sem, s_store.at(t, 1, back=1))
                        dve.wait_ge(s_down.sem, s_down.at(t, downs))
                        for s in range(4):
                            last = ve.scalar_tensor_tensor(acc[:, s, :], ps[:, 6 + s // 2, 256 * (s % 2):256 * (s % 2) + 256],
                                                           wt[:, s, dst:dst + 1], (x2_tok if downs == 1 else acc)[:, s, :],
                                                           ALU.mult, ALU.add)
                        last.then_inc(s_sum.sem, s_sum.up())
                        dve.wait_ge(s_sum.sem, s_sum.at(t))
                        if more and name == "e0_down":
                            normalise(t)
                        if more and name == "e1_down":
                            shift_logits(t)
                        if more and name == "e3_out":
                            top_two(t)
                dve.wait_ge(s_xin.sem, s_xin.at(t, 1))
                dve.wait_ge(s_gated.sem, s_gated.at(t, 1))
                ve.tensor_tensor(acc[:, :, :], acc[:, :, :], s_tok[:, :, :], ALU.mult).then_inc(dve_step.sem, dve_step.up())
                dve.wait_ge(dve_step.sem, dve_step.at(t))
                ve.tensor_tensor(acc[:, :, :], acc[:, :, :], x_tok[:, :, :], ALU.add).then_inc(s_out.sem, 1)
                if more:
                    dve_step.whole()
                for q in (by["V"], s_sum, dve_step):
                    q.restart()

            divide(-1)
            residual(-1)
            normalise(-1)
            shift_logits(-1)
            top_two(-1)
            dve_step.restart(dve)
            with dve.Fori(0, ENT - 1) as t:
                turn(t, True)
            turn(ENT - 1, False)


def program(nc, io):
    ctx = ExitStack()
    with ctx:
        at, width = table_at()
        io["s_dram"] = nc.dram_tensor("s_scratch", (B, T, C), FP32, kind="Internal").ap()
        for n in "qk":
            io[n + "_dram"] = nc.dram_tensor(n + "_scratch", (3, B, C, T), BF16, kind="Internal").ap()
        io["o_dram"] = nc.dram_tensor("o_scratch", (B, AH * 32, T), FP32, kind="Internal").ap()
        keep = {"at": at, "n_const": 32}
        keep["cst"] = ctx.enter_context(nc.sbuf_tensor("cst", [128, width], FP32))
        keep["vec"] = ctx.enter_context(nc.sbuf_tensor("vec", [128, len(VECS), 2], FP32))
        keep["xn_all"] = ctx.enter_context(nc.sbuf_tensor("xn_all", [128, HALVES, B, T + 1], FP32))
        keep["s_const"] = ctx.enter_context(nc.semaphore("s_const"))

        def signal(name, per, unit=1):
            return Signal(ctx.enter_context(nc.semaphore(name)), per, unit)

        nc.sync.dma_start(keep["cst"][:, :], io["table"]).then_inc(keep["s_const"], 16)
        nc.sync.dma_start(keep["vec"][:, :, :], io["vecs"]).then_inc(keep["s_const"], 16)
        with ExitStack() as v_life:
            keep["v_all"] = v_life.enter_context(nc.sbuf_tensor("v_all", [128, B, T // 128, C], FP32))
            recurrent_phase(nc, io, keep, signal)
            attention_phase(nc, io, keep, signal)
        expert_phase(nc, io, keep, signal)


def host_tables():
    import numpy as np
    at, width = table_at()
    tab = np.zeros((128, width), np.float32)
    def put(name, a):
        tab[:, at[name][0]:at[name][1]] = a.reshape(128, -1)
    r = np.arange(128)
    put("ident", np.eye(128))
    put("neg_kq", (r[None] < r[:, None]) * -1e30)
    put("neg_qk", (r[None] > r[:, None]) * -1e30)
    put("ones64", (r[:, None] // 64 == r[None] // 64))
    put("ones16", (r[:, None] // 16 == r[None] // 16))
    put("ones128", np.ones((128, 128)))
    i, j = np.arange(64)[:, None], np.arange(64)[None]
    two = lambda a: np.concatenate([a, a], axis=0).astype(np.float32)
    one = np.ones((64, 64))
    put("amask", two(np.concatenate([i < j, i <= j, one, i < j, i <= j, one, i > j], axis=1)))
    put("eye64", two(i == j))
    off = lambda n: (i // (2 * n) == j // (2 * n)) & ((i // n) % 2 == 1) & ((j // n) % 2 == 0)
    put("low0", two(off(1)))
    put("low0t", two(off(1).T))
    put("lev", two(np.concatenate([off(2 ** k).T for k in range(1, LEVELS)], axis=1)))
    put("reset", np.broadcast_to((np.arange(COLS) % CH != 0), (128, COLS)))
    put("eps", np.broadcast_to(np.array([LN_EPS, GN_EPS, RMS_EPS, AD * RMS_EPS]), (128, 4)))
    e, j = np.arange(4)[:, None], np.arange(4)[None]
    put("earlier", np.broadcast_to((j < e).reshape(1, 16), (128, 16)))
    return tab


def ffn_arrays(give, g, rows):
    for n in ("wq", "wk", "wv", "wo", "gate_w", "e0_up", "e0_down", "e1_w1", "e1_w2", "e1_down",
              "e2_l1", "e2_l2", "e2_l3", "e2_l4", "e3_down", "e3_up", "e3_out"):
        give(n, rows(g("L0_ffn_" + n).T))


def kernel(**inputs):
    import numpy as np
    import concourse.bacc as _bacc
    from concourse.bass_utils import run_bass_kernel_spmd as _run

    nc = _bacc.Bacc("TRN2", target_bir_lowering=False, num_devices=1)
    arrays, io = {}, {}

    def give(name, a):
        a = np.ascontiguousarray(a)
        arrays["in_" + name] = a
        io[name] = nc.dram_tensor("in_" + name, a.shape, mybir.dt.from_np(a.dtype), kind="ExternalInput").ap()

    g = lambda n: np.asarray(inputs[n])
    rows = lambda a: a.reshape(-1, 128, a.shape[1]).transpose(1, 0, 2)
    give("x", g("L0_attn_x"))
    for n in ("W_r", "W_k", "W_v", "W_o", "w1", "a1", "g1"):
        give(n, rows(g("L0_attn_" + n)))
    for n in ("w2", "a2", "g2"):
        give(n, g("L0_attn_" + n))
    vecs = [g("L0_ffn_" + n) if n in ("n1_w", "n2_w") else np.tile(g("L0_ffn_" + n), AH) if n in ("qn_w", "kn_w")
            else g("L0_attn_" + n).reshape(-1) for n in VECS]
    give("vecs", np.stack(vecs).reshape(len(VECS), 2, 128).transpose(2, 0, 1))
    give("table", host_tables())
    ffn_arrays(give, g, rows)
    io["out"] = nc.dram_tensor("out_dram", (B, T, C), FP32, kind="ExternalOutput").ap()
    program(nc, io)
    r = _run(nc, [arrays], core_ids=[0])
    return r.results[0]["out_dram"]
```

```python
import concourse.bass as bass
from concourse import mybir
from contextlib import ExitStack
import math

FP32 = mybir.dt.float32
BF16 = mybir.dt.bfloat16
F32R = mybir.dt.float32r
ALU = mybir.AluOpType
ACT = mybir.ActivationFunctionType
AX = mybir.AxisListType

B, T, C = 2, 2048, 256
HALVES = C // 128
RH, RD = 4, 64
CH = 64
TT = 128
NT = T // TT
COLS = B * TT
NCH = TT // CH
CB = COLS // CH
PAIRS = CB * HALVES
LEVELS = int(math.log2(CH))
LN_EPS, GN_EPS, RMS_EPS = 1e-5, 0.00064, 1.1920929e-07
NEG_DECAY = math.exp(-0.5)

AH, AD, HID = 16, 16, 512
EXPERTS = 4
ETT = 128
ENT, ECOLS = T // ETT, B * ETT

F32_TABLE = [("ident", 128), ("neg_kq", 128), ("neg_qk", 128), ("ones64", 128), ("ones16", 128), ("ones128", 128),
             ("amask", 7 * 64), ("eye64", 64), ("low0", 64), ("low0t", 64),
             ("lev", (LEVELS - 1) * 64), ("reset", COLS), ("eps", 4), ("earlier", EXPERTS * EXPERTS)]
VECS = ["x_r", "x_w", "x_k", "x_v", "x_a", "x_g", "w0", "a0", "k_k", "k_a", "r_k", "ln_w", "ln_b",
        "n1_w", "n2_w", "qn_w", "kn_w"]


def table_at():
    at, n = {}, 0
    for name, width in F32_TABLE:
        at[name] = (n, n + width)
        n += width
    return at, n


class Signal:

    def __init__(self, sem, per, unit=1):
        self.sem, self.per, self.unit, self.n = sem, per, unit, 0

    def open(self, eng):
        eng.sem_inc(self.sem, self.per * self.unit)

    def up(self):
        self.n += 1
        return self.unit

    def at(self, turn, n=None, back=0):
        return turn * (self.per * self.unit) + (self.per * (1 - back) + (self.n if n is None else n)) * self.unit

    def restart(self, eng=None):
        if eng is not None and self.n < self.per:
            eng.sem_inc(self.sem, (self.per - self.n) * self.unit)
        self.n = 0

    def whole(self):
        assert self.n == self.per, (self.n, self.per)


FIRST = -1


def all_strands(eng, front, back, tail):
    for _ in front(FIRST):
        pass

    def turn(t, before, after):
        strands = [tail(t - 1) if before else iter(()), front(t) if after else iter(())]

        def give_way():
            for strand in strands:
                next(strand, None)

        back(t, give_way)
        for strand in strands:
            for _ in strand:
                raise AssertionError("the strands differ in length")

    turn(0, False, True)
    with eng.Fori(1, NT - 1) as t:
        turn(t, True, True)
    turn(NT - 1, True, False)
    for _ in tail(NT - 1):
        pass


def recurrent_phase(nc, io, keep, signal):
    ctx = ExitStack()
    with ctx:
        def sb(name, shape, dt=FP32):
            return ctx.enter_context(nc.sbuf_tensor("r_" + name, shape, dt))

        def sig(name, per, unit=1):
            return signal("r_" + name, per, unit)

        cst, at, vec, xn_all, v_all = (keep[n] for n in ("cst", "at", "vec", "xn_all", "v_all"))
        s_const = keep["s_const"]

        def const(name, lo=0, hi=None):
            a, b = at[name]
            return cst[:, a + lo:(a + hi if hi is not None else b)]

        def v(name, h):
            return vec[:, VECS.index(name), h:h + 1]

        ident, ones64 = const("ident"), const("ones64")
        FM = [128, HALVES, COLS]
        w_in = {n: sb(n, [128, HALVES, w]) for n, w in
                [("W_r", C), ("W_k", C), ("W_v", C), ("W_o", C), ("w1", 64), ("a1", 64), ("g1", 128),
                 ("wq", C), ("wk", C), ("wv", C)]}
        w_up = {n: sb(n, [k, C]) for n, k in [("w2", 64), ("a2", 64), ("g2", 128)]}
        NWT = len(w_in) + len(w_up)
        x_tok, xn_tok = sb("x_tok", [128, B, C]), sb("xn_tok", [128, B, C])
        bn6, mv = sb("bn6", [128, B, 6]), sb("mv", [128, B, 2])
        std, rstd = sb("std", [128, B]), sb("rstd", [128, B])
        dx = sb("dx", FM)
        mixed = {n: sb("x" + n, FM) for n in "gwakrv"}
        tg, tw, ta = sb("tg", [128, COLS]), sb("tw", [64, COLS]), sb("ta", [64, COLS])
        kraw, rT, vT, gT, sg, av, kk, sq, nrm, kmod, bonus = (
            sb(n, FM) for n in ("kraw", "rT", "vT", "gT", "sg", "av", "kk", "sq", "nrm", "kmod", "bonus"))
        cs, csp = dx, mixed["g"]
        p_now, p_inv, p_prev, rk = mixed["w"], mixed["a"], mixed["k"], mixed["r"]
        rdec = sb("rdec", FM)
        xsq, rms = sb("xsq", FM), sb("rms", [128, COLS])
        hT = xsq
        raw = {n: sb(n + "_raw", FM) for n in "qk"}
        hsq = {n: sb(n + "_sq", FM) for n in "qk"}
        part = {n: sb(n + "_part", [128, 3, HALVES, COLS], BF16) for n in "qk"}
        v_st = sb("v_st", [128, CB, HALVES, 64])
        ari = sb("ari", [128, HALVES, CB, 3, 64])
        bT, kT = sb("bT", [128, HALVES, CB, 64]), sb("kT", [128, HALVES, CB, 64])
        p_end = sb("p_end", [128, NCH, B, HALVES])
        am = sb("am", [128, PAIRS, 7, 64])
        inv, invT, zz = (sb(n, [128, PAIRS, 64]) for n in ("inv", "invT", "zz"))
        lj = [sb(f"lj{i}", [128, PAIRS, 64]) for i in range(2)]
        state, stmp, g_sb, u_sb = (sb(n, [128, B, HALVES, 64]) for n in ("state", "stmp", "g_sb", "u_sb"))
        yT, yc, ystd, yg, gain, shift = (sb(n, FM) for n in ("yT", "yc", "ystd", "yg", "gain", "shift"))
        ysq = yg
        s_tok = sb("s_tok", [128, B, C])

        ps = ctx.enter_context(nc.psum_tensor("r_ps", [128, 8, 512], FP32))
        F = 4
        JOBS = [("tr", "A"), ("g1", "A"), ("w1", "A"), ("a1", "V"), ("k", "V"), ("ms", "A"), ("w2", "A"),
                ("a2", "A"), ("r", "A"), ("v", "A"), ("n", "A"), ("aq", "A"), ("ak", "A"), ("av", "A"),
                ("qs", "A"), ("ks", "A"), ("vst", "V"), ("g2", "V"), ("b", "V")]
        NJ = len(JOBS)
        job_no = {n: i for i, (n, _) in enumerate(JOBS)}
        taken = {}
        for who in "AV":
            for i, n in enumerate([n for n, w in JOBS if w == who]):
                taken[n] = (who, i + 1)

        def bank(name, m=128, wide=2 * COLS):
            return ps[0:m, job_no[name] % F, 0:wide]

        def halves(ap):
            return ap.rearrange("p (h c) -> p h c", h=HALVES)

        def by_batch(ap):
            return ap.rearrange("p (b t) -> p b t", b=B)

        s_w = sig("weights", 1, 16 * NWT)
        s_x, s_parts = sig("x_in", 1, 32), sig("parts_stored", 1, 16 * 24)
        s_var, s_std, s_xn, s_mix = sig("var", 1), sig("std", 1), sig("xn", 1), sig("mixed", 6)
        s_job = sig("job", NJ)
        took = {"A": sig("act_took", sum(w == "A" for _, w in JOBS)),
                "V": sig("dve_took", sum(w == "V" for _, w in JOBS))}
        s_kk, s_sq, s_cs, s_exp, s_rk, s_feat = (sig(n, 1) for n in (
            "kk", "kk_squared", "log_decay", "decays", "r_times_k", "features"))
        s_adec, s_vst = sig("a_r_decayed", 1), sig("v_stacked", 1)
        s_xsq, s_h, s_hsq, s_cut = sig("xn_squared", 1), sig("h", 1), sig("qk_squared", 2), sig("parts", 2)
        s_am, s_amsb = sig("products", PAIRS), sig("products_kept", PAIRS)
        s_lj, (s_z, s_zsb, s_inv, s_invsb) = sig("level_off", LEVELS), (sig(n, LEVELS - 1) for n in (
            "z", "z_kept", "inverse_step", "inverse_kept"))
        s_g, s_gsb, s_u, s_usb, s_sn, s_state, s_y, s_ysb = (sig(n, NCH) for n in (
            "chunk_g", "chunk_g_kept", "chunk_u", "chunk_u_kept", "state_gain", "state", "chunk_y", "chunk_y_kept"))
        s_mean, s_yc, s_ycsq, s_gvar, s_gstd, s_yg, s_out, s_outsb = (sig(n, 1) for n in (
            "y_mean", "y_centred", "y_squared", "y_var", "y_std", "y_gated", "s_out", "s_out_kept"))
        s_store = sig("s_stored", 1, 32)
        front_step, back_step, tail_step = sig("dve_front_step", 21), sig("dve_back_step", 5), sig("dve_tail_step", 3)
        s_base = sig("transposed_base", 2)
        s_init, s_passed = sig("init", 1), sig("passed", 1).sem
        SLOTS = 3 + 2 * (LEVELS - 1) + 3 * NCH

        block = ctx.enter_context(nc.Block())

        @block.sync
        def _(sp):
            for n, tile in list(w_in.items()):
                sp.dma_start(tile[:, :, :], io[n]).then_inc(s_w.sem, 16)
            for n, tile in list(w_up.items()):
                sp.dma_start(tile[:, :], io[n]).then_inc(s_w.sem, 16)
            s_store.open(sp)

            def load_x(t):
                for b in range(B):
                    sp.dma_start(x_tok[:, b, :], io["x"][b, bass.ds((t + 1) * TT, TT), :]).then_inc(s_x.sem, 16)

            def store_parts(t):
                for i, n in enumerate("qk"):
                    sp.wait_ge(s_cut.sem, s_cut.at(t, i + 1))
                    sp.sem_inc(s_passed, 1)
                    for k in range(3):
                        for h in range(HALVES):
                            for b in range(B):
                                sp.dma_start(io[n + "_dram"][k, b, 128 * h:128 * h + 128, bass.ds((t + 1) * TT, TT)],
                                             part[n][:, k, h, TT * b:TT * b + TT]).then_inc(s_parts.sem, 16)

            def store_s(t):
                sp.wait_ge(s_outsb.sem, s_outsb.at(t, 1))
                sp.sem_inc(s_passed, 1)
                for b in range(B):
                    sp.dma_start(io["s_dram"][b, bass.ds(t * TT, TT), :], s_tok[:, b, :]).then_inc(s_store.sem, 16)

            def next_x(t):
                sp.wait_ge(s_xn.sem, s_xn.at(t, 1))
                sp.sem_inc(s_passed, 1)
                load_x(t + 1)

            load_x(-1)
            next_x(-1)
            store_parts(-1)
            next_x(0)
            store_parts(0)
            with sp.Fori(1, NT - 2) as t:
                store_s(t - 1)
                next_x(t)
                store_parts(t)
            store_s(NT - 3)
            store_parts(NT - 2)
            store_s(NT - 2)
            store_s(NT - 1)
            sp.wait_ge(s_store.sem, s_store.at(NT - 1, 1))
            sp.wait_ge(s_parts.sem, s_parts.at(NT - 2, 1))

        @block.tensor
        def _(pe):
            back_signals, tail_signals = (s_am, s_z, s_inv, s_g, s_u, s_sn, s_y), (s_mean, s_gvar, s_out)
            for q in back_signals + tail_signals:
                q.open(pe)
            pe.wait_ge(s_const, keep["n_const"])
            pe.wait_ge(s_w.sem, 16 * NWT)
            mm = nc.tensor.matmul

            def front(t):
                def free(name):
                    n = job_no[name] - F
                    if n >= 0:
                        who, i = taken[JOBS[n][0]]
                        pe.wait_ge(took[who].sem, took[who].at(t, i))
                    elif t is not FIRST:
                        n = max(m for m in range(NJ) if m % F == job_no[name] % F)
                        who, i = taken[JOBS[n][0]]
                        pe.wait_ge(took[who].sem, took[who].at(t, i, back=1))

                def project(name, weights, src, m=128):
                    free(name)
                    outs = weights[0].shape[1] // m
                    for o in range(outs):
                        for i, (wt, x) in enumerate(zip(weights, src)):
                            last = mm(ps[0:m, job_no[name] % F, COLS * o:COLS * o + COLS], wt[:, m * o:m * o + m], x,
                                      start=(i == 0), stop=(i == len(src) - 1))
                    last.then_inc(s_job.sem, s_job.up())

                def per_half(name, ones, src):
                    free(name)
                    for h in range(2):
                        last = mm(ps[:, job_no[name] % F, COLS * h:COLS * h + COLS], ones, src[:, h, :], start=True, stop=True)
                    last.then_inc(s_job.sem, s_job.up())

                two = lambda a: [a[:, i, :] for i in range(2)]
                yield 0
                yield 1
                pe.wait_ge(s_xn.sem, s_xn.at(t, 1))
                free("tr")
                for h in range(HALVES):
                    for b in range(B):
                        last = nc.tensor.transpose(ps[:, job_no["tr"] % F, COLS * h + TT * b:COLS * h + TT * b + TT],
                                                   xn_tok[:, b, 128 * h:128 * h + 128], ident)
                last.then_inc(s_job.sem, s_job.up())
                yield 2
                pe.wait_ge(s_mix.sem, s_mix.at(t, 1))
                project("g1", two(w_in["g1"]), two(mixed["g"]))
                pe.wait_ge(s_mix.sem, s_mix.at(t, 2))
                project("w1", two(w_in["w1"]), two(mixed["w"]), 64)
                yield 3
                pe.wait_ge(s_mix.sem, s_mix.at(t, 3))
                project("a1", two(w_in["a1"]), two(mixed["a"]), 64)
                pe.wait_ge(s_mix.sem, s_mix.at(t, 4))
                project("k", two(w_in["W_k"]), two(mixed["k"]))
                yield 4
                pe.wait_ge(s_xsq.sem, s_xsq.at(t, 1))
                free("ms")
                for h in range(2):
                    last = mm(bank("ms", wide=COLS), const("ones128"), xsq[:, h, :], start=(h == 0), stop=(h == 1))
                last.then_inc(s_job.sem, s_job.up())
                pe.wait_ge(took["A"].sem, took["A"].at(t, taken["w1"][1]))
                project("w2", [w_up["w2"]], [tw[:, :]])
                yield 5
                pe.wait_ge(took["V"].sem, took["V"].at(t, taken["a1"][1]))
                project("a2", [w_up["a2"]], [ta[:, :]])
                pe.wait_ge(s_mix.sem, s_mix.at(t, 5))
                project("r", two(w_in["W_r"]), two(mixed["r"]))
                yield 6
                pe.wait_ge(s_mix.sem, s_mix.at(t, 6))
                project("v", two(w_in["W_v"]), two(mixed["v"]))
                pe.wait_ge(s_sq.sem, s_sq.at(t, 1))
                per_half("n", ones64, sq)
                yield 7
                pe.wait_ge(s_h.sem, s_h.at(t, 1))
                project("aq", two(w_in["wq"]), two(hT))
                yield 8
                project("ak", two(w_in["wk"]), two(hT))
                yield 9
                free("av")
                for b in range(B):
                    for k in range(2):
                        last = mm(ps[:, job_no["av"] % F, C * b:C * b + C], hT[:, k, TT * b:TT * b + TT],
                                  w_in["wv"][:, k, :], start=(k == 0), stop=(k == 1))
                last.then_inc(s_job.sem, s_job.up())
                yield 10
                pe.wait_ge(s_hsq.sem, s_hsq.at(t, 1))
                per_half("qs", const("ones16"), hsq["q"])
                yield 11
                pe.wait_ge(s_hsq.sem, s_hsq.at(t, 2))
                per_half("ks", const("ones16"), hsq["k"])
                for k in range(12, 16):
                    yield k
                free("vst")
                w_v = w_in["W_v"][:, :, :].rearrange("p k (g j d) -> p k g j d", j=2, d=64)
                for cb in range(CB):
                    for i in range(2):
                        for j in range(2):
                            last = mm(ps[64 * j:64 * j + 64, job_no["vst"] % F, 128 * cb:128 * cb + 128],
                                      mixed["v"][:, i, 64 * cb:64 * cb + 64], w_v[:, i, :, j, :],
                                      start=(i == 0), stop=(i == 1))
                last.then_inc(s_job.sem, s_job.up())
                yield 16
                yield 17
                project("g2", [w_up["g2"]], [tg[:, :]])
                pe.wait_ge(s_rk.sem, s_rk.at(t, 1))
                per_half("b", ones64, rk)
                yield 18
                s_job.whole()
                s_job.restart()

            def apart():
                pe.sem_inc(s_passed, 1)

            def back(t, give_way):
                give_way()
                pe.wait_ge(s_feat.sem, s_feat.at(t, 0))
                for p in range(PAIRS):
                    cb, g = divmod(p, 2)
                    if p >= 3:
                        pe.wait_ge(s_amsb.sem, s_amsb.at(t, p - 2))
                    elif p == 2:
                        pe.wait_ge(s_state.sem, s_state.at(t, NCH, back=1))
                    apart()
                    for lo, n, left, right in ((0, 192, bT[:, g, cb, :], ari[:, g, cb, :, :].rearrange("p a c -> p (a c)")),
                                               (192, 192, kT[:, g, cb, :], ari[:, g, cb, :, :].rearrange("p a c -> p (a c)")),
                                               (384, 64, ari[:, g, cb, 0, :], bT[:, g, cb, :])):
                        for j in range(2):
                            q = slice(64 * j, 64 * j + 64)
                            last = mm(ps[q, 4 + p % 3, lo:lo + n], left[q], right[q], start=True, stop=True)
                    last.then_inc(s_am.sem, s_am.up())
                    if p == 3:
                        give_way()
                give_way()

                def pairwise(bk, left, right):
                    apart()
                    for p in range(PAIRS):
                        for j in range(2):
                            q = slice(64 * j, 64 * j + 64)
                            last = mm(ps[q, bk, 64 * p:64 * p + 64], left[q, p, :], right[q, p, :], start=True, stop=True)
                    return last

                for lev in range(LEVELS - 1):
                    if lev:
                        pe.wait_ge(s_invsb.sem, s_invsb.at(t, lev))
                    pe.wait_ge(s_lj.sem, s_lj.at(t, lev + 2))
                    pairwise(4, lj[lev % 2], inv).then_inc(s_z.sem, s_z.up())
                    give_way()
                    pe.wait_ge(s_zsb.sem, s_zsb.at(t, lev + 1))
                    if lev == 0:
                        pe.wait_ge(s_base.sem, s_base.at(t, 2))
                    if lev < LEVELS - 2:
                        pairwise(5, invT, zz)
                    pairwise(6, zz, invT).then_inc(s_inv.sem, s_inv.up())
                    give_way()

                pe.wait_ge(s_vst.sem, s_vst.at(t, 0))
                pe.wait_ge(s_invsb.sem, s_invsb.at(t, LEVELS - 1))
                for c in range(NCH):
                    units = [(b, g, (b * NCH + c) * 2 + g, b * NCH + c) for b in range(B) for g in range(2)]

                    def into(bk, left, right, first):
                        last = None
                        apart()
                        for n, (b, g, p, cb) in enumerate(units):
                            for j in range(2):
                                q = slice(64 * j, 64 * j + 64)
                                o = 64 * (2 * b + g)
                                last = mm(ps[q, bk, o:o + 64], left(q, b, g, p, cb), right(q, b, g, p, cb),
                                          start=(first and n == 0), stop=True, skip_group_check=True)
                        return last

                    a_t = lambda q, b, g, p, cb: ari[q, g, cb, 0, :]
                    r_t = lambda q, b, g, p, cb: ari[q, g, cb, 1, :]
                    st = lambda q, b, g, p, cb: state[q, b, g, :]
                    vv = lambda q, b, g, p, cb: v_st[q, cb, g, :]
                    gg = lambda q, b, g, p, cb: g_sb[q, b, g, :]
                    uu = lambda q, b, g, p, cb: u_sb[q, b, g, :]
                    prod = lambda k: (lambda q, b, g, p, cb: am[q, p, k, :])
                    into(4, prod(3), vv, True)
                    pe.wait_ge(s_state.sem, s_state.at(t, c) if c else s_state.at(t, NCH, back=1))
                    into(4, a_t, st, False).then_inc(s_g.sem, s_g.up())
                    if c:
                        pe.wait_ge(s_ysb.sem, s_ysb.at(t, c))
                    else:
                        pe.wait_ge(s_outsb.sem, s_outsb.at(t, 0))
                    into(7, st, r_t, True)
                    into(7, vv, prod(4), False)
                    into(6, prod(5), vv, True)
                    give_way()
                    pe.wait_ge(s_gsb.sem, s_gsb.at(t, c + 1))
                    into(5, lambda q, b, g, p, cb: invT[q, p, :], gg, True).then_inc(s_u.sem, s_u.up())
                    give_way()
                    pe.wait_ge(s_usb.sem, s_usb.at(t, c + 1))
                    into(6, prod(2), uu, False).then_inc(s_sn.sem, s_sn.up())
                    into(7, uu, prod(1), False).then_inc(s_y.sem, s_y.up())
                    give_way()

                for q in back_signals:
                    q.restart()

            def tail(t):
                pe.wait_ge(s_ysb.sem, s_ysb.at(t, NCH))
                for h in range(2):
                    last = mm(ps[:, 7, COLS * h:COLS * h + COLS], ones64, yT[:, h, :], start=True, stop=True)
                last.then_inc(s_mean.sem, s_mean.up())
                yield 0
                pe.wait_ge(s_ycsq.sem, s_ycsq.at(t, 1))
                for h in range(2):
                    last = mm(ps[:, 7, COLS * h:COLS * h + COLS], ones64, ysq[:, h, :], start=True, stop=True)
                last.then_inc(s_gvar.sem, s_gvar.up())
                for k in range(1, 6):
                    yield k
                pe.wait_ge(s_yg.sem, s_yg.at(t, 1))
                for b in range(B):
                    for h in range(2):
                        last = mm(ps[:, 7, C * b:C * b + C], yg[:, h, TT * b:TT * b + TT], w_in["W_o"][:, h, :],
                                  start=(h == 0), stop=(h == 1))
                last.then_inc(s_out.sem, s_out.up())
                yield 6
                for q in tail_signals:
                    q.restart()

            all_strands(pe, front, back, tail)

        @block.scalar
        def _(act):
            back_signals, tail_signals = (s_zsb, s_gsb, s_usb, s_ysb), (s_ycsq, s_gstd, s_outsb)
            for q in back_signals + tail_signals:
                q.open(act)
            act.wait_ge(s_const, keep["n_const"])
            f = nc.scalar.activation
            eps_ln, eps_gn, eps_rms, eps_rms16 = (const("eps", i, i + 1) for i in range(4))

            def front(t):
                def ready(name):
                    act.wait_ge(s_job.sem, s_job.at(t, job_no[name] + 1))

                act.wait_ge(s_var.sem, s_var.at(t, 1))
                f(std[:, :], mv[:, :, 1], ACT.Sqrt, bias=eps_ln, scale=1.0).then_inc(s_std.sem, 1)
                yield 0
                yield 1
                ready("tr")
                nc.scalar.copy(xn_all[:, :, :, bass.ds((t + 1) * TT + 1, TT)],
                               bank("tr").rearrange("p (h b t) -> p h b t", h=HALVES, b=B)
                               ).then_inc(took["A"].sem, took["A"].up())
                act.wait_ge(took["A"].sem, took["A"].at(t, 1))
                if t is not FIRST:
                    act.wait_ge(took["A"].sem, took["A"].at(t, taken["ms"][1], back=1))
                act.sem_inc(s_passed, 1)
                f(xsq[:, :, :].rearrange("p h (b t) -> p h b t", b=B), xn_all[:, :, :, bass.ds((t + 1) * TT + 1, TT)],
                  ACT.Square).then_inc(s_xsq.sem, 1)
                yield 2
                ready("g1")
                f(tg[:, :], bank("g1", wide=COLS), ACT.Sigmoid).then_inc(took["A"].sem, took["A"].up())
                ready("w1")
                f(tw[:, :], bank("w1", 64, COLS), ACT.Tanh).then_inc(took["A"].sem, took["A"].up())
                yield 3
                yield 4
                ready("ms")
                f(rms[:, :], bank("ms", wide=COLS), ACT.Sqrt, bias=eps_rms, scale=1.0 / C
                  ).then_inc(took["A"].sem, took["A"].up())
                ready("w2")
                f(sg[:, 0, :], halves(bank("w2"))[:, 0, :], ACT.Sigmoid, bias=v("w0", 0), scale=1.0)
                f(sg[:, 1, :], halves(bank("w2"))[:, 1, :], ACT.Sigmoid, bias=v("w0", 1), scale=1.0
                  ).then_inc(took["A"].sem, took["A"].up())
                yield 5
                ready("a2")
                f(av[:, 0, :], halves(bank("a2"))[:, 0, :], ACT.Sigmoid, bias=v("a0", 0), scale=1.0)
                f(av[:, 1, :], halves(bank("a2"))[:, 1, :], ACT.Sigmoid, bias=v("a0", 1), scale=1.0
                  ).then_inc(took["A"].sem, took["A"].up())
                act.wait_ge(s_kk.sem, s_kk.at(t, 1))
                f(sq[:, :, :], kk[:, :, :], ACT.Square).then_inc(s_sq.sem, 1)
                ready("r")
                f(rT[:, :, :], halves(bank("r")), ACT.Copy).then_inc(took["A"].sem, took["A"].up())
                yield 6
                ready("v")
                f(vT[:, :, :], halves(bank("v")), ACT.Copy).then_inc(took["A"].sem, took["A"].up())
                ready("n")
                f(nrm[:, :, :], halves(bank("n")), ACT.Sqrt).then_inc(took["A"].sem, took["A"].up())
                yield 7
                act.wait_ge(s_cs.sem, s_cs.at(t, 1))
                f(p_now[:, :, :], cs[:, :, :], ACT.Exp, scale=-NEG_DECAY)
                f(p_inv[:, :, :], cs[:, :, :], ACT.Exp, scale=NEG_DECAY)
                f(p_prev[:, :, :], csp[:, :, :], ACT.Exp, scale=-NEG_DECAY).then_inc(s_exp.sem, 1)
                yield 8
                for i, n in enumerate("qk"):
                    ready("a" + n)
                    f(hsq[n][:, :, :], halves(bank("a" + n)), ACT.Square).then_inc(s_hsq.sem, 1)
                    f(raw[n][:, :, :], halves(bank("a" + n)), ACT.Copy).then_inc(took["A"].sem, took["A"].up())
                    if n == "q":
                        yield 9
                ready("av")
                nc.scalar.copy(v_all[:, :, bass.ds(t + 1, 1), :].rearrange("p b o c -> p (b o) c"),
                               bank("av").rearrange("p (b c) -> p b c", b=B)).then_inc(took["A"].sem, took["A"].up())
                yield 10
                ready("qs")
                f(hsq["q"][:, :, :], halves(bank("qs")), ACT.Sqrt, bias=eps_rms16, scale=1.0
                  ).then_inc(took["A"].sem, took["A"].up())
                yield 11
                ready("ks")
                f(hsq["k"][:, :, :], halves(bank("ks")), ACT.Sqrt, bias=eps_rms, scale=1.0 / AD
                  ).then_inc(took["A"].sem, took["A"].up())
                for k in range(12, 18):
                    yield k
                if t is not FIRST:
                    act.wait_ge(s_y.sem, s_y.at(t, NCH))
                act.wait_ge(s_adec.sem, s_adec.at(t, 1))
                for h in range(2):
                    f(ari[:, h, :, 0, :], kk[:, h, :].rearrange("p (c t) -> p c t", c=CB), ACT.Copy)
                    last = f(ari[:, h, :, 1, :], rdec[:, h, :].rearrange("p (c t) -> p c t", c=CB), ACT.Copy)
                last.then_inc(s_feat.sem, 1)
                yield 18
                took["A"].whole()
                took["A"].restart()

            def back(t, give_way):
                give_way()
                give_way()
                give_way()
                for lev in range(LEVELS - 1):
                    act.wait_ge(s_z.sem, s_z.at(t, lev + 1))
                    f(zz[:, :, :].rearrange("p a c -> p (a c)"), ps[:, 4, :], ACT.Copy).then_inc(s_zsb.sem, s_zsb.up())
                    give_way()
                    give_way()
                for c in range(NCH):
                    fl = lambda a: a[:, :, :, :].rearrange("p b g v -> p (b g v)")
                    act.wait_ge(s_g.sem, s_g.at(t, c + 1))
                    nc.scalar.copy(fl(g_sb), ps[:, 4, 0:256]).then_inc(s_gsb.sem, s_gsb.up())
                    give_way()
                    act.wait_ge(s_u.sem, s_u.at(t, c + 1))
                    nc.scalar.copy(fl(u_sb), ps[:, 5, 0:256]).then_inc(s_usb.sem, s_usb.up())
                    give_way()
                    act.wait_ge(s_y.sem, s_y.at(t, c + 1))
                    nc.scalar.copy(yT[:, :, :].rearrange("p h (b t) -> p h b t", b=B)[:, :, :, 64 * c:64 * c + 64],
                                   ps[:, 7, 0:256].rearrange("p (b g v) -> p g b v", b=2, g=2)
                                   ).then_inc(s_ysb.sem, s_ysb.up())
                    give_way()
                for q in back_signals:
                    q.restart()

            def tail(t):
                act.wait_ge(s_yc.sem, s_yc.at(t, 1))
                f(ysq[:, :, :], yc[:, :, :], ACT.Square).then_inc(s_ycsq.sem, s_ycsq.up())
                yield 0
                act.wait_ge(s_gvar.sem, s_gvar.at(t, 1))
                f(ystd[:, :, :], halves(ps[:, 7, :]), ACT.Sqrt, bias=eps_gn, scale=1.0 / RD).then_inc(s_gstd.sem, s_gstd.up())
                for k in range(1, 6):
                    yield k
                act.wait_ge(s_out.sem, s_out.at(t, 1))
                act.wait_ge(s_store.sem, s_store.at(t, 1, back=1))
                f(s_tok[:, :, :], ps[:, 7, :].rearrange("p (b c) -> p b c", b=B), ACT.Copy).then_inc(s_outsb.sem, s_outsb.up())
                yield 6
                for q in tail_signals:
                    q.restart()

            all_strands(act, front, back, tail)

        @block.vector
        def _(dve):
            back_signals = (s_amsb, s_base, s_lj, s_invsb, s_state, back_step)
            tail_signals = (s_yc, s_yg, tail_step)
            for q in back_signals + tail_signals:
                q.open(dve)
            dve.wait_ge(s_const, keep["n_const"])
            ve = nc.vector
            ve.memset(state[:, :, :, :], 0.0)
            ve.memset(xn_all[:, :, :, 0:1], 0.0)
            for g in range(2):
                last = ve.tensor_copy(ari[:, g, :, 2, :], const("eye64").unsqueeze(1).to_broadcast([128, CB, 64]))
            last.then_inc(s_init.sem, 1)
            dve.wait_ge(s_init.sem, 1)

            def cut(ap):
                return ap.rearrange("p (c t) -> p c t", c=CB)

            def front(t):
                def ready(name):
                    dve.wait_ge(s_job.sem, s_job.at(t, job_no[name] + 1))

                def mix(n):
                    for h in range(2):
                        last = ve.scalar_tensor_tensor(by_batch(mixed[n][:, h, :]), by_batch(dx[:, h, :]), v("x_" + n, h),
                                                       xn_all[:, h, :, bass.ds((t + 1) * TT + 1, TT)], ALU.mult, ALU.add)
                    last.then_inc(s_mix.sem, s_mix.up())

                dve.wait_ge(s_x.sem, s_x.at(t, 1))
                for b in range(B):
                    last = ve.bn_stats(bn6[:, b, :], x_tok[:, b, :])
                last.then_inc(front_step.sem, front_step.up())
                dve.wait_ge(front_step.sem, front_step.at(t))
                dve.sem_inc(s_passed, 1)
                for b in range(B):
                    last = ve.bn_aggr(mv[:, b, :], bn6[:, b, :])
                last.then_inc(s_var.sem, 1)
                yield 0
                dve.wait_ge(s_std.sem, s_std.at(t, 1))
                ve.reciprocal(rstd[:, :], std[:, :]).then_inc(front_step.sem, front_step.up())
                dve.wait_ge(front_step.sem, front_step.at(t))
                for b in range(B):
                    last = ve.tensor_scalar(xn_tok[:, b, :], x_tok[:, b, :], mv[:, b, 0:1], rstd[:, b:b + 1],
                                            ALU.subtract, ALU.mult)
                last.then_inc(s_xn.sem, 1)
                yield 1
                dve.wait_ge(took["A"].sem, took["A"].at(t, 1))
                ve.tensor_tensor(dx[:, :, :].rearrange("p h (b t) -> p h b t", b=B),
                                 xn_all[:, :, :, bass.ds((t + 1) * TT, TT)],
                                 xn_all[:, :, :, bass.ds((t + 1) * TT + 1, TT)], ALU.subtract
                                 ).then_inc(front_step.sem, front_step.up())
                dve.wait_ge(front_step.sem, front_step.at(t))
                mix("g")
                mix("w")
                yield 2
                mix("a")
                mix("k")
                yield 3
                mix("r")
                mix("v")
                ready("a1")
                ve.tensor_copy(ta[:, :], bank("a1", 64, COLS)).then_inc(took["V"].sem, took["V"].up())
                ready("k")
                ve.tensor_copy(kraw[:, :, :], halves(bank("k"))).then_inc(took["V"].sem, took["V"].up())
                dve.wait_ge(took["V"].sem, took["V"].at(t))
                yield 4
                for h in range(2):
                    last = ve.tensor_scalar(kk[:, h, :], kraw[:, h, :], v("k_k", h), None, ALU.mult)
                last.then_inc(s_kk.sem, 1)
                dve.wait_ge(took["A"].sem, took["A"].at(t, taken["ms"][1]))
                ve.reciprocal(rms[:, :], rms[:, :]).then_inc(front_step.sem, front_step.up())
                dve.wait_ge(front_step.sem, front_step.at(t))
                for h in range(2):
                    last = ve.scalar_tensor_tensor(by_batch(hT[:, h, :]), xn_all[:, h, :, bass.ds((t + 1) * TT + 1, TT)],
                                                   v("n1_w", h), by_batch(rms[:, :]), ALU.mult, ALU.mult)
                last.then_inc(s_h.sem, 1)
                yield 5
                dve.wait_ge(took["A"].sem, took["A"].at(t, taken["w2"][1]))
                for h in range(2):
                    last = ve.tensor_tensor_scan(cs[:, h, :], const("reset"), sg[:, h, :], 0.0, ALU.mult, ALU.add)
                last.then_inc(front_step.sem, front_step.up())
                dve.wait_ge(front_step.sem, front_step.at(t))
                ve.tensor_tensor(csp[:, :, :], cs[:, :, :], sg[:, :, :], ALU.subtract).then_inc(s_cs.sem, 1)
                yield 6
                dve.wait_ge(took["A"].sem, took["A"].at(t, taken["a2"][1]))
                for h in range(2):
                    last = ve.tensor_scalar(kmod[:, h, :], av[:, h, :], 1.0, v("k_a", h), ALU.subtract, ALU.mult)
                last.then_inc(front_step.sem, front_step.up())
                dve.wait_ge(front_step.sem, front_step.at(t))
                ve.scalar_tensor_tensor(kmod[:, :, :], kmod[:, :, :], 1.0, kraw[:, :, :], ALU.add, ALU.mult
                                        ).then_inc(front_step.sem, front_step.up())
                dve.wait_ge(front_step.sem, front_step.at(t))
                yield 7
                dve.wait_ge(took["A"].sem, took["A"].at(t, taken["r"][1]))
                for h in range(2):
                    last = ve.scalar_tensor_tensor(rk[:, h, :], rT[:, h, :], v("r_k", h), kmod[:, h, :], ALU.mult, ALU.mult)
                last.then_inc(s_rk.sem, 1)
                dve.wait_ge(took["A"].sem, took["A"].at(t, taken["n"][1]))
                ve.tensor_scalar(nrm[:, :, :], nrm[:, :, :], 1e-12, None, ALU.max).then_inc(front_step.sem, front_step.up())
                dve.wait_ge(front_step.sem, front_step.at(t))
                ve.reciprocal(nrm[:, 0, :], nrm[:, 0, :])
                yield 8
                ve.reciprocal(nrm[:, 1, :], nrm[:, 1, :]).then_inc(front_step.sem, front_step.up())
                dve.wait_ge(front_step.sem, front_step.at(t))
                ve.tensor_tensor(kk[:, :, :], kk[:, :, :], nrm[:, :, :], ALU.mult).then_inc(front_step.sem, front_step.up())
                dve.wait_ge(front_step.sem, front_step.at(t))
                ve.tensor_tensor(av[:, :, :], kk[:, :, :], av[:, :, :], ALU.mult).then_inc(front_step.sem, front_step.up())
                dve.wait_ge(front_step.sem, front_step.at(t))
                yield 9
                dve.wait_ge(s_exp.sem, s_exp.at(t, 1))
                for h in range(2):
                    ve.tensor_tensor(bT[:, h, :, :], cut(av[:, h, :]), cut(p_inv[:, h, :]), ALU.mult)
                    ve.tensor_tensor(kT[:, h, :, :], cut(kmod[:, h, :]), cut(p_inv[:, h, :]), ALU.mult)
                yield 10
                for h in range(2):
                    ve.scalar_tensor_tensor(kk[:, h, :], kk[:, h, :], -1.0, p_prev[:, h, :], ALU.mult, ALU.mult)
                    last = ve.tensor_tensor(rdec[:, h, :], rT[:, h, :], p_now[:, h, :], ALU.mult)
                last.then_inc(s_adec.sem, 1)
                yield 11
                for i, n in enumerate("qk"):
                    hi, mid, lo = (part[n][:, k, :, :] for k in range(3))
                    dve.wait_ge(took["A"].sem, took["A"].at(t, taken[n + "s"][1]))
                    ve.reciprocal(hsq[n][:, :, :], hsq[n][:, :, :]).then_inc(front_step.sem, front_step.up())
                    dve.wait_ge(front_step.sem, front_step.at(t))
                    for h in range(2):
                        last = ve.scalar_tensor_tensor(raw[n][:, h, :], raw[n][:, h, :], v(n + "n_w", h), hsq[n][:, h, :],
                                                       ALU.mult, ALU.mult)
                    last.then_inc(front_step.sem, front_step.up())
                    dve.wait_ge(front_step.sem, front_step.at(t))
                    yield 12 + 3 * i
                    if t is not FIRST:
                        dve.wait_ge(s_parts.sem, s_parts.at(t, 1, back=1))
                    ve.tensor_copy(hi, raw[n][:, :, :]).then_inc(front_step.sem, front_step.up())
                    dve.wait_ge(front_step.sem, front_step.at(t))
                    ve.tensor_tensor(raw[n][:, :, :], raw[n][:, :, :], hi, ALU.subtract
                                     ).then_inc(front_step.sem, front_step.up())
                    dve.wait_ge(front_step.sem, front_step.at(t))
                    yield 13 + 3 * i
                    ve.tensor_copy(mid, raw[n][:, :, :]).then_inc(front_step.sem, front_step.up())
                    dve.wait_ge(front_step.sem, front_step.at(t))
                    ve.tensor_tensor(lo, raw[n][:, :, :], mid, ALU.subtract).then_inc(s_cut.sem, 1)
                    yield 14 + 3 * i
                if t is not FIRST:
                    dve.wait_ge(s_y.sem, s_y.at(t, NCH))
                ends = p_now[:, :, :].rearrange("p h (b c t) -> p c b h t", b=B, c=NCH)
                for c in range(NCH):
                    ve.tensor_copy(p_end[:, c, :, :], ends[:, c, :, :, CH - 1])
                ready("vst")
                ve.tensor_copy(v_st[:, :, :, :].rearrange("p a g d -> p (a g d)"), bank("vst")
                               ).then_inc(took["V"].sem, took["V"].up())
                dve.sem_inc(s_vst.sem, 1)
                ready("g2")
                ve.tensor_copy(gT[:, :, :], halves(bank("g2"))).then_inc(took["V"].sem, took["V"].up())
                ready("b")
                ve.tensor_tensor(bonus[:, :, :], halves(bank("b")), vT[:, :, :], ALU.mult
                                 ).then_inc(took["V"].sem, took["V"].up())
                dve.wait_ge(took["V"].sem, took["V"].at(t))
                yield 18
                front_step.whole()
                for q in (s_mix, took["V"], front_step):
                    q.restart()

            def back(t, give_way):
                flat = lambda a: a[:, :, :].rearrange("p a c -> p (a c)")
                wide = lambda name, lo=0, hi=64, n=PAIRS: const(name, lo, hi).unsqueeze(1).to_broadcast([128, n, 64])

                def base(p):
                    n = PAIRS // 2
                    dve.wait_ge(s_amsb.sem, s_amsb.at(t))
                    ve.tensor_tensor(inv[:, p, :], am[:, p, 6, :], wide("low0", n=n), ALU.mult)
                    ve.tensor_tensor(invT[:, p, :], am[:, p, 0, :], wide("low0t", n=n), ALU.mult
                                     ).then_inc(back_step.sem, back_step.up())
                    ve.tensor_tensor(lj[0][:, p, :], am[:, p, 0, :], wide("lev", 0, 64, n), ALU.mult)
                    dve.wait_ge(back_step.sem, back_step.at(t))
                    ve.tensor_tensor(inv[:, p, :], inv[:, p, :], wide("eye64", n=n), ALU.add).then_inc(s_lj.sem, s_lj.up())
                    ve.tensor_tensor(invT[:, p, :], invT[:, p, :], wide("eye64", n=n), ALU.add
                                     ).then_inc(s_base.sem, s_base.up())

                give_way()
                for p in range(PAIRS):
                    dve.wait_ge(s_am.sem, s_am.at(t, p + 1))
                    ve.tensor_tensor(am[:, p, :, :].rearrange("p a c -> p (a c)"), ps[:, 4 + p % 3, 0:448],
                                     const("amask"), ALU.mult).then_inc(s_amsb.sem, s_amsb.up())
                    if p == PAIRS // 2 - 1:
                        base(slice(0, PAIRS // 2))
                        give_way()
                base(slice(PAIRS // 2, PAIRS))
                dve.wait_ge(s_base.sem, s_base.at(t))
                give_way()
                for lev in range(LEVELS - 1):
                    if lev < LEVELS - 2:
                        ve.tensor_tensor(lj[(lev + 1) % 2][:, :, :], am[:, :, 0, :], wide("lev", 64 * lev + 64, 64 * lev + 128),
                                         ALU.mult).then_inc(s_lj.sem, s_lj.up())
                    give_way()
                    dve.wait_ge(s_inv.sem, s_inv.at(t, lev + 1))
                    if lev < LEVELS - 2:
                        ve.tensor_tensor(flat(inv), flat(inv), ps[:, 5, :], ALU.add)
                    ve.tensor_tensor(flat(invT), flat(invT), ps[:, 6, :], ALU.add).then_inc(s_invsb.sem, s_invsb.up())
                    dve.wait_ge(s_invsb.sem, s_invsb.at(t))
                    if lev == 2:
                        for h in range(2):
                            ve.tensor_scalar(gain[:, h, :], gT[:, h, :], v("ln_w", h), None, ALU.mult)
                            last = ve.scalar_tensor_tensor(shift[:, h, :], bonus[:, h, :], v("ln_b", h), gT[:, h, :],
                                                           ALU.add, ALU.mult)
                        last.then_inc(back_step.sem, back_step.up())
                        dve.wait_ge(back_step.sem, back_step.at(t))
                    give_way()
                for c in range(NCH):
                    fl = lambda a: a[:, :, :, :].rearrange("p b g v -> p (b g v)")
                    give_way()
                    give_way()
                    dve.wait_ge(s_sn.sem, s_sn.at(t, c + 1))
                    ve.tensor_tensor(fl(stmp), fl(state), ps[:, 6, 0:256], ALU.add).then_inc(back_step.sem, back_step.up())
                    dve.wait_ge(back_step.sem, back_step.at(t))
                    ve.tensor_tensor(state[:, :, :, :], stmp[:, :, :, :],
                                     p_end[:, c, :, :].unsqueeze(3).to_broadcast([128, B, 2, 64]), ALU.mult
                                     ).then_inc(s_state.sem, s_state.up())
                    dve.wait_ge(s_state.sem, s_state.at(t))
                    give_way()
                back_step.whole()
                for q in back_signals:
                    q.restart()

            def tail(t):
                dve.wait_ge(s_mean.sem, s_mean.at(t, 1))
                ve.scalar_tensor_tensor(yc[:, :, :].rearrange("p h c -> p (h c)"), ps[:, 7, :], -1.0 / RD, yT[:, :, :].rearrange("p h c -> p (h c)"), ALU.mult, ALU.add
                                        ).then_inc(s_yc.sem, s_yc.up())
                dve.wait_ge(s_yc.sem, s_yc.at(t))
                for k in range(3):
                    yield k
                dve.wait_ge(s_gstd.sem, s_gstd.at(t, 1))
                ve.reciprocal(ystd[:, 0, :], ystd[:, 0, :])
                yield 3
                ve.reciprocal(ystd[:, 1, :], ystd[:, 1, :]).then_inc(tail_step.sem, tail_step.up())
                dve.wait_ge(tail_step.sem, tail_step.at(t))
                yield 4
                ve.tensor_tensor(yg[:, :, :], yc[:, :, :], ystd[:, :, :], ALU.mult).then_inc(tail_step.sem, tail_step.up())
                dve.wait_ge(tail_step.sem, tail_step.at(t))
                ve.tensor_tensor(yg[:, :, :], yg[:, :, :], gain[:, :, :], ALU.mult).then_inc(tail_step.sem, tail_step.up())
                dve.wait_ge(tail_step.sem, tail_step.at(t))
                ve.tensor_tensor(yg[:, :, :], yg[:, :, :], shift[:, :, :], ALU.add).then_inc(s_yg.sem, s_yg.up())
                dve.wait_ge(s_yg.sem, s_yg.at(t))
                yield 5
                yield 6
                tail_step.whole()
                for q in tail_signals:
                    q.restart()

            all_strands(dve, front, back, tail)


PARTS_Q, PARTS_K = (0, 0, 0, 1, 1, 2), (0, 1, 2, 0, 1, 0)
NP = 6 * AD
NROW = NP + 2
KTS, QC = T // 128, T // 512
UNTIL = 37


def attention_phase(nc, io, keep, signal):
    ctx = ExitStack()
    with ctx:
        def sb(name, shape, dt=FP32):
            return ctx.enter_context(nc.sbuf_tensor("a_" + name, shape, dt))

        def sig(name, per, unit=1):
            return signal("a_" + name, per, unit)

        cst, at, v_all = keep["cst"], keep["at"], keep["v_all"]
        const = lambda name, lo=0, hi=None: cst[:, at[name][0] + lo:(at[name][0] + hi if hi is not None else at[name][1])]
        cb16 = sb("masks", [128, 3, 128], BF16)
        qa = [sb(f"qa{b}", [NROW, 4, T], BF16) for b in range(B)]
        ka = [sb(f"ka{b}", [NROW, 4, T], BF16) for b in range(B)]
        v_st = [sb(f"v_st{b}", [128, KTS, 4, 32]) for b in range(B)]
        pt = [[sb(f"pt{x}{i}", [128, 2, 512]) for i in range(2)] for x in range(2)]
        o_sb = [sb(f"o_sb{b}", [128, T]) for b in range(B)]
        stage = [sb(f"stage{i}", [128, CUT]) for i in range(2)]
        s_raw = [sig(f"raw_weights{i}", 1, 16) for i in range(2)]
        s_whi, s_wlo, s_cut = sig("weights_hi", 1), sig("weights_lo", 1), sig("weights_cut", 1)
        mx = sb("mx", [128, 4, KTS, 4])
        m = sb("m", [128, 4 * KTS])
        mt, mrow = sb("mt", [4 * KTS, 128]), sb("mrow", [4 * KTS, 2, 128], BF16)
        sc = [ctx.enter_context(nc.psum_tensor(f"a_sc{x}", [128, 2, 512], FP32)) for x in range(2)]
        po = [ctx.enter_context(nc.psum_tensor(f"a_po{x}", [128, 512], FP32)) for x in range(2)]
        pm = [ctx.enter_context(nc.psum_tensor(f"a_pm{x}", [128, 512], FP32)) for x in range(2)]

        CHUNKS = list(range(QC))[::-1]
        STEPS = [(qc, j) for qc in CHUNKS for j in range(4 * qc + 4)]
        NS = len(STEPS)
        last_step = {qc: max(s for s, (c, _) in enumerate(STEPS) if c == qc) + 1 for qc in CHUNKS}
        UNITS = [(qt, kc, h) for kc in CHUNKS for qt in range(KTS)[::-1] if qt // 4 >= kc for h in range(4)]
        NU = len(UNITS)
        unit_width = [min(512, 128 * (qt + 1) - 512 * kc) for qt, kc, h in UNITS]
        step_width = [512 - max(0, 128 * (j - 4 * qc)) for qc, j in STEPS]

        def units_of(step):
            upto = [sum(step_width[:min(s, UNTIL)]) / sum(step_width[:UNTIL]) for s in (step, step + 1)]
            edge = [sum(sum(unit_width[:i + 1]) <= f * sum(unit_width) + 1e-6 for i in range(NU)) for f in upto]
            return list(range(*edge))

        s_passed = sig("passed", 1).sem
        s_load = [[sig(f"loaded{b}{c}", 1, 16 * 12) for c in range(QC)] for b in range(B)]
        s_vst = [sig(f"v_ready{b}", 1) for b in range(B)]
        s_ones, s_one = sig("ones", 1), sig("dve_ones", 1)
        s_sc = [sig(f"scores{x}", B * NS) for x in range(2)]
        s_p = [sig(f"weights{x}", B * NS) for x in range(2)]
        s_pv = sig("summed", B * NS)
        s_o = sig("out_kept", B * QC)
        s_max, s_red = sig("max_scores", B * NU), sig("max_found", B * NU)
        s_m, s_mt, s_mrow = sig("m", B), sig("m_transposed", B), sig("m_rows", B)
        s_mload = [sig(f"m_loaded{b}", 1, 16 * 2) for b in range(B)]
        s_ostore = [sig(f"o_stored{b}", 1, 16) for b in range(B)]
        dve_step = sig("dve_step", 2 * B)
        block = ctx.enter_context(nc.Block())

        def load(sp, b, hg, c):
            tok = slice(512 * c, 512 * c + 512)
            for tile, n, parts in ((qa[b], "q", PARTS_Q), (ka[b], "k", PARTS_K)):
                for r, k in enumerate(parts):
                    src = io[n + "_dram"][k, b, bass.ds(hg * 64, 64), tok]
                    sp.dma_start(tile[AD * r:AD * r + AD, :, tok], src.rearrange("(h d) t -> d h t", d=AD)
                                 ).then_inc(s_load[b][c].sem, 16)

        def load_rows(sp, b, turn):
            for k in range(2):
                sp.dma_start(qa[b][NP + k:NP + k + 1, :, :].rearrange("o h (q t) -> o (h q) t", t=128),
                             mrow[:, k, :]).then_inc(s_mload[b].sem, 16)

        @block.sync
        def _(sp):
            for b in range(B):
                s_mload[b].open(sp)
                s_ostore[b].open(sp)
            for b in range(B):
                for c in CHUNKS:
                    load(sp, b, 0, c)
            sp.wait_ge(s_mrow.sem, B)
            load_rows(sp, 0, 0)
            with sp.Fori(0, 4) as u:
                for b in range(B):
                    for c in CHUNKS:
                        if c == 0:
                            sp.wait_ge(s_mrow.sem, s_mrow.at(u, b + 1))
                            load_rows(sp, 1 - b, u)
                        sp.wait_ge(s_pv.sem, s_pv.at(u, b * NS + last_step[c]))
                        sp.sem_inc(s_passed, 1)
                        load(sp, b, (u + 1) % 4, c)
                    sp.wait_ge(s_o.sem, s_o.at(u, (b + 1) * QC))
                    sp.dma_start(io["o_dram"][b, bass.ds(u * 128, 128), :], o_sb[b][:, :]).then_inc(s_ostore[b].sem, 16)
            for b in range(B):
                sp.wait_ge(s_ostore[b].sem, s_ostore[b].at(3, 1))
            sp.wait_ge(s_mload[0].sem, 32 * 6)
            for b in range(B):
                for c in CHUNKS:
                    sp.wait_ge(s_load[b][c].sem, 192 * 5)

        @block.gpsimd
        def _(pool):
            for b in range(B):
                nc.gpsimd.memset(v_st[b][:, :, :, 16:32], 1.0).then_inc(s_ones.sem, 1)
                s_vst[b].open(pool)
            pool.wait_ge(s_ones.sem, B)
            pool.wait_ge(s_load[1][0].sem, 16 * 12)
            cut_weights(nc, pool, io, EARLY, keep["w_hi"], keep["w_lo"], stage, s_raw, s_whi, s_wlo, s_cut)
            with pool.Fori(0, 4) as u:
                for b in range(B):
                    pool.wait_ge(s_pv.sem, s_pv.at(u, NS * (b + 1), back=1))
                    nc.gpsimd.tensor_copy(
                        v_st[b][:, :, :, 0:16],
                        v_all[:, b, :, bass.ds(u * 64, 64)].rearrange("p k (h d) -> p k h d", h=4)).then_inc(s_vst[b].sem, s_vst[b].up())

        @block.tensor
        def _(pe):
            for q in (*s_sc, s_pv):
                q.open(pe)
            pe.wait_ge(s_ones.sem, B)
            pe.wait_ge(s_one.sem, 1)
            mm = nc.tensor.matmul
            ident16, neg_kq, neg_qk = (cb16[:, i, :] for i in range(3))

            def max_unit(b, i):
                qt, kc, h = UNITS[i]
                width = min(512, 128 * (qt + 1) - 512 * kc)
                diag = kc == qt // 4
                out = pm[i % 2]
                last = mm(out[:, 0:width], qa[b][0:NP, h, 128 * qt:128 * qt + 128],
                          ka[b][0:NP, h, 512 * kc:512 * kc + width], start=True, stop=not diag)
                if diag:
                    last = mm(out[:, width - 128:width], ident16, neg_qk, start=False, stop=True)
                return last

            pe.sem_inc(s_max.sem, NU)
            for i, (qt, kc, h) in enumerate(UNITS):
                if i == 0 or kc != UNITS[i - 1][1]:
                    pe.wait_ge(s_load[0][kc].sem, 16 * 12)
                if i >= 2:
                    pe.wait_ge(s_red.sem, NU + i - 1)
                max_unit(0, i).then_inc(s_max.sem, 1)
            pe.wait_ge(s_m.sem, B)
            nc.tensor.transpose(pm[0][0:4 * KTS, 0:128], m[:, :], const("ident")).then_inc(s_mt.sem, B)
            with pe.Fori(0, 4) as u:
                for b in range(B):
                    other = 1 - b

                    def scores(s, x, turn=u):
                        qc, j = STEPS[s]
                        off = max(0, 128 * (j - 4 * qc))
                        n = b * NS + s
                        if n:
                            pe.wait_ge(s_p[x].sem, s_p[x].at(u, n))
                        else:
                            pe.wait_ge(s_p[x].sem, s_p[x].at(u, B * NS, back=1))
                        for y in range(2):
                            h = 2 * x + y
                            diag = j >= 4 * qc
                            last = mm(sc[x][:, y, off:512], ka[b][:, h, 128 * j:128 * j + 128],
                                      qa[b][:, h, 512 * qc + off:512 * qc + 512], start=True, stop=not diag)
                            if diag:
                                last = mm(sc[x][:, y, off:off + 128], ident16, neg_kq, start=False, stop=True)
                        last.then_inc(s_sc[x].sem, s_sc[x].up())

                    pe.wait_ge(s_mload[b].sem, s_mload[1].at(u, 1) if b else u * 32 + 64)
                    pe.wait_ge(s_vst[b].sem, s_vst[b].at(u, 1))

                    def maxima(units):
                        for i in units:
                            kc = UNITS[i][1]
                            if i == 0 or kc != UNITS[i - 1][1]:
                                pe.wait_ge(s_load[other][kc].sem, u * 192 + 192 * (b + 1))
                            k = b * NU + i
                            if k >= 2:
                                pe.wait_ge(s_red.sem, s_red.at(u, k - 1))
                            else:
                                pe.wait_ge(s_red.sem, s_red.at(u, B * NU + k - 1, back=1))
                            if i == 0:
                                pe.wait_ge(s_mrow.sem, s_mrow.at(u, 1) if b else s_mrow.at(u, 2, back=1))
                            max_unit(other, i).then_inc(s_max.sem, s_max.up())

                    scores(0, 0)
                    scores(0, 1)
                    for s, (qc, j) in enumerate(STEPS):
                        n = b * NS + s
                        off = max(0, 128 * (j - 4 * qc))
                        if s + 1 < NS:
                            scores(s + 1, 0)
                        us = units_of(s)
                        maxima(us[:2])
                        if s + 1 < NS:
                            scores(s + 1, 1)
                        maxima(us[2:3])
                        pe.wait_ge(s_p[0].sem, s_p[0].at(u, n + 1))
                        pe.wait_ge(s_p[1].sem, s_p[1].at(u, n + 1))
                        if j == 0:
                            o = b * QC + QC - 1 - qc
                            if o >= 2:
                                pe.wait_ge(s_o.sem, s_o.at(u, o - 1))
                            else:
                                pe.wait_ge(s_o.sem, s_o.at(u, B * QC + o - 1, back=1))
                        for h in range(4):
                            last = mm(po[qc % 2][32 * h:32 * h + 32, off:512], v_st[b][:, j, h, :],
                                      pt[h // 2][n % 2][:, h % 2, off:512], start=(j == 0), stop=(j == 4 * qc + 3),
                                      tile_position=(0, 32 * h), skip_group_check=True)
                        last.then_inc(s_pv.sem, s_pv.up())
                        maxima(us[3:])
                        if s == UNTIL + 1:
                            pe.wait_ge(s_m.sem, s_m.at(u, b + 1))
                            pe.sem_inc(s_passed, 1)
                            nc.tensor.transpose(pm[0][0:4 * KTS, 0:128], m[:, :], const("ident")).then_inc(s_mt.sem, s_mt.up())

        @block.scalar
        def _(act):
            for q in s_p:
                q.open(act)
            with act.Fori(0, 4) as u:
                for b in range(B):
                    for s, (qc, j) in enumerate(STEPS):
                        n = b * NS + s
                        off = max(0, 128 * (j - 4 * qc))
                        if n >= 2:
                            act.wait_ge(s_pv.sem, s_pv.at(u, n - 1))
                        else:
                            act.wait_ge(s_pv.sem, s_pv.at(u, B * NS + n - 1, back=1))
                        for x in range(2):
                            act.wait_ge(s_sc[x].sem, s_sc[x].at(u, n + 1))
                            nc.scalar.activation(pt[x][n % 2][:, :, off:512], sc[x][:, :, off:512],
                                                               ACT.Exp).then_inc(s_p[x].sem, s_p[x].up())

        @block.vector
        def _(dve):
            ve = nc.vector
            s_o.open(dve)
            for b in range(B):
                ve.memset(ka[b][NP:NROW, :, :], 1.0)
            for i, name in enumerate(("ident", "neg_kq", "neg_qk")):
                ve.tensor_copy(cb16[:, i, :], const(name))
            ve.memset(mx[:, :, :, :], -3e38).then_inc(s_one.sem, 1)
            dve.wait_ge(s_one.sem, 1)

            def reduce_unit(i):
                qt, kc, h = UNITS[i]
                width = min(512, 128 * (qt + 1) - 512 * kc)
                return ve.tensor_reduce(mx[:, h, qt, kc:kc + 1], pm[i % 2][:, 0:width], axis=AX.X, op=ALU.max)

            by_tile = mx[:, :, :, :].rearrange("p h q k -> p (h q) k")
            dve.sem_inc(s_red.sem, NU)
            for i in range(NU):
                dve.wait_ge(s_max.sem, NU + i + 1)
                reduce_unit(i).then_inc(s_red.sem, 1)
            dve.wait_ge(s_red.sem, 2 * NU)
            ve.tensor_reduce(m[:, :], by_tile, axis=AX.X, op=ALU.max).then_inc(s_m.sem, B)
            dve.wait_ge(s_mt.sem, B)
            ve.tensor_scalar(mt[:, :], pm[0][0:4 * KTS, 0:128], -1.0, None, ALU.mult).then_inc(dve_step.sem, B)
            dve.wait_ge(dve_step.sem, B)
            ve.tensor_copy(mrow[:, 0, :], mt[:, :]).then_inc(dve_step.sem, B)
            dve.wait_ge(dve_step.sem, 2 * B)
            ve.tensor_tensor(mrow[:, 1, :], mt[:, :], mrow[:, 0, :], ALU.subtract).then_inc(s_mrow.sem, B)
            with dve.Fori(0, 4) as u:
                for b in range(B):
                    for s, (qc, j) in enumerate(STEPS):
                        us = units_of(s)
                        for i in us:
                            dve.wait_ge(s_max.sem, s_max.at(u, b * NU + i + 1))
                            reduce_unit(i).then_inc(s_red.sem, s_red.up())
                            if i == NU - 1:
                                dve.wait_ge(s_red.sem, s_red.at(u))
                                ve.tensor_reduce(m[:, :], by_tile, axis=AX.X, op=ALU.max).then_inc(s_m.sem, s_m.up())
                        if s == UNTIL + 1:
                            dve.wait_ge(s_mt.sem, s_mt.at(u, b + 1))
                            dve.wait_ge(s_mload[b].sem, s_mload[1].at(u, 1) if b else u * 32 + 64)
                            ve.tensor_scalar(mt[:, :], pm[0][0:4 * KTS, 0:128], -1.0, None, ALU.mult).then_inc(dve_step.sem, dve_step.up())
                            dve.wait_ge(dve_step.sem, dve_step.at(u))
                            ve.tensor_copy(mrow[:, 0, :], mt[:, :]).then_inc(dve_step.sem, dve_step.up())
                            dve.wait_ge(dve_step.sem, dve_step.at(u))
                            ve.tensor_tensor(mrow[:, 1, :], mt[:, :], mrow[:, 0, :], ALU.subtract).then_inc(s_mrow.sem, s_mrow.up())
                        if j == 4 * qc + 3:
                            dve.wait_ge(s_pv.sem, s_pv.at(u, b * NS + s + 1))
                            if qc == QC - 1:
                                dve.wait_ge(s_ostore[b].sem, s_ostore[b].at(u, 1, back=1))
                            ve.tensor_copy(o_sb[b][:, 512 * qc:512 * qc + 512], po[qc % 2][:, :]).then_inc(s_o.sem, s_o.up())


STAGES = [("e2_l1", "xf", "h0", "Gelu"), ("e0_up", "xf", "h1", "Gelu"), ("e3_down", "xf", "h2", "Gelu"),
          ("e0_down", "h1", 0, "out"), ("e2_l2", "h0", "h1", "Gelu"), ("e1_w1", "xf", "gate", "Silu"),
          ("e2_l3", "h1", "h0", "Gelu"), ("e3_up", "h2", "h1", "Gelu"), ("e2_l4", "h0", 2, "out"),
          ("e1_w2", "xf", "h0", "times"), ("e3_out", "h1", 3, "out"), ("e1_down", "h0", 1, "out")]
WIDE = {"e0_up": (2, 4), "e2_l1": (2, 4), "e3_down": (2, 2), "e1_w1": (2, 4), "e1_w2": (2, 4),
        "e2_l2": (4, 4), "e3_up": (2, 4), "e2_l3": (4, 4),
        "e0_down": (4, 2), "e1_down": (4, 2), "e3_out": (4, 2), "e2_l4": (4, 2)}
CUT = 512
EARLY = ["e2_l1", "e0_up"]
MIDDLE = ["e3_down", "e2_l2", "e1_w1"]
LATE = [name for name, *_ in STAGES if name not in EARLY + MIDDLE]


LAST_LAYERS = [name for name, _, _, func in STAGES if func == "out"]
MASKED = 64


def pieces_of(names):
    return [(n, c) for n in names for c in range(0, 128 * WIDE[n][0] * WIDE[n][1], CUT)]


def cut_weights(nc, pool, io, names, hi, lo, stage, s_raw, s_hi, s_lo, s_cut):
    flat = lambda a: a[:, :, :].rearrange("p k c -> p (k c)")
    pieces = pieces_of(names)

    def load(p):
        n, c = pieces[p]
        pool.dma_start(stage[p % 2][:, :], io[n].rearrange("p k c -> p (k c)")[:, c:c + CUT]).then_inc(s_raw[p % 2].sem, 16)

    load(0)
    for p, (n, c) in enumerate(pieces):
        if p + 1 < len(pieces):
            if p:
                pool.wait_ge(s_lo.sem, p)
            load(p + 1)
        pool.wait_ge(s_raw[p % 2].sem, 16 * (p // 2 + 1))
        if n in LAST_LAYERS:
            for k in range(0, CUT, C):
                nc.gpsimd.memset(stage[p % 2][:, k:k + MASKED], 0.0).then_inc(s_hi.sem, 1)
                s_hi.n += 1
            pool.wait_ge(s_hi.sem, s_hi.n)
        nc.gpsimd.tensor_copy(flat(hi[n])[:, c:c + CUT], stage[p % 2][:, :]).then_inc(s_hi.sem, 1)
        s_hi.n += 1
        pool.wait_ge(s_hi.sem, s_hi.n)
        nc.gpsimd.tensor_tensor(flat(lo[n])[:, c:c + CUT], stage[p % 2][:, :], flat(hi[n])[:, c:c + CUT], ALU.subtract
                                ).then_inc(s_lo.sem, 1)
        if p + 1 == len(pieces) or pieces[p + 1][0] != n:
            pool.wait_ge(s_lo.sem, p + 1)
            pool.sem_inc(s_cut.sem, 1)


def expert_phase(nc, io, keep, signal):
    ctx = ExitStack()
    with ctx:
        def sb(name, shape, dt=FP32):
            return ctx.enter_context(nc.sbuf_tensor("e_" + name, shape, dt))

        def sig(name, per, unit=1):
            return signal("e_" + name, per, unit)

        cst, at, vec, xn_all = (keep[n] for n in ("cst", "at", "vec", "xn_all"))
        const = lambda name, lo=0, hi=None: cst[:, at[name][0] + lo:(at[name][0] + hi if hi is not None else at[name][1])]
        v = lambda name, h: vec[:, VECS.index(name), h:h + 1]
        w_hi, w_lo = (dict(keep["w_" + part], **{n: sb(f"{n}_{part}", [128, WIDE[n][0], 128 * WIDE[n][1]], F32R)
                                                 for n in MIDDLE + LATE}) for part in ("hi", "lo"))
        DEEP = {"xf": 2, "h0": 4, "h1": 4, "h2": 2}
        hi, lo = ({n: sb(f"{n}_{part}", [128, d, ECOLS], F32R) for n, d in DEEP.items()} for part in ("hi", "lo"))
        room, used = keep["v_all"][:, :, :, :].rearrange("p b k c -> p (b k c)"), 0

        def tile(deep, width):
            nonlocal used
            used += deep * width
            return room[:, used - deep * width:used].rearrange("p (k c) -> p k c", k=deep)

        wo, ao, asum, x2, xf = (tile(2, C), *(tile(HALVES, ECOLS) for _ in range(4)))
        x2sq = xf
        gate = tile(4, ECOLS)
        tmp = [tile(2, ECOLS) for _ in range(2)]
        acc, s_tok, x_tok, x2_tok = (tile(B, C) for _ in range(4))
        stage = [tile(1, CUT)[:, 0, :] for _ in range(2)]
        rms = tile(1, ECOLS)[:, 0, :]
        middle = pieces_of(MIDDLE)
        gate_flat = gate.rearrange("p k c -> p (k c)")
        places = [a.rearrange("p k c -> p (k c)") for a in (acc, tmp[0], tmp[1], s_tok, x_tok)] \
            + [gate_flat[:, 0:CUT], gate_flat[:, CUT:2 * CUT]]
        assert len(middle) <= len(places)
        gate_w = sb("gate_w", [128, 2, EXPERTS])
        SE = [128, B, EXPERTS]
        lg, ok_, zero, ex, pr, sel, wt = (
            sb(n, SE) for n in ("lg", "ok_", "zero", "ex", "pr", "sel", "wt"))
        okm = sb("okm", SE, mybir.dt.int32)
        mxl, den = sb("mxl", [128, B]), sb("den", [128, B])
        cmp_, eq = sb("cmp_", [128, B, EXPERTS, EXPERTS]), sb("eq", [128, B, EXPERTS, EXPERTS])
        ps = ctx.enter_context(nc.psum_tensor("e_ps", [128, 8, 512], FP32))

        s_wo_in, s_gate_in, s_wo_masked = sig("wo_loaded", 1, 16), sig("gate_loaded", 1, 16), sig("wo_masked", 1)
        s_raw = [sig(f"raw_weights{i}", 1, 16) for i in range(2)]
        s_piece = [sig(f"piece{i}", 1, 16) for i in range(len(middle))]
        s_piece_hi, s_piece_lo = sig("pieces_hi", 1), sig("pieces_cut", 1)
        s_whi, s_wlo, s_cut = sig("weights_hi", 1), sig("weights_lo", 1), sig("weights_cut", 1)
        s_in, s_xin, s_zero = sig("attention_in", 1, 16 * 16), sig("x_s_in", 1, 16 * 4), sig("zero", 1)
        s_ao, s_wo, s_x2, s_x2sq, s_ms, s_rms, s_xf = (sig(n, 1) for n in (
            "ao", "projected", "x2", "x2_squared", "x2_sum", "x2_rms", "xf"))
        s_gate, s_x2t, s_acc0, s_soft, s_exp, s_wt = (sig(n, 1) for n in (
            "logits", "x2_transposed", "x2_kept", "logits_shifted", "logits_exp", "gates"))
        BLOCKS = [(i, o) for i, (n, _, _, f) in enumerate(STAGES) if f != "out" for o in range(0, WIDE[n][1], 2)]
        s_hid = sig("hidden", len(BLOCKS))
        by = {"A": sig("act_took", sum(STAGES[i][3] != "times" for i, _ in BLOCKS)),
              "V": sig("dve_took", sum(STAGES[i][3] == "times" for i, _ in BLOCKS))}
        took = []
        for i, o in BLOCKS:
            who = "V" if STAGES[i][3] == "times" else "A"
            took.append((who, 1 + sum(w_ == who for w_, _ in took)))
        first_block = {i: min(n for n, (k, _) in enumerate(BLOCKS) if k == i) for i in {i for i, _ in BLOCKS}}
        GATE = next(i for i, (n, *_) in enumerate(STAGES) if n == "e1_w1")
        cuts = [n for n, (i, _) in enumerate(BLOCKS) if STAGES[i][3] != "Silu"]
        cut_no = {n: m for m, n in enumerate(cuts)}
        s_hi = sig("hidden_hi", sum(STAGES[BLOCKS[n][0]][3] == "Gelu" for n in cuts))
        s_lo = sig("hidden_lo", len(cuts))
        s_down, s_sum = sig("expert_out", 4), sig("expert_added", 4)
        s_gated, s_out = sig("silu", 1), sig("out", 1)
        s_store = sig("out_stored", 1, 16 * B)
        s_xhi, s_times_s = sig("xf_hi", 1), sig("silu_times_s", 1)
        s_passed = sig("passed", 1).sem
        dve_step = sig("dve_step", 23)
        block = ctx.enter_context(nc.Block())

        @block.sync
        def _(sp):
            def load_attention(t):
                for h in range(HALVES):
                    for b in range(B):
                        rows_ = io["o_dram"][b, :, bass.ds(t * ETT, ETT)].rearrange("(g h e) t -> g h e t", h=8, e=32)
                        for tile, lo in ((ao, 0), (asum, 16)):
                            for r in range(2):
                                sp.dma_start(tile[64 * r:64 * r + 64, h, ETT * b:ETT * b + ETT],
                                             rows_[h, 4 * r:4 * r + 4, lo:lo + 16, :]).then_inc(s_in.sem, 16)

            def load_x_s(t):
                for b in range(B):
                    sp.dma_start(s_tok[:, b, :], io["s_dram"][b, bass.ds(t * ETT, ETT), :]).then_inc(s_xin.sem, 16)
                    sp.dma_start(x_tok[:, b, :], io["x"][b, bass.ds(t * ETT, ETT), :]).then_inc(s_xin.sem, 16)

            def store(t):
                sp.wait_ge(s_out.sem, s_out.at(t, 1))
                sp.sem_inc(s_passed, 1)
                for b in range(B):
                    sp.dma_start(io["out"][b, bass.ds(t * ETT, ETT), :], acc[:, b, :]).then_inc(s_store.sem, 16)

            def turn(t, more):
                store(t - 1)
                load_x_s(t)
                if more:
                    sp.wait_ge(s_wo.sem, s_wo.at(t, 1))
                    sp.sem_inc(s_passed, 1)
                    load_attention(t + 2)

            s_store.open(sp)
            s_xin.open(sp)
            sp.dma_start(wo[:, :, :], io["wo"]).then_inc(s_wo_in.sem, 16)
            load_attention(0)
            sp.dma_start(gate_w[:, :, :], io["gate_w"]).then_inc(s_gate_in.sem, 16)
            for i, (n, c) in enumerate(middle):
                sp.dma_start(places[i], io[n].rearrange("p k c -> p (k c)")[:, c:c + CUT]).then_inc(s_piece[i].sem, 16)
            sp.wait_ge(s_piece_lo.sem, len(middle))
            load_x_s(0)
            sp.wait_ge(s_wo.sem, s_wo.at(-1, 1))
            load_attention(1)
            sp.wait_ge(s_wo.sem, s_wo.at(0, 1))
            load_attention(2)
            with sp.Fori(1, ENT - 2) as t:
                turn(t, True)
            turn(ENT - 2, False)
            turn(ENT - 1, False)
            store(ENT - 1)
            sp.wait_ge(s_store.sem, s_store.at(ENT - 1, 1))

        @block.gpsimd
        def _(pool):
            pool.wait_ge(s_wo_in.sem, 16)
            nc.gpsimd.memset(wo[:, :, 0:MASKED], 0.0).then_inc(s_wo_masked.sem, 1)
            cut_weights(nc, pool, io, LATE, w_hi, w_lo, stage, s_raw, s_whi, s_wlo, s_cut)

        @block.tensor
        def _(pe):
            for q in (s_hid, s_down):
                q.open(pe)
            mm = nc.tensor.matmul
            pe.wait_ge(s_wo_masked.sem, 1)
            pe.wait_ge(s_gate_in.sem, 16)

            def project(t):
                pe.wait_ge(s_ao.sem, s_ao.at(t, 1))
                for h in range(2):
                    for k in range(2):
                        last = mm(ps[:, 4, ECOLS * h:ECOLS * h + ECOLS], wo[:, k, 128 * h:128 * h + 128], ao[:, k, :],
                                  start=(k == 0), stop=(k == 1))
                last.then_inc(s_wo.sem, 1)

            def sum_and_transpose(t):
                pe.wait_ge(s_x2sq.sem, s_x2sq.at(t, 1))
                for h in range(2):
                    last = mm(ps[:, 3, 0:ECOLS], const("ones128"), x2sq[:, h, :], start=(h == 0), stop=(h == 1))
                last.then_inc(s_ms.sem, 1)
                for b in range(B):
                    for h in range(2):
                        last = nc.tensor.transpose(ps[:, 5, C * b + 128 * h:C * b + 128 * h + 128],
                                                   x2[:, h, ETT * b:ETT * b + ETT], const("ident"))
                last.then_inc(s_x2t.sem, 1)

            def logits(t):
                pe.wait_ge(s_xf.sem, s_xf.at(t, 1))
                for b in range(B):
                    for h in range(2):
                        last = mm(ps[:, 3, EXPERTS * b:EXPERTS * b + EXPERTS], xf[:, h, ETT * b:ETT * b + ETT],
                                  gate_w[:, h, :], start=(h == 0), stop=(h == 1))
                last.then_inc(s_gate.sem, 1)

            def three_passes(out, a_hi, a_lo, b_hi, b_lo, ins):
                products = [(a(k), b(k)) for k in range(ins) for a, b in ((a_hi, b_hi), (a_hi, b_lo), (a_lo, b_hi))]
                for n, (a, b) in enumerate(products):
                    last = mm(out, a, b, start=(n == 0), stop=(n == len(products) - 1))
                return last

            def turn(t, more):
                downs = 0
                written = {}
                for i, (name, src, dst, func) in enumerate(STAGES):
                    ins, outs = WIDE[name]
                    if src == "xf":
                        pe.wait_ge(s_xhi.sem, s_xhi.at(t, 0))
                    else:
                        pe.wait_ge(s_lo.sem, s_lo.at(t, cut_no[written[src]] + 1))
                    if name in MIDDLE:
                        pe.wait_ge(s_piece_lo.sem, len(middle))
                    if name in LATE:
                        pe.wait_ge(s_cut.sem, LATE.index(name) + 1)
                    wh, wl = w_hi[name], w_lo[name]
                    if func == "out":
                        downs += 1
                        if downs > 2:
                            pe.wait_ge(s_sum.sem, s_sum.at(t, downs - 2))
                        else:
                            pe.wait_ge(s_sum.sem, s_sum.at(t, downs + 2, back=1))
                        for b in range(B):
                            tok = slice(ETT * b, ETT * b + ETT)
                            last = three_passes(ps[:, 6 + downs % 2, C * b:C * b + C],
                                                lambda k: hi[src][:, k, tok], lambda k: lo[src][:, k, tok],
                                                lambda k: wh[:, k, :], lambda k: wl[:, k, :], ins)
                        last.then_inc(s_down.sem, s_down.up())
                    for o in range(0, outs if func != "out" else 0, 2):
                        n = first_block[i] + o // 2
                        if n >= 3:
                            who, m = took[n - 3]
                            pe.wait_ge(by[who].sem, by[who].at(t, m))
                        else:
                            who, m = took[len(took) - 3 + n]
                            pe.wait_ge(by[who].sem, by[who].at(t, m, back=1))
                        for j in range(2):
                            cols = slice(128 * (o + j), 128 * (o + j) + 128)
                            last = three_passes(ps[:, n % 3, ECOLS * j:ECOLS * j + ECOLS],
                                                lambda k: wh[:, k, cols], lambda k: wl[:, k, cols],
                                                lambda k: hi[src][:, k, :], lambda k: lo[src][:, k, :], ins)
                        last.then_inc(s_hid.sem, s_hid.up())
                        written[dst] = n
                    if more and name == "e1_w1":
                        project(t)
                    if more and name == "e2_l3":
                        sum_and_transpose(t)
                    if more and name == "e1_w2":
                        logits(t)
                for q in (s_hid, s_down):
                    q.restart()

            project(-1)
            sum_and_transpose(-1)
            logits(-1)
            with pe.Fori(0, ENT - 1) as t:
                turn(t, True)
            turn(ENT - 1, False)

        @block.scalar
        def _(act):
            for q in (by["A"], s_hi, s_gated):
                q.open(act)
            f = nc.scalar.activation

            def squares(t):
                act.wait_ge(s_x2.sem, s_x2.at(t, 1))
                f(x2sq[:, :, :], x2[:, :, :], ACT.Square).then_inc(s_x2sq.sem, 1)

            def roots(t):
                act.wait_ge(s_ms.sem, s_ms.at(t, 1))
                f(rms[:, :], ps[:, 3, 0:ECOLS], ACT.Sqrt, bias=const("eps", 2, 3), scale=1.0 / C).then_inc(s_rms.sem, 1)
                act.wait_ge(s_x2t.sem, s_x2t.at(t, 1))
                f(x2_tok[:, :, :].rearrange("p b c -> p (b c)"), ps[:, 5, :], ACT.Copy).then_inc(s_acc0.sem, 1)

            def exps(t):
                act.wait_ge(s_soft.sem, s_soft.at(t, 1))
                f(ex[:, :, :], lg[:, :, :], ACT.Exp).then_inc(s_exp.sem, 1)

            def gated(t):
                act.wait_ge(s_sum.sem, s_sum.at(t, 4))
                f(acc[:, :, :], acc[:, :, :], ACT.Silu).then_inc(s_gated.sem, 1)

            def turn(t, before, more):
                for n, (i, o) in enumerate(BLOCKS):
                    name, src, dst, func = STAGES[i]
                    if func == "times":
                        continue
                    if more and name == "e2_l3" and o == 0:
                        squares(t)
                    if before and name == "e1_w1" and o == 0:
                        gated(t - 1)
                    act.wait_ge(s_hid.sem, s_hid.at(t, n + 1))
                    two = ps[:, n % 3, :].rearrange("p (j c) -> p j c", j=2)
                    if func == "Silu":
                        f(gate[:, o:o + 2, :], two, ACT.Silu).then_inc(by["A"].sem, by["A"].up())
                    else:
                        m = cut_no[n]
                        if m >= 2:
                            act.wait_ge(s_lo.sem, s_lo.at(t, m - 1))
                        else:
                            act.wait_ge(s_lo.sem, s_lo.at(t, len(cuts), back=1))
                        f(tmp[m % 2][:, :, :], two, ACT.Gelu).then_inc(by["A"].sem, by["A"].up())
                        act.wait_ge(by["A"].sem, by["A"].at(t))
                        f(hi[dst][:, o:o + 2, :], tmp[m % 2][:, :, :], ACT.Copy).then_inc(s_hi.sem, s_hi.up())
                if more:
                    act.wait_ge(s_sum.sem, s_sum.at(t, 1))
                    roots(t)
                    exps(t)
                for q in (by["A"], s_hi):
                    q.restart()

            squares(-1)
            for i, (n, c) in enumerate(middle):
                act.wait_ge(s_piece[i].sem, 16)
                f(w_hi[n][:, :, :].rearrange("p k c -> p (k c)")[:, c:c + CUT], places[i], ACT.Copy
                  ).then_inc(s_piece_hi.sem, 1)
            roots(-1)
            exps(-1)
            turn(0, False, True)
            with act.Fori(1, ENT - 1) as t:
                turn(t, True, True)
            turn(ENT - 1, True, False)
            gated(ENT - 1)

        @block.vector
        def _(dve):
            for q in (by["V"], s_lo, s_sum, s_out, s_times_s):
                q.open(dve)
            ve = nc.vector
            ve.memset(zero[:, :, :], 0.0).then_inc(s_zero.sem, 1)
            dve.wait_ge(s_zero.sem, 1)

            def divide(t):
                dve.wait_ge(s_in.sem, s_in.at(t, 1))
                ve.reciprocal(asum[:, :, :], asum[:, :, :]).then_inc(dve_step.sem, dve_step.up())
                dve.wait_ge(dve_step.sem, dve_step.at(t))
                ve.tensor_tensor(ao[:, :, :], ao[:, :, :], asum[:, :, :], ALU.mult).then_inc(s_ao.sem, 1)

            def residual(t):
                dve.wait_ge(s_wo.sem, s_wo.at(t, 1))
                for h in range(2):
                    last = ve.tensor_tensor(x2[:, h, :].rearrange("p (b t) -> p b t", b=B),
                                            ps[:, 4, ECOLS * h:ECOLS * h + ECOLS].rearrange("p (b t) -> p b t", b=B),
                                            xn_all[:, h, :, bass.ds((t + 1) * ETT + 1, ETT)], ALU.add)
                last.then_inc(s_x2.sem, 1)
                dve.wait_ge(s_x2.sem, s_x2.at(t, 1))

            def normalise(t):
                dve.wait_ge(s_rms.sem, s_rms.at(t, 1))
                ve.reciprocal(rms[:, :], rms[:, :]).then_inc(dve_step.sem, dve_step.up())
                dve.wait_ge(dve_step.sem, dve_step.at(t))
                for h in range(2):
                    last = ve.scalar_tensor_tensor(xf[:, h, :], x2[:, h, :], v("n2_w", h), rms[:, :], ALU.mult, ALU.mult)
                last.then_inc(s_xf.sem, 1)
                dve.wait_ge(s_xf.sem, s_xf.at(t, 1))

            def cut_xf(t):
                ve.tensor_copy(hi["xf"][:, :, :], xf[:, :, :]).then_inc(dve_step.sem, dve_step.up())
                dve.wait_ge(dve_step.sem, dve_step.at(t))
                ve.tensor_tensor(lo["xf"][:, :, :], xf[:, :, :], hi["xf"][:, :, :], ALU.subtract).then_inc(s_xhi.sem, 1)

            wide = lambda a: a.unsqueeze(2).to_broadcast([128, B, EXPERTS])

            def shift_logits(t):
                dve.wait_ge(s_gate.sem, s_gate.at(t, 1))
                ve.tensor_copy(lg[:, :, :], ps[:, 3, 0:B * EXPERTS].rearrange("p (s e) -> p s e", e=EXPERTS)).then_inc(dve_step.sem, dve_step.up())
                dve.wait_ge(dve_step.sem, dve_step.at(t))
                ve.tensor_tensor(okm[:, :, :], lg[:, :, :], lg[:, :, :], ALU.is_equal).then_inc(dve_step.sem, dve_step.up())
                dve.wait_ge(dve_step.sem, dve_step.at(t))
                ve.tensor_copy(ok_[:, :, :], zero[:, :, :]).then_inc(dve_step.sem, dve_step.up())
                dve.wait_ge(dve_step.sem, dve_step.at(t))
                dve.sem_inc(s_passed, 1)
                ve.copy_predicated(ok_[:, :, :], okm[:, :, :], lg[:, :, :]).then_inc(dve_step.sem, dve_step.up())
                dve.wait_ge(dve_step.sem, dve_step.at(t))
                ve.tensor_scalar(ok_[:, :, :], ok_[:, :, :], 3.4028234e38, -3.4028234e38, ALU.min, ALU.max).then_inc(dve_step.sem, dve_step.up())
                dve.wait_ge(dve_step.sem, dve_step.at(t))
                ve.tensor_reduce(mxl[:, :], ok_[:, :, :], axis=AX.X, op=ALU.max).then_inc(dve_step.sem, dve_step.up())
                dve.wait_ge(dve_step.sem, dve_step.at(t))
                ve.tensor_tensor(lg[:, :, :], ok_[:, :, :], wide(mxl[:, :]), ALU.subtract).then_inc(s_soft.sem, 1)
                dve.wait_ge(s_soft.sem, s_soft.at(t, 1))

            def top_two(before, t):
                dve.wait_ge(s_exp.sem, s_exp.at(before, 1))
                ve.tensor_reduce(den[:, :], ex[:, :, :], axis=AX.X, op=ALU.add).then_inc(dve_step.sem, dve_step.up())
                dve.wait_ge(dve_step.sem, dve_step.at(t))
                ve.reciprocal(den[:, :], den[:, :]).then_inc(dve_step.sem, dve_step.up())
                dve.wait_ge(dve_step.sem, dve_step.at(t))
                ve.tensor_tensor(pr[:, :, :], ex[:, :, :], wide(den[:, :]), ALU.mult).then_inc(dve_step.sem, dve_step.up())
                dve.wait_ge(dve_step.sem, dve_step.at(t))
                other = pr[:, :, :].unsqueeze(2).to_broadcast([128, B, EXPERTS, EXPERTS])
                this = pr[:, :, :].unsqueeze(3).to_broadcast([128, B, EXPERTS, EXPERTS])
                ve.tensor_tensor(cmp_[:, :, :, :], other, this, ALU.is_gt)
                ve.tensor_tensor(eq[:, :, :, :], other, this, ALU.is_equal).then_inc(dve_step.sem, dve_step.up())
                dve.wait_ge(dve_step.sem, dve_step.at(t))
                earlier = const("earlier").rearrange("p (e j) -> p e j", j=EXPERTS).unsqueeze(1)\
                    .to_broadcast([128, B, EXPERTS, EXPERTS])
                ve.tensor_tensor(eq[:, :, :, :], eq[:, :, :, :], earlier, ALU.mult).then_inc(dve_step.sem, dve_step.up())
                dve.wait_ge(dve_step.sem, dve_step.at(t))
                ve.tensor_tensor(cmp_[:, :, :, :], cmp_[:, :, :, :], eq[:, :, :, :], ALU.add).then_inc(dve_step.sem, dve_step.up())
                dve.wait_ge(dve_step.sem, dve_step.at(t))
                ve.tensor_reduce(sel[:, :, :], cmp_[:, :, :, :], axis=AX.X, op=ALU.add).then_inc(dve_step.sem, dve_step.up())
                dve.wait_ge(dve_step.sem, dve_step.at(t))
                ve.scalar_tensor_tensor(wt[:, :, :], sel[:, :, :], 2.0, pr[:, :, :], ALU.is_lt, ALU.mult).then_inc(dve_step.sem, dve_step.up())
                dve.wait_ge(dve_step.sem, dve_step.at(t))
                ve.tensor_reduce(den[:, :], wt[:, :, :], axis=AX.X, op=ALU.add).then_inc(dve_step.sem, dve_step.up())
                dve.wait_ge(dve_step.sem, dve_step.at(t))
                ve.tensor_scalar(den[:, :], den[:, :], 1e-8, None, ALU.add).then_inc(dve_step.sem, dve_step.up())
                dve.wait_ge(dve_step.sem, dve_step.at(t))
                ve.reciprocal(den[:, :], den[:, :]).then_inc(dve_step.sem, dve_step.up())
                dve.wait_ge(dve_step.sem, dve_step.at(t))
                ve.tensor_tensor(wt[:, :, :], wt[:, :, :], wide(den[:, :]), ALU.mult).then_inc(dve_step.sem, dve_step.up())
                dve.wait_ge(dve_step.sem, dve_step.at(t))

            def finish(t):
                dve.wait_ge(s_xin.sem, s_xin.at(t, 1))
                dve.wait_ge(s_gated.sem, s_gated.at(t, 1))
                ve.tensor_tensor(acc[:, :, :], acc[:, :, :], s_tok[:, :, :], ALU.mult).then_inc(s_times_s.sem, 1)
                dve.wait_ge(s_times_s.sem, s_times_s.at(t, 1))
                ve.tensor_tensor(acc[:, :, :], acc[:, :, :], x_tok[:, :, :], ALU.add).then_inc(s_out.sem, 1)

            def turn(t, before, more):
                dve.wait_ge(s_acc0.sem, s_acc0.at(t, 0))
                downs = 0

                def add_expert(e, total):
                    nonlocal downs
                    downs += 1
                    dve.wait_ge(s_down.sem, s_down.at(t, downs))
                    for b in range(B):
                        last = ve.scalar_tensor_tensor(acc[:, b, :], ps[:, 6 + downs % 2, C * b:C * b + C],
                                                       wt[:, b, e:e + 1], total[:, b, :], ALU.mult, ALU.add)
                    last.then_inc(s_sum.sem, s_sum.up())
                    dve.wait_ge(s_sum.sem, s_sum.at(t))

                for i, (name, src, dst, func) in enumerate(STAGES):
                    if func in ("Gelu", "times"):
                        for o in range(0, WIDE[name][1], 2):
                            n = first_block[i] + o // 2
                            m = cut_no[n]
                            if func == "times":
                                dve.wait_ge(s_hid.sem, s_hid.at(t, n + 1))
                                who, k = took[first_block[GATE] + o // 2]
                                dve.wait_ge(by[who].sem, by[who].at(t, k))
                                ve.tensor_tensor(tmp[m % 2][:, :, :], ps[:, n % 3, :].rearrange("p (j c) -> p j c", j=2),
                                                 gate[:, o:o + 2, :], ALU.mult).then_inc(by["V"].sem, by["V"].up())
                                dve.wait_ge(by["V"].sem, by["V"].at(t))
                                ve.tensor_copy(hi[dst][:, o:o + 2, :], tmp[m % 2][:, :, :]
                                               ).then_inc(dve_step.sem, dve_step.up())
                                dve.wait_ge(dve_step.sem, dve_step.at(t))
                            else:
                                dve.wait_ge(s_hi.sem, s_hi.at(t, 1 + sum(STAGES[BLOCKS[c][0]][3] == "Gelu" for c in cuts[:m])))
                            ve.tensor_tensor(lo[dst][:, o:o + 2, :], tmp[m % 2][:, :, :], hi[dst][:, o:o + 2, :],
                                             ALU.subtract).then_inc(s_lo.sem, s_lo.up())
                        if more and name == "e0_up":
                            divide(t)
                        if name == "e3_down":
                            top_two(t - 1, t)
                        if more and name == "e3_up":
                            normalise(t)
                        if more and name == "e1_w2":
                            cut_xf(t)
                    if name == "e1_w1":
                        if before:
                            finish(t - 1)
                        dve.wait_ge(s_store.sem, s_store.at(t, 1, back=1))
                        add_expert(0, x2_tok)
                        if more:
                            residual(t)
                    if func == "out" and name != "e0_down":
                        add_expert(dst, acc)
                        if more and name == "e3_out":
                            shift_logits(t)
                if more:
                    dve_step.whole()
                for q in (by["V"], s_lo, s_sum, dve_step):
                    q.restart()

            divide(-1)
            residual(-1)
            for i, (n, c) in enumerate(middle):
                dve.wait_ge(s_piece_hi.sem, i + 1)
                h, l = (tile_[n][:, :, :].rearrange("p k c -> p (k c)")[:, c:c + CUT] for tile_ in (w_hi, w_lo))
                ve.tensor_tensor(l, places[i], h, ALU.subtract).then_inc(s_piece_lo.sem, 1)
            normalise(-1)
            cut_xf(-1)
            shift_logits(-1)
            dve_step.restart(dve)
            turn(0, False, True)
            with dve.Fori(1, ENT - 1) as t:
                turn(t, True, True)
            turn(ENT - 1, True, False)
            finish(ENT - 1)


def program(nc, io):
    ctx = ExitStack()
    with ctx:
        at, width = table_at()
        io["s_dram"] = nc.dram_tensor("s_scratch", (B, T, C), FP32, kind="Internal").ap()
        for n in "qk":
            io[n + "_dram"] = nc.dram_tensor(n + "_scratch", (3, B, C, T), BF16, kind="Internal").ap()
        io["o_dram"] = nc.dram_tensor("o_scratch", (B, AH * 32, T), FP32, kind="Internal").ap()
        keep = {"at": at, "n_const": 32}
        keep["cst"] = ctx.enter_context(nc.sbuf_tensor("cst", [128, width], FP32))
        keep["vec"] = ctx.enter_context(nc.sbuf_tensor("vec", [128, len(VECS), 2], FP32))
        keep["xn_all"] = ctx.enter_context(nc.sbuf_tensor("xn_all", [128, HALVES, B, T + 1], FP32))
        keep["s_const"] = ctx.enter_context(nc.semaphore("s_const"))

        def signal(name, per, unit=1):
            return Signal(ctx.enter_context(nc.semaphore(name)), per, unit)

        nc.sync.dma_start(keep["cst"][:, :], io["table"]).then_inc(keep["s_const"], 16)
        nc.sync.dma_start(keep["vec"][:, :, :], io["vecs"]).then_inc(keep["s_const"], 16)
        keep["v_all"] = ctx.enter_context(nc.sbuf_tensor("v_all", [128, B, T // 128, C], FP32))
        recurrent_phase(nc, io, keep, signal)
        for part in ("hi", "lo"):
            keep["w_" + part] = {n: ctx.enter_context(nc.sbuf_tensor(f"{n}_{part}", [128, WIDE[n][0], 128 * WIDE[n][1]], F32R))
                                 for n in EARLY}
        attention_phase(nc, io, keep, signal)
        expert_phase(nc, io, keep, signal)




def host_tables():
    import numpy as np
    at, width = table_at()
    tab = np.zeros((128, width), np.float32)
    def put(name, a):
        tab[:, at[name][0]:at[name][1]] = a.reshape(128, -1)
    r = np.arange(128)
    put("ident", np.eye(128))
    put("neg_kq", (r[None] < r[:, None]) * -1e30)
    put("neg_qk", (r[None] > r[:, None]) * -1e30)
    put("ones64", (r[:, None] // 64 == r[None] // 64))
    put("ones16", (r[:, None] // 16 == r[None] // 16))
    put("ones128", np.ones((128, 128)))
    i, j = np.arange(64)[:, None], np.arange(64)[None]
    two = lambda a: np.concatenate([a, a], axis=0).astype(np.float32)
    one = np.ones((64, 64))
    put("amask", two(np.concatenate([i < j, i <= j, one, i < j, i <= j, one, i > j], axis=1)))
    put("eye64", two(i == j))
    off = lambda n: (i // (2 * n) == j // (2 * n)) & ((i // n) % 2 == 1) & ((j // n) % 2 == 0)
    put("low0", two(off(1)))
    put("low0t", two(off(1).T))
    put("lev", two(np.concatenate([off(2 ** k).T for k in range(1, LEVELS)], axis=1)))
    put("reset", np.broadcast_to((np.arange(COLS) % CH != 0), (128, COLS)))
    put("eps", np.broadcast_to(np.array([LN_EPS, GN_EPS, RMS_EPS, AD * RMS_EPS]), (128, 4)))
    e, j = np.arange(4)[:, None], np.arange(4)[None]
    put("earlier", np.broadcast_to((j < e).reshape(1, 16), (128, 16)))
    return tab


def ffn_arrays(give, g, rows):
    for n in ("wq", "wk", "wv", "wo", "gate_w", "e0_up", "e0_down", "e1_w1", "e1_w2", "e1_down",
              "e2_l1", "e2_l2", "e2_l3", "e2_l4", "e3_down", "e3_up", "e3_out"):
        give(n, rows(g("L0_ffn_" + n).T))


def kernel(**inputs):
    import numpy as np
    import concourse.bacc as _bacc
    from concourse.bass_utils import run_bass_kernel_spmd as _run

    nc = _bacc.Bacc("TRN2", target_bir_lowering=False, num_devices=1)
    arrays, io = {}, {}

    def give(name, a):
        a = np.ascontiguousarray(a)
        arrays["in_" + name] = a
        io[name] = nc.dram_tensor("in_" + name, a.shape, mybir.dt.from_np(a.dtype), kind="ExternalInput").ap()

    g = lambda n: np.asarray(inputs[n])
    rows = lambda a: a.reshape(-1, 128, a.shape[1]).transpose(1, 0, 2)
    give("x", g("L0_attn_x"))
    for n in ("W_r", "W_k", "W_v", "W_o", "w1", "a1", "g1"):
        give(n, rows(g("L0_attn_" + n)))
    for n in ("w2", "a2", "g2"):
        give(n, g("L0_attn_" + n))
    vecs = [g("L0_ffn_" + n) if n in ("n1_w", "n2_w") else np.tile(g("L0_ffn_" + n), AH) if n in ("qn_w", "kn_w")
            else g("L0_attn_" + n).reshape(-1) for n in VECS]
    give("vecs", np.stack(vecs).reshape(len(VECS), 2, 128).transpose(2, 0, 1))
    give("table", host_tables())
    ffn_arrays(give, g, rows)
    io["out"] = nc.dram_tensor("out_dram", (B, T, C), FP32, kind="ExternalOutput").ap()
    program(nc, io)
    r = _run(nc, [arrays], core_ids=[0])
    return r.results[0]["out_dram"]
```
